# Optimizing a Trainium2 kernel written in Bass

```python
import numpy as np
import jax
import jax.numpy as jnp

def _softmax(x, axis=-1):
    return jax.nn.softmax(x, axis=axis)
def _gelu(x):
    return jax.nn.gelu(x, approximate=True)
def _silu(x):
    return jax.nn.silu(x)
def _sigmoid(x):
    return jax.nn.sigmoid(x)
def _layernorm(x, axis=-1, eps=1e-5):
    m = jnp.mean(x, axis=axis, keepdims=True)
    v = jnp.var(x, axis=axis, keepdims=True)
    return (x - m) / jnp.sqrt(v + eps)
def _scatter_add(tgt, idx, src, axis=0):
    return tgt.at[idx].add(src)
def _segment_sum(src, seg, n):
    return jax.ops.segment_sum(src, seg, n)

kernel_name = 'mk_metaformer_d1_conv_nchw512_0ef11e'

def setup_inputs(seed: int = 0):
    np.random.seed(seed)
    _w = jnp.asarray
    def _rec_inputs():
        import jax
        import jax.numpy as jnp
        _gk = jax.random.key(seed)
        x = -0.0002928 + 1 * jax.random.normal(jax.random.fold_in(_gk, 1), (2, 512, 64, 64), jnp.float32)
        return x
    x = _rec_inputs()
    def _L0_conv_setup():
        import jax, jax.numpy as jnp
        import numpy as np
        DIM = 512
        D_STATE = 16
        D_CONV = 4
        D_INNER = 1024
        DT_RANK = 32
        EPS = 1e-05

        def _selective_scan(u, delta, A, Bm, Cm, D_skip):

            def step(h, inp):
                u_t, d_t, b_t, c_t = inp
                dA = jnp.exp(d_t[..., None] * A)
                dBu = (d_t * u_t)[..., None] * b_t[:, None, :]
                h = dA * h + dBu
                y = jnp.einsum('bdn,bn->bd', h, c_t)
                return (h, y)
            B, L, d = u.shape
            h0 = jnp.zeros((B, d, A.shape[1]), u.dtype)
            xs = (u.transpose(1, 0, 2), delta.transpose(1, 0, 2), Bm.transpose(1, 0, 2), Cm.transpose(1, 0, 2))
            _, ys = jax.lax.scan(step, h0, xs)
            y = ys.transpose(1, 0, 2)
            return y + u * D_skip

        def _mamba_layer(x, ln_w, ln_b, in_proj_w, conv_w, conv_b, x_proj_w, dt_proj_w, dt_proj_b, A_log, D_skip, out_proj_w):
            B, C = x.shape[:2]
            img_dims = x.shape[2:]
            xf = x.reshape(B, C, -1).transpose(0, 2, 1)
            mu = jnp.mean(xf, -1, keepdims=True)
            var = jnp.mean(jnp.square(xf - mu), -1, keepdims=True)
            xn = (xf - mu) * jax.lax.rsqrt(var + EPS) * ln_w + ln_b
            xz = xn @ in_proj_w.T
            xin, z = jnp.split(xz, 2, axis=-1)
            xc = xin.transpose(0, 2, 1)
            w = conv_w[:, None, :]
            xc = jax.lax.conv_general_dilated(xc, w, window_strides=(1,), padding=[(D_CONV - 1, 0)], feature_group_count=D_INNER, dimension_numbers=('NCH', 'OIH', 'NCH'))
            xc = jax.nn.silu(xc + conv_b[None, :, None])
            xs = xc.transpose(0, 2, 1)
            x_dbl = xs @ x_proj_w.T
            dt = x_dbl[..., :DT_RANK]
            Bm = x_dbl[..., DT_RANK:DT_RANK + D_STATE]
            Cm = x_dbl[..., DT_RANK + D_STATE:]
            delta = jax.nn.softplus(dt @ dt_proj_w.T + dt_proj_b)
            A = -jnp.exp(A_log)
            y = _selective_scan(xs, delta, A, Bm, Cm, D_skip)
            y = y * jax.nn.silu(z)
            out = y @ out_proj_w.T
            return out.transpose(0, 2, 1).reshape(B, C, *img_dims)
        key = jax.random.key(seed)
        ks = jax.random.split(key, 8)
        s = 0.02
        x = jax.random.normal(ks[0], (2, DIM, 64, 64), jnp.float32)
        in_proj_w = jax.random.normal(ks[1], (2 * D_INNER, DIM), jnp.float32) * s
        conv_w = jax.random.normal(ks[2], (D_INNER, D_CONV), jnp.float32) * 0.25
        conv_b = jnp.zeros((D_INNER,), jnp.float32)
        x_proj_w = jax.random.normal(ks[3], (DT_RANK + 2 * D_STATE, D_INNER), jnp.float32) * s
        dt_proj_w = jax.random.normal(ks[4], (D_INNER, DT_RANK), jnp.float32) * DT_RANK ** (-0.5)
        dt_proj_b = jnp.full((D_INNER,), -4.0, jnp.float32)
        A_log = jnp.log(jnp.broadcast_to(jnp.arange(1, D_STATE + 1, dtype=jnp.float32), (D_INNER, D_STATE)))
        D_skip = jnp.ones((D_INNER,), jnp.float32)
        out_proj_w = jax.random.normal(ks[5], (DIM, D_INNER), jnp.float32) * s
        ln_w = jnp.ones((DIM,), jnp.float32)
        ln_b = jnp.zeros((DIM,), jnp.float32)
        return {'x': x, 'ln_w': ln_w, 'ln_b': ln_b, 'in_proj_w': in_proj_w, 'conv_w': conv_w, 'conv_b': conv_b, 'x_proj_w': x_proj_w, 'dt_proj_w': dt_proj_w, 'dt_proj_b': dt_proj_b, 'A_log': A_log, 'D_skip': D_skip, 'out_proj_w': out_proj_w}
    _L0_conv_all = _L0_conv_setup()
    _L0_conv_in = {k: v for k, v in _L0_conv_all.items() if k in ('ln_w', 'ln_b', 'in_proj_w', 'conv_w', 'conv_b', 'x_proj_w', 'dt_proj_w', 'dt_proj_b', 'A_log', 'D_skip', 'out_proj_w', )}
    del _L0_conv_all

    def _L0_ffn_setup():
        import jax, jax.numpy as jnp
        import numpy as np
        DIM = 512
        NE = 8
        TOPK = 2
        CF = 1.2
        HID = 4 * DIM
        B, S = (8, 4096)
        key = jax.random.key(seed)
        ks = jax.random.split(key, 4)
        s = 0.02
        return {'x': jax.random.normal(ks[0], (B, S, DIM), jnp.float32), 'gate_w': jax.random.normal(ks[1], (NE, DIM), jnp.float32) * s, 'gate_b': jnp.zeros((NE,), jnp.float32), 'w1': jax.random.normal(ks[2], (NE, DIM, HID), jnp.float32) * s, 'b1': jnp.zeros((NE, HID), jnp.float32), 'w2': jax.random.normal(ks[3], (NE, HID, DIM), jnp.float32) * s, 'b2': jnp.zeros((NE, DIM), jnp.float32)}
    _L0_ffn_all = _L0_ffn_setup()
    _L0_ffn_in = {k: v for k, v in _L0_ffn_all.items() if k in ('gate_w', 'gate_b', 'w1', 'b1', 'w2', 'b2', )}
    del _L0_ffn_all

    return {
        "x": x,
        "L0_conv_ln_w": _L0_conv_in["ln_w"],
        "L0_conv_ln_b": _L0_conv_in["ln_b"],
        "L0_conv_in_proj_w": _L0_conv_in["in_proj_w"],
        "L0_conv_conv_w": _L0_conv_in["conv_w"],
        "L0_conv_conv_b": _L0_conv_in["conv_b"],
        "L0_conv_x_proj_w": _L0_conv_in["x_proj_w"],
        "L0_conv_dt_proj_w": _L0_conv_in["dt_proj_w"],
        "L0_conv_dt_proj_b": _L0_conv_in["dt_proj_b"],
        "L0_conv_A_log": _L0_conv_in["A_log"],
        "L0_conv_D_skip": _L0_conv_in["D_skip"],
        "L0_conv_out_proj_w": _L0_conv_in["out_proj_w"],
        "L0_ffn_gate_w": _L0_ffn_in["gate_w"],
        "L0_ffn_gate_b": _L0_ffn_in["gate_b"],
        "L0_ffn_w1": _L0_ffn_in["w1"],
        "L0_ffn_b1": _L0_ffn_in["b1"],
        "L0_ffn_w2": _L0_ffn_in["w2"],
        "L0_ffn_b2": _L0_ffn_in["b2"],
    }

def reference(x, L0_conv_ln_w, L0_conv_ln_b, L0_conv_in_proj_w, L0_conv_conv_w, L0_conv_conv_b, L0_conv_x_proj_w, L0_conv_dt_proj_w, L0_conv_dt_proj_b, L0_conv_A_log, L0_conv_D_skip, L0_conv_out_proj_w, L0_ffn_gate_w, L0_ffn_gate_b, L0_ffn_w1, L0_ffn_b1, L0_ffn_w2, L0_ffn_b2):
    import jax
    import jax.numpy as jnp
    def _L0_conv_ref(x, ln_w, ln_b, in_proj_w, conv_w, conv_b, x_proj_w, dt_proj_w, dt_proj_b, A_log, D_skip, out_proj_w):
        import jax, jax.numpy as jnp
        import numpy as np
        DIM = 512
        D_STATE = 16
        D_CONV = 4
        D_INNER = 1024
        DT_RANK = 32
        EPS = 1e-05

        def _selective_scan(u, delta, A, Bm, Cm, D_skip):

            def step(h, inp):
                u_t, d_t, b_t, c_t = inp
                dA = jnp.exp(d_t[..., None] * A)
                dBu = (d_t * u_t)[..., None] * b_t[:, None, :]
                h = dA * h + dBu
                y = jnp.einsum('bdn,bn->bd', h, c_t)
                return (h, y)
            B, L, d = u.shape
            h0 = jnp.zeros((B, d, A.shape[1]), u.dtype)
            xs = (u.transpose(1, 0, 2), delta.transpose(1, 0, 2), Bm.transpose(1, 0, 2), Cm.transpose(1, 0, 2))
            _, ys = jax.lax.scan(step, h0, xs)
            y = ys.transpose(1, 0, 2)
            return y + u * D_skip

        def _mamba_layer(x, ln_w, ln_b, in_proj_w, conv_w, conv_b, x_proj_w, dt_proj_w, dt_proj_b, A_log, D_skip, out_proj_w):
            B, C = x.shape[:2]
            img_dims = x.shape[2:]
            xf = x.reshape(B, C, -1).transpose(0, 2, 1)
            mu = jnp.mean(xf, -1, keepdims=True)
            var = jnp.mean(jnp.square(xf - mu), -1, keepdims=True)
            xn = (xf - mu) * jax.lax.rsqrt(var + EPS) * ln_w + ln_b
            xz = xn @ in_proj_w.T
            xin, z = jnp.split(xz, 2, axis=-1)
            xc = xin.transpose(0, 2, 1)
            w = conv_w[:, None, :]
            xc = jax.lax.conv_general_dilated(xc, w, window_strides=(1,), padding=[(D_CONV - 1, 0)], feature_group_count=D_INNER, dimension_numbers=('NCH', 'OIH', 'NCH'))
            xc = jax.nn.silu(xc + conv_b[None, :, None])
            xs = xc.transpose(0, 2, 1)
            x_dbl = xs @ x_proj_w.T
            dt = x_dbl[..., :DT_RANK]
            Bm = x_dbl[..., DT_RANK:DT_RANK + D_STATE]
            Cm = x_dbl[..., DT_RANK + D_STATE:]
            delta = jax.nn.softplus(dt @ dt_proj_w.T + dt_proj_b)
            A = -jnp.exp(A_log)
            y = _selective_scan(xs, delta, A, Bm, Cm, D_skip)
            y = y * jax.nn.silu(z)
            out = y @ out_proj_w.T
            return out.transpose(0, 2, 1).reshape(B, C, *img_dims)
        return _mamba_layer(x, ln_w, ln_b, in_proj_w, conv_w, conv_b, x_proj_w, dt_proj_w, dt_proj_b, A_log, D_skip, out_proj_w)

    def _L0_ffn_ref(x, gate_w, gate_b, w1, b1, w2, b2):
        import jax, jax.numpy as jnp
        import numpy as np
        DIM = 512
        NE = 8
        TOPK = 2
        CF = 1.2
        HID = 4 * DIM
        B, S = (8, 4096)
        Bq, Sq, D = x.shape
        T = Bq * Sq
        cap = int(CF * T / NE)
        xf = x.reshape(T, D)
        probs = jax.nn.softmax(xf @ gate_w.T + gate_b, axis=-1)
        topw, topi = jax.lax.top_k(probs, TOPK)
        onehot = jax.nn.one_hot(topi, NE, dtype=topw.dtype)
        w_te = jnp.einsum('tk,tke->te', topw, onehot)
        routed = onehot.sum(axis=1) > 0
        wm = jnp.where(routed, w_te, -1.0)
        sel_w, sel_idx = jax.lax.top_k(wm.T, cap)
        sel_w = jnp.maximum(sel_w, 0.0)
        xg = xf[sel_idx]
        h = jax.nn.gelu(jnp.einsum('ecd,edh->ech', xg, w1) + b1[:, None, :], approximate=False)
        out = jnp.einsum('ech,ehd->ecd', h, w2) + b2[:, None, :]
        weighted = out * sel_w[..., None]
        of = jnp.zeros((T, D), x.dtype).at[sel_idx.reshape(-1)].add(weighted.reshape(-1, D))
        return of.reshape(Bq, Sq, D)

    def _gn(v, G=32, eps=1e-5):
        B_, C_, H_, W_ = v.shape
        g = v.reshape(B_, G, C_ // G, H_, W_)
        m = jnp.mean(g, axis=(2, 3, 4), keepdims=True)
        s = jnp.var(g, axis=(2, 3, 4), keepdims=True)
        return ((g - m) / jnp.sqrt(s + eps)).reshape(v.shape)

    def _ln_c(v, eps=1e-6):
        m = jnp.mean(v, axis=1, keepdims=True)
        s = jnp.var(v, axis=1, keepdims=True)
        return (v - m) / jnp.sqrt(s + eps)

    def _ln_t(v, eps=1e-5):
        m = jnp.mean(v, axis=-1, keepdims=True)
        s = jnp.var(v, axis=-1, keepdims=True)
        return (v - m) / jnp.sqrt(s + eps)

    def _to_tokens(v):
        B_, C_, H_, W_ = v.shape
        return v.reshape(B_, C_, H_ * W_).transpose(0, 2, 1)
    def _from_tokens(t, like):
        B_, C_, H_, W_ = like.shape
        return t.transpose(0, 2, 1).reshape(B_, C_, H_, W_)

    x = x + _L0_conv_ref(_ln_c(x), L0_conv_ln_w, L0_conv_ln_b, L0_conv_in_proj_w, L0_conv_conv_w, L0_conv_conv_b, L0_conv_x_proj_w, L0_conv_dt_proj_w, L0_conv_dt_proj_b, L0_conv_A_log, L0_conv_D_skip, L0_conv_out_proj_w)
    t = _to_tokens(x)
    t = t + _L0_ffn_ref(_ln_t(t), L0_ffn_gate_w, L0_ffn_gate_b, L0_ffn_w1, L0_ffn_b1, L0_ffn_w2, L0_ffn_b2)
    x = _from_tokens(t, x)
    return x


_drawn_inputs = setup_inputs


def setup_inputs(seed=0):
    import zlib

    import numpy as np

    out = dict(_drawn_inputs(seed))
    spreads = {'L0_conv_ln_w': (1.0, 0.6),
     'L0_conv_ln_b': (0.0, 0.8),
     'L0_conv_conv_b': (0.0, 0.799),
     'L0_conv_dt_proj_b': (-4.0, 0.6),
     'L0_conv_D_skip': (1.0, 0.6),
     'L0_ffn_gate_b': (0.0, 2.0),
     'L0_ffn_b1': (0.0, 2.0),
     'L0_ffn_b2': (0.0, 2.0)}
    factors = {'L0_conv_x_proj_w': 8.0,
     'L0_conv_dt_proj_w': 8.0,
     'L0_conv_A_log': 8.0,
     'L0_ffn_gate_w': 8.0,
     'L0_ffn_w1': 8.0,
     'L0_ffn_w2': 8.0}
    for name, (base, spread) in spreads.items():
        noise = np.random.default_rng([zlib.crc32(name.encode()), seed]).standard_normal(out[name].shape)
        drawn = base * np.exp(spread * noise) if base else spread * noise
        out[name] = jnp.asarray(drawn.astype(out[name].dtype))
    for name, factor in factors.items():
        out[name] = (out[name] * factor).astype(out[name].dtype)
    return out
```

```python
from contextlib import ExitStack

import concourse.bass as bass
from concourse import mybir

F32 = mybir.dt.float32
I32 = mybir.dt.int32
ALU = mybir.AluOpType
ACT = mybir.ActivationFunctionType
AX_X = mybir.AxisListType.X

P = 128
EPS_CHANNEL = 1e-6
EPS_MAMBA = 1e-5
EPS_TOKEN = 1e-5
TC = 256
TOPK = 2
CAPACITY_FACTOR = 1.2
ARENA = 48 * 1024 - 0


LOG1P = (-0.0085392045, 0.044089615, -0.10768169, 0.1774524, -0.24495462, 0.3327548, -0.49997404, 0.9999998)


class Arena:

    def __init__(self, tensor, width):
        self.tensor, self.width, self.at = tensor, width, 0

    def take(self, cols, partitions=P):
        view = self.tensor[0:partitions, self.at:self.at + cols]
        self.at += cols
        assert self.at <= self.width, (self.at, self.width)
        return view


def at_least(eng, sem, value):
    if isinstance(value, int) and value <= 0:
        return
    eng.wait_ge(sem, value)


def metaformer_layer(nc, x, x_tok, ln_w, ln_b, in_wT, conv_w, conv_b, xp_wT, dt_wT, dt_b, A_log, D_skip,
                     out_wT, gate_wT, gate_b, w1, b1, w2, b2, out):
    NB, DIM, L = x.shape
    T = NB * L
    KD = DIM // P
    DI = in_wT.shape[1] // 2
    CI = DI // P
    NTAP = conv_w.shape[1] // CI
    HALO = NTAP - 1
    NS = A_log.shape[1] // CI
    R = dt_wT.shape[0]
    XD = xp_wT.shape[1]
    NE, _, HID = w1.shape
    HM = HID // P
    CAP = int(CAPACITY_FACTOR * T / NE)
    IDS = -(-NE * CAP // P) * P
    NT = T // P
    STEPS = L // TC
    W2T = NB * TC
    HN = NS // 2
    SEG = TC + 1
    TT = TC // P
    assert NB == 2 and STEPS % 2 == 0 and STEPS >= 4 and W2T == 512 and DIM == 512

    u_d = nc.dram_tensor("u_d", [DI, T], F32).ap()
    z_d = nc.dram_tensor("z_d", [DI, T], F32).ap()
    xdbl_d = nc.dram_tensor("xdbl_d", [XD, T], F32).ap()
    x1_d = nc.dram_tensor("x1_d", [T, DIM], F32).ap()
    tn_d = nc.dram_tensor("tn_d", [T, DIM], F32).ap()
    ids_d = nc.dram_tensor("ids_d", [IDS, 1], I32).ap()
    y_d = nc.dram_tensor("y_d", [NE * CAP, DIM], F32).ap()

    with ExitStack() as ctx:
        sems = {}

        def sem(name):
            if name not in sems:
                sems[name] = ctx.enter_context(nc.semaphore(name))
            return sems[name]

        arena = Arena(ctx.enter_context(nc.sbuf_tensor("arena", [P, ARENA], F32)), ARENA)
        bank = [ctx.enter_context(nc.psum_tensor(f"bank{i}", [P, 512], F32)) for i in range(8)]

        ident = arena.take(P)
        mean_w = arena.take(P)
        ones = arena.take(P)
        below = arena.take(P)
        weight = arena.take(TOPK * NT)
        weight_v = weight.rearrange("p (k j) -> p k j", k=TOPK)
        logits = arena.take(NT * NE)
        row_i = arena.take(NT * 4).bitcast(I32)
        get_i = arena.take(NT * 2).bitcast(I32)
        LASTING = arena.at

        s_const = sem("constants_made")
        s_phase = sem("engines_through_phase")
        phase_count = {}

        in_w = arena.take(KD * 2 * DI).rearrange("p (k m) -> p k m", k=KD)
        xp_w = arena.take(CI * XD).rearrange("p (c m) -> p c m", c=CI)
        cw = arena.take(CI * NTAP)
        cb = arena.take(CI)
        lw = arena.take(KD)
        lb = arena.take(KD)
        xn = [arena.take(KD * W2T).rearrange("p (k t) -> p k t", k=KD) for _ in range(2)]
        sq = arena.take(KD * W2T).rearrange("p (k t) -> p k t", k=KD)
        rstd = arena.take(W2T)
        xin = arena.take(CI * NB * (TC + HALO)).rearrange("p (c b t) -> p c b t", c=CI, b=NB)
        acc = [arena.take(W2T).rearrange("p (b t) -> p b t", b=NB) for _ in range(2)]
        ub = [arena.take(CI * W2T).rearrange("p (c b t) -> p c b t", c=CI, b=NB) for _ in range(2)]
        zb = [arena.take(CI * W2T).rearrange("p (c b t) -> p c b t", c=CI, b=NB) for _ in range(2)]
        xd = arena.take(W2T, XD)
        proj_ps = bank[0:4]
        mean_ps, var_ps, xd_ps = bank[4], bank[5], bank[6]

        def tok(q, b):
            return bass.ds(q * TC + b * L, TC)

        arena.at = LASTING
        out_w = arena.take(CI * DIM).rearrange("p (c m) -> p c m", c=CI)
        dt_w = arena.take(DI, R + 1)
        A_neg = arena.take(CI * NS)
        dsk = arena.take(CI)
        gate_w = arena.take(KD * NE).rearrange("p (k e) -> p k e", k=KD)
        gate_bb = arena.take(NE)
        state = arena.take(NB * CI * NS).rearrange("p (b c n) -> p b c n", b=NB, c=CI)
        dtT = [arena.take(TC, R + 1) for _ in range(2)]
        Brep = [arena.take(NS * TC).rearrange("p (n t) -> p n t", n=NS) for _ in range(2)]
        Crep = [arena.take(NS * TC).rearrange("p (n t) -> p n t", n=NS) for _ in range(2)]
        delta = [arena.take(CI * TC).rearrange("p (c t) -> p c t", c=CI) for _ in range(2)]
        HC = CI // 2
        sp_e = arena.take(HC * TC)
        sp_l = arena.take(HC * TC)
        RING = 4
        u_t = [arena.take(TC) for _ in range(RING)]
        z_t = [arena.take(TC) for _ in range(RING)]
        du = arena.take(TC)
        dA = [arena.take(HN * SEG) for _ in range(2)]
        hb = [arena.take(HN * SEG) for _ in range(4)]
        y1 = arena.take(TC)
        yg = [arena.take(TC) for _ in range(2)]
        x1 = arena.take(TT * DIM).rearrange("p (a m) -> p a m", a=TT)
        tn = arena.take(TT * DIM).rearrange("p (a m) -> p a m", a=TT)
        tnT = arena.take(DIM)
        bst = arena.take(TT * 6)
        mv = arena.take(TT * 2)
        rs = arena.take(TT)
        newt = arena.take(TT)
        sum_ps = bank[0:2]
        dt_ps = bank[2:4]
        out_ps = bank[4:6]
        tr_ps, lg_ps = bank[6], bank[7]

        def seg(t):
            return t.rearrange("p (n t) -> p n t", n=HN)

        arena.at = LASTING

        def table():
            return arena.take(NE * NT).rearrange("p (e j) -> p e j", e=NE)

        prob, rank, wm, hit, gtm, eqm, posg, posq, tmp, keep = (table() for _ in range(10))
        seg0 = table()
        tmax = arena.take(NT)
        tsum = arena.take(NT)
        pick = arena.take(NT)
        miss = arena.take(NT)
        thr = arena.take(NE).bitcast(I32)
        cand = arena.take(NE).bitcast(I32)
        bit = arena.take(NE).bitcast(I32)
        cnt = arena.take(NE)
        cond = arena.take(NE).bitcast(I32)
        need = arena.take(NE)
        base = arena.take(NE)
        zero_ids = arena.take(IDS // P).bitcast(I32)
        scat = [arena.take(4).bitcast(I32) for _ in range(2)]

        arena.at = LASTING
        w1_s = [arena.take(KD * HID).rearrange("p (k m) -> p k m", k=KD) for _ in range(2)]
        w2_s = arena.take(HM * DIM).rearrange("p (h m) -> p h m", h=HM)
        b1_s = [arena.take(HM) for _ in range(2)]
        b2_s = [arena.take(DIM) for _ in range(2)]
        BLK = 512
        blocks = [(t0, min(BLK, CAP - t0)) for t0 in range(0, CAP, BLK)]
        NBLK = len(blocks)
        BT = BLK // P
        tiles_of = [[(t0 + i, min(P, n - i)) for i in range(0, n, P)] for t0, n in blocks]
        hT = arena.take(HM * BLK).rearrange("p (h t) -> p h t", h=HM)
        xgT = [arena.take(KD * BLK).rearrange("p (k t) -> p k t", k=KD) for _ in range(2)]
        XG = 4
        xg = [arena.take(DIM) for _ in range(XG)]
        gid = [arena.take(1).bitcast(I32) for _ in range(XG)]
        ye = [arena.take(DIM) for _ in range(2)]
        up_ps = bank[0:3]
        dn_ps = bank[3:5]
        xt_ps = bank[5:7]

        arena.at = LASTING
        ER = 4
        e_x1 = [arena.take(DIM) for _ in range(ER)]
        e_y = [[arena.take(DIM) for _ in range(TOPK)] for _ in range(ER)]
        e_o = [arena.take(DIM) for _ in range(ER)]
        e_w = [arena.take(TOPK) for _ in range(ER)]
        e_i = [arena.take(TOPK).bitcast(I32) for _ in range(ER)]

        def carry(eng, register):
            eng.reg_add(register, register, 1)
            eng.reg_sub(register, register, 1)

        def alone(eng):
            eng.wait_ge(s_const, 1)

        def barrier(eng):
            n = phase_count[eng] = phase_count.get(eng, 0) + 1
            eng.drain().then_inc(s_phase, 1)
            eng.wait_ge(s_phase, 5 * n)

        block = ctx.enter_context(nc.Block())

        @block.sync
        def _(sp):
            s_w = sem("A_weights_loaded")
            sp.dma_start(in_w, in_wT.rearrange("(k p) m -> p k m", p=P)).then_inc(s_w, 16)
            sp.dma_start(xp_w, xp_wT.rearrange("(c p) m -> p c m", p=P)).then_inc(s_w, 16)
            for dst, src in ((cw, conv_w), (cb, conv_b), (lw, ln_w), (lb, ln_b)):
                sp.dma_start(dst, src).then_inc(s_w, 16)
            x_v = x.rearrange("b (k p) t -> b p k t", p=P)
            u_v = u_d.rearrange("(c p) t -> p c t", p=P)
            z_v = z_d.rearrange("(c p) t -> p c t", p=P)

            def load_x(q, s):
                at_least(sp, sem("A_projected"), 16 * (q - 1))
                for b in range(NB):
                    sp.dma_start(xn[s][:, :, b * TC:(b + 1) * TC],
                                 x_v[b][:, :, bass.ds(q * TC, TC)]).then_inc(sem(f"A_x_loaded{s}"), 16)

            def store_xdbl(q):
                sp.wait_ge(sem("A_xdbl_copied"), q + 1)
                for b in range(NB):
                    sp.dma_start(xdbl_d[:, tok(q, b)], xd[:, b * TC:(b + 1) * TC]).then_inc(sem("A_xdbl_stored"), 16)

            def step_a(q, s, first, last):
                if not last:
                    load_x(q + 1, 1 - s)
                if not first:
                    store_xdbl(q - 1)
                sp.wait_ge(sem("A_proj_read"), 16 * q + CI)
                for b in range(NB):
                    sp.dma_start(z_v[:, :, tok(q, b)], zb[s][:, :, b, :]).then_inc(sem(f"A_z_stored{s}"), 16)
                sp.wait_ge(sem("A_silu_done"), CI * (q + 1))
                for b in range(NB):
                    sp.dma_start(u_v[:, :, tok(q, b)], ub[s][:, :, b, :]).then_inc(sem(f"A_u_stored{s}"), 16)

            load_x(0, 0)
            step_a(0, 0, True, False)
            with sp.Fori(0, STEPS // 2 - 1) as j:
                step_a(2 * j + 1, 1, False, False)
                step_a(2 * j + 2, 0, False, False)
            step_a(STEPS - 1, 1, False, True)
            store_xdbl(STEPS - 1)
            for name in ("A_z_stored", "A_u_stored"):
                for s in range(2):
                    sp.wait_ge(sem(f"{name}{s}"), 16 * STEPS)
            sp.wait_ge(sem("A_xdbl_stored"), 32 * STEPS)
            barrier(sp)

            s_w = sem("B_weights_loaded")
            sp.dma_start(out_w, out_wT.rearrange("(c p) m -> p c m", p=P)).then_inc(s_w, 16)
            sp.dma_start(dt_w[0:R, :], dt_wT).then_inc(s_w, 16)
            sp.dma_start(dt_w[R:R + 1, :], dt_b).then_inc(s_w, 16)
            sp.dma_start(A_neg, A_log).then_inc(s_w, 16)
            sp.dma_start(dsk, D_skip).then_inc(s_w, 16)
            sp.dma_start(gate_w, gate_wT.rearrange("(k p) e -> p k e", p=P)).then_inc(s_w, 16)
            sp.dma_start(gate_bb, gate_b.broadcast_to([P, NE])).then_inc(s_w, 16)

            def load_dt(q, b):
                n = NB * CI * q + CI * b
                at_least(sp, sem("B_dt_multiplied"), 2 * (2 * q + b - 1))
                sp.dma_start(dtT[b][0:R, :], xdbl_d[0:R, tok(q, b)]).then_inc(sem(f"B_dt_loaded{b}"), 16)
                at_least(sp, sem("B_scanned"), 2 * (n - CI))
                at_least(sp, sem("B_c_multiplied"), 2 * (n - CI))
                for rep, r0 in ((Brep, R), (Crep, R + NS)):
                    src = xdbl_d[r0:r0 + NS, tok(q, b)].rearrange("(a n) t -> a n t", a=1)
                    sp.dma_start(rep[b], src.broadcast_to([P, NS, TC])).then_inc(sem(f"B_bc_loaded{b}"), 16)

            def load_unit(q, b, c):
                n = NB * CI * q + CI * b + c
                at_least(sp, sem("B_gated"), n - RING + 1)
                r = c % RING
                for t, d in ((u_t, u_d), (z_t, z_d)):
                    sp.dma_start(t[r], d[c * P:(c + 1) * P, tok(q, b)]).then_inc(sem(f"B_uz_loaded{r}"), 16)

            def tile_rows(q, b):
                return bass.ds(q * TC + b * L, TC)

            def store_group(q, b):
                g = 2 * q + b
                sp.wait_ge(sem("B_normed"), TT * (g + 1))
                for t, d in ((x1, x1_d), (tn, tn_d)):
                    sp.dma_start(d[tile_rows(q, b), :].rearrange("(a p) m -> p a m", p=P), t)\
                        .then_inc(sem("B_tokens_stored"), 16)

            def load_xt(q, b):
                at_least(sp, sem("B_tokens_stored"), 32 * (2 * q + b))
                sp.dma_start(x1, x_tok[tile_rows(q, b), :].rearrange("(a p) m -> p a m", p=P))\
                    .then_inc(sem("B_xt_loaded"), 16)

            def before(q, b):
                return (q, 0) if b else (q - 1, 1)

            def after(q, b):
                return (q + 1, 0) if b else (q, 1)

            def group_b(q, b, first, last):
                for c in range(CI):
                    load_unit(q, b, c)
                    if c == 4 and not last:
                        load_dt(*after(q, b))
                    if c == 6:
                        if not first:
                            store_group(*before(q, b))
                        load_xt(q, b)

            load_dt(0, 0)
            for b in range(NB):
                group_b(0, b, b == 0, False)
            with sp.Fori(1, STEPS - 1) as q:
                for b in range(NB):
                    group_b(q, b, False, False)
            for b in range(NB):
                group_b(STEPS - 1, b, False, b == 1)
            store_group(STEPS - 1, 1)
            sp.wait_ge(sem("B_tokens_stored"), 32 * NB * STEPS)
            barrier(sp)

            sp.wait_ge(sem("C_zeros"), 1)
            sp.dma_start(ids_d.rearrange("(p a) o -> p (a o)", p=P), zero_ids).then_inc(sem("C_ids_cleared"), 16)
            sp.wait_ge(sem("C_ids_cleared"), 16)
            barrier(sp)

            def load_expert(e, r):
                at_least(sp, sem("D_down_done"), ND * (e - 1))
                at_least(sp, sem("D_y_made"), ND * (e - 1))
                sp.dma_start(w1_s[r], w1[bass.ds(e, 1)].rearrange("e (k p) m -> p (e k) m", p=P)).then_inc(sem(f"D_w1_loaded{r}"), 16)
                sp.dma_start(b1_s[r], b1[bass.ds(e, 1)].rearrange("e p h -> p (e h)")).then_inc(sem(f"D_w1_loaded{r}"), 16)
                sp.dma_start(b2_s[r], b2[bass.ds(e, 1)].broadcast_to([P, DIM])).then_inc(sem(f"D_w1_loaded{r}"), 16)

            ND = sum(map(len, tiles_of))

            def load_w2(e):
                at_least(sp, sem("D_down_done"), ND * e)
                sp.dma_start(w2_s, w2[bass.ds(e, 1)].rearrange("e (h p) m -> p (e h) m", p=P)).then_inc(sem("D_w2_loaded"), 16)

            y_v = y_d.rearrange("(e s) m -> e s m", s=CAP)

            def store_y(e, i):
                t0, n = [t for b in tiles_of for t in b][i]
                sp.wait_ge(sem("D_y_made"), ND * e + i + 1)
                sp.dma_start(y_v[bass.ds(e, 1), t0:t0 + n, :].rearrange("e s m -> (e s) m"), ye[i % 2][0:n, :])\
                    .then_inc(sem(f"D_y_stored{i % 2}"), 16)

            load_expert(0, 0)
            load_w2(0)
            load_expert(1, 1)
            assert ND % 2 == 0

            def expert_d(e, r, last_two, last):
                for i in range(ND):
                    store_y(e, i)
                if not last:
                    load_w2(e + 1)
                if not last_two:
                    load_expert(e + 2, r)

            with sp.Fori(0, NE // 2 - 1) as j:
                for r in range(2):
                    expert_d(2 * j + r, r, False, False)
            for r in range(2):
                expert_d(NE - 2 + r, r, True, r == 1)
            for r in range(2):
                sp.wait_ge(sem(f"D_y_stored{r}"), 16 * NE * ND // 2)
            barrier(sp)

            def load_e(j, r):
                at_least(sp, sem(f"E_summed{r}"), j)
                sp.dma_start(e_x1[r], x1_d[bass.ds(j * (ER * P) + r * P, P), :]).then_inc(sem(f"E_x1_loaded{r}"), 16)

            def store_e(j, r):
                sp.wait_ge(sem(f"E_summed{r}"), j + 1)
                sp.dma_start(out[bass.ds(j * (ER * P) + r * P, P), :], e_o[r]).then_inc(sem(f"E_stored{r}"), 16)

            for r in range(ER):
                load_e(0, r)
            with sp.Fori(0, NT // ER - 1) as j:
                for r in range(ER):
                    store_e(j, r)
                    load_e(j + 1, r)
            for r in range(ER):
                store_e(NT // ER - 1, r)
            for r in range(ER):
                sp.wait_ge(sem(f"E_stored{r}"), 16 * NT // ER)

        @block.gpsimd
        def _(pool):
            pool.memset(ident, 0.0).then_inc(sem("pool_const"), 1)
            pool.memset(below, 1.0).then_inc(sem("pool_const"), 1)
            pool.memset(ones, 1.0).then_inc(s_const, 1)
            pool.memset(mean_w, 1.0 / DIM).then_inc(s_const, 1)
            pool.wait_ge(sem("pool_const"), 2)
            pool.affine_select(out=ident, in_=ident, compare_op=ALU.not_equal, fill=1.0, base=0,
                               pattern=[[-1, P]], channel_multiplier=1).then_inc(s_const, 1)
            pool.affine_select(out=below, in_=below, compare_op=ALU.is_gt, fill=0.0, base=0,
                               pattern=[[1, P]], channel_multiplier=-1).then_inc(s_const, 1)
            barrier(pool)

            def group_b(q, b):
                for c in range(CI):
                    if c == 0:
                        pool.wait_ge(sem(f"B_bc_loaded{b}"), 32 * (q + 1))
                    for h in range(2):
                        m = 2 * (NB * CI * q + CI * b + c) + h
                        pool.wait_ge(sem("B_scanned"), m + 1)
                        hv = seg(hb[m_slot(c, h)])[:, :, 1:SEG]
                        pool.tensor_tensor(hv, hv, Crep[b][:, h * HN:(h + 1) * HN, :], ALU.mult)\
                            .then_inc(sem("B_c_multiplied"), 1)

            def m_slot(c, h):
                return (2 * c + h) % 4

            with pool.Fori(0, STEPS) as q:
                for b in range(NB):
                    group_b(q, b)
            barrier(pool)

            pool.iota(row_i.rearrange("p (j c) -> p j c", c=4)[:, :, 2], pattern=[[P, NT]], base=0,
                      channel_multiplier=1).then_inc(sem("C_token_ids"), 1)
            pool.memset(zero_ids, 0).then_inc(sem("C_zeros"), 1)
            for e in range(NE):
                pool.memset(rank[:, e, :], float(NE - 1 - e)).then_inc(sem("C_tables"), 1)
                pool.memset(base[:, e:e + 1], float(e * CAP)).then_inc(sem("C_tables"), 1)
            pool.memset(seg0, 1.0).then_inc(sem("C_seg"), 1)
            pool.wait_ge(sem("C_seg"), 1)
            pool.memset(seg0[:, :, 0], 0.0).then_inc(sem("C_tables"), 1)
            pool.wait_ge(sem("C_ids_cleared"), 16)
            last_slot = pool.alloc_register("last_slot")
            pool.reg_mov(last_slot, NE * CAP - 1)
            last_token = pool.alloc_register("last_token")
            pool.reg_mov(last_token, T - 1)

            def scatter(j, r):
                pool.wait_ge(sem(f"C_row_copied{r}"), j + 1)
                carry(pool, last_slot)
                for k in range(TOPK):
                    pool.indirect_dma_start(ids_d, bass.IndirectOffsetOnAxis(scat[r][:, k:k + 1], 0),
                                            scat[r][:, 2:3], None, bounds_check=last_slot,
                                            oob_is_err=False).then_inc(sem(f"C_scattered{r}"), 16)

            with pool.Fori(0, NT // 2) as j:
                for r in range(2):
                    scatter(j, r)
            for r in range(2):
                pool.wait_ge(sem(f"C_scattered{r}"), 16 * NT)
            barrier(pool)

            ND = sum(map(len, tiles_of))
            flat = [t for b in tiles_of for t in b]
            ids_v = ids_d[0:NE * CAP, :].rearrange("(e s) o -> e s o", s=CAP)

            def gather(e, i, gslot, use):
                t0, n = flat[i]
                at_least(pool, sem(f"D_transposed{gslot}"), use)
                pool.dma_start(gid[gslot][0:n, :], ids_v[bass.ds(e, 1), t0:t0 + n, :].rearrange("e s o -> (e s) o"))\
                    .then_inc(sem(f"D_ids_loaded{gslot}"), 16)
                pool.wait_ge(sem(f"D_ids_loaded{gslot}"), use * 16 + 16)
                carry(pool, last_token)
                pool.indirect_dma_start(xg[gslot][0:n, :], None, tn_d,
                                        bass.IndirectOffsetOnAxis(gid[gslot][0:n, :], 0),
                                        bounds_check=last_token, oob_is_err=False).then_inc(sem(f"D_gathered{gslot}"), 16)

            with pool.Fori(0, NE // 2) as j:
                for r in range(2):
                    for i in range(ND):
                        w = r * ND + i
                        gather(2 * j + r, i, w % XG, j * (2 * ND // XG) + w // XG)
            assert 2 * ND % XG == 0
            barrier(pool)

            def get_rows(j, r):
                pool.wait_ge(sem(f"E_index_copied{r}"), j + 1)
                carry(pool, last_slot)
                for k in range(TOPK):
                    pool.indirect_dma_start(e_y[r][k], None, y_d,
                                            bass.IndirectOffsetOnAxis(e_i[r][:, k:k + 1], 0),
                                            bounds_check=last_slot, oob_is_err=False)\
                        .then_inc(sem(f"E_rows{r}"), 16)

            with pool.Fori(0, NT // ER) as j:
                for r in range(ER):
                    get_rows(j, r)

        @block.scalar
        def _(act):
            act.wait_ge(sem("A_weights_loaded"), 96)

            def square(q, s):
                act.wait_ge(sem("A_centred"), q + 1)
                at_least(act, sem("A_var_done"), q)
                act.activation(sq, xn[s], ACT.Square).then_inc(sem("A_squared"), 1)

            def root(q):
                act.wait_ge(sem("A_var_scaled"), q + 1)
                act.activation(rstd, rstd, ACT.Sqrt).then_inc(sem("A_rooted"), 1)

            def affine(q, s):
                act.wait_ge(sem("A_scaled"), q + 1)
                for k in range(KD):
                    i = act.activation(xn[s][:, k, :], xn[s][:, k, :], ACT.Identity,
                                       bias=lb[:, k:k + 1], scale=lw[:, k:k + 1])
                i.then_inc(sem("A_xn_ready"), 1)

            def copy_z(q, s, i):
                act.wait_ge(sem("A_projected"), 16 * q + i + 1)
                act.activation(zb[s][:, i], proj_ps[i % 4][:, :].rearrange("p (b t) -> p b t", b=NB), ACT.Silu)\
                    .then_inc(sem("A_proj_read"), 1)

            def copy_xin(q, c):
                act.wait_ge(sem("A_projected"), 16 * q + CI + c + 1)
                if c == 0:
                    at_least(act, sem("A_halo_saved"), q + 1)
                act.activation(xin[:, c, :, HALO:], proj_ps[c % 4][:, :].rearrange("p (b t) -> p b t", b=NB),
                               ACT.Copy).then_inc(sem("A_proj_read"), 1)

            def silu_u(q, s, c):
                act.wait_ge(sem("A_convolved"), CI * q + c + 1)
                act.activation(ub[s][:, c], acc[c % 2], ACT.Silu).then_inc(sem("A_silu_done"), 1)

            def copy_xdbl(q):
                act.wait_ge(sem("A_xdbl_done"), q + 1)
                at_least(act, sem("A_xdbl_stored"), 32 * q)
                act.activation(xd, xd_ps[0:XD, :], ACT.Copy).then_inc(sem("A_xdbl_copied"), 1)

            def step_a(q, s, half, first, last):
                at_least(act, sem(f"A_z_stored{s}"), 32 * half)
                for i in range(4):
                    copy_z(q, s, i)
                if not first:
                    copy_xdbl(q - 1)
                for i in range(4, CI):
                    copy_z(q, s, i)
                at_least(act, sem(f"A_u_stored{s}"), 32 * half)
                for c in range(CI):
                    copy_xin(q, c)
                    if c >= 1:
                        silu_u(q, s, c - 1)
                    if c == 3 and not last:
                        square(q + 1, 1 - s)
                    if c == 6 and not last:
                        root(q + 1)
                silu_u(q, s, CI - 1)
                if not last:
                    affine(q + 1, 1 - s)

            square(0, 0)
            root(0)
            affine(0, 0)
            step_a(0, 0, 0, True, False)
            with act.Fori(0, STEPS // 2 - 1) as j:
                step_a(2 * j + 1, 1, j, False, False)
                step_a(2 * j + 2, 0, j + 1, False, False)
            step_a(STEPS - 1, 1, STEPS // 2 - 1, False, True)
            copy_xdbl(STEPS - 1)
            barrier(act)

            act.wait_ge(sem("B_weights_loaded"), 112)
            nc.scalar.preload_act_table_set("natural_log_exp_and_others")
            act.activation(A_neg, A_neg, ACT.Exp).then_inc(sem("B_a_exp"), 1)
            act.wait_ge(sem("B_a_exp"), 1)
            act.activation(A_neg, A_neg, ACT.Copy, scale=-1.0).then_inc(sem("B_a_ready"), 1)
            act.wait_ge(sem("B_a_ready"), 1)
            act.wait_ge(sem("B_set_up"), 5)

            def softplus(q, b, i):
                g2 = 2 * (2 * q + b) + i
                at_least(act, sem("B_delta_made"), g2)
                act.wait_ge(sem("B_dt_multiplied"), g2 + 1)
                for a in range(2):
                    v = sp_e[:, a * 512:(a + 1) * 512]
                    i_ = act.activation(v, dt_ps[a][:, :], ACT.Abs)
                i_.then_inc(sem("B_abs"), 1)
                act.wait_ge(sem("B_abs"), g2 + 1)
                act.activation(sp_e, sp_e, ACT.Exp, scale=-1.0).then_inc(sem("B_exp"), 1)

            def exps(q, b, c, h):
                m = 2 * (NB * CI * q + CI * b + c) + h
                if c == 0 and h == 0:
                    act.wait_ge(sem("B_delta_made"), 2 * (2 * q + b + 1))
                at_least(act, sem("B_scanned"), m - 1)
                for n in range(HN):
                    i = act.activation(seg(dA[h])[:, n, 1:SEG], delta[b][:, c, :], ACT.Exp,
                                       scale=A_neg[:, c * NS + h * HN + n:c * NS + h * HN + n + 1])
                i.then_inc(sem("B_decays"), 1)

            def token_rstd(q, b):
                g = 2 * q + b
                act.wait_ge(sem("B_stats"), g + 1)
                act.activation(rs, mv.rearrange("p (a c) -> p a c", c=2)[:, :, 1], ACT.Ln).then_inc(sem("B_rs_log"), 1)
                act.wait_ge(sem("B_rs_log"), g + 1)
                act.activation(rs, rs, ACT.Exp, scale=-0.5).then_inc(sem("B_rs"), 1)

            def copy_tnT(q, b, a):
                act.wait_ge(sem("B_transposed"), TT * (2 * q + b) + a + 1)
                at_least(act, sem("B_logits_done"), TT * (2 * q + b) + a)
                act.activation(tnT, tr_ps[:, :], ACT.Copy).then_inc(sem("B_tnT"), 1)

            def before(q, b):
                return (q, 0) if b else (q - 1, 1)

            def after(q, b):
                return (q + 1, 0) if b else (q, 1)

            def group_b(q, b, first, last):
                for c in range(CI):
                    exps(q, b, c, 0)
                    exps(q, b, c, 1)
                    if c in (2, 4) and not last:
                        softplus(*after(q, b), c // 2 - 1)
                    if not first:
                        if c == 2:
                            token_rstd(*before(q, b))
                        if c in (4, 5):
                            copy_tnT(*before(q, b), c - 4)

            for i in range(2):
                softplus(0, 0, i)
            for b in range(NB):
                group_b(0, b, b == 0, False)
            with act.Fori(1, STEPS - 1) as q:
                for b in range(NB):
                    group_b(q, b, False, False)
            for b in range(NB):
                group_b(STEPS - 1, b, False, b == 1)
            token_rstd(STEPS - 1, 1)
            for a in range(TT):
                copy_tnT(STEPS - 1, 1, a)
            barrier(act)

            act.wait_ge(sem("C_shifted"), 1)
            act.activation(prob, prob, ACT.Exp).then_inc(sem("C_exp"), 1)
            barrier(act)

            def gelu(j, r, k, h):
                t0, n = blocks[k]
                up = ((2 * j + r) * NBLK + k) * HM + h
                if k == 0 and h == 0:
                    act.wait_ge(sem(f"D_w1_loaded{r}"), 48 * (j + 1))
                act.wait_ge(sem("D_up_done"), up + 1)
                act.activation(hT[:, h, 0:n], up_ps[h % 3][:, 0:n], ACT.Gelu,
                               bias=b1_s[r][:, h:h + 1]).then_inc(sem("D_gelu"), 1)

            with act.Fori(0, NE // 2) as j:
                for r in range(2):
                    for k in range(NBLK):
                        for h in range(HM):
                            gelu(j, r, k, h)
            barrier(act)

        @block.tensor
        def _(pe):
            pe.wait_ge(s_const, 4)
            pe.wait_ge(sem("A_weights_loaded"), 96)

            def mean(q, s, half):
                pe.wait_ge(sem(f"A_x_loaded{s}"), 32 * (half + 1))
                at_least(pe, sem("A_centred"), q)
                for k in range(KD):
                    i = pe.matmul(mean_ps[:, :], mean_w, xn[s][:, k, :], start=(k == 0), stop=(k == KD - 1))
                i.then_inc(sem("A_mean_done"), 1)

            def var(q):
                pe.wait_ge(sem("A_squared"), q + 1)
                at_least(pe, sem("A_var_scaled"), q)
                for k in range(KD):
                    i = pe.matmul(var_ps[:, :], mean_w, sq[:, k, :], start=(k == 0), stop=(k == KD - 1))
                i.then_inc(sem("A_var_done"), 1)

            def project(q, s, i):
                at_least(pe, sem("A_proj_read"), 16 * q + i - 3)
                m = (CI + i) % (2 * CI)
                for k in range(KD):
                    ins = pe.matmul(proj_ps[i % 4][:, :], in_w[:, k, m * P:(m + 1) * P], xn[s][:, k, :],
                                    start=(k == 0), stop=(k == KD - 1))
                ins.then_inc(sem("A_projected"), 1)

            def xdbl(q, s):
                pe.wait_ge(sem("A_silu_done"), CI * (q + 1))
                at_least(pe, sem("A_xdbl_copied"), q)
                for c in range(CI):
                    i = pe.matmul(xd_ps[0:XD, :], xp_w[:, c, :], ub[s][:, c].rearrange("p b t -> p (b t)"),
                                  start=(c == 0), stop=(c == CI - 1))
                i.then_inc(sem("A_xdbl_done"), 1)

            def step_a(q, s, half, first, last):
                pe.wait_ge(sem("A_xn_ready"), q + 1)
                for i in range(16):
                    if i == 4 and not first:
                        xdbl(q - 1, 1 - s)
                    if i == 8 and not last:
                        mean(q + 1, 1 - s, half + s)
                    if i == 12 and not last:
                        var(q + 1)
                    project(q, s, i)

            mean(0, 0, 0)
            var(0)
            step_a(0, 0, 0, True, False)
            with pe.Fori(0, STEPS // 2 - 1) as j:
                step_a(2 * j + 1, 1, j, False, False)
                step_a(2 * j + 2, 0, j + 1, False, False)
            step_a(STEPS - 1, 1, STEPS // 2 - 1, False, True)
            xdbl(STEPS - 1, 1)
            barrier(pe)

            pe.wait_ge(sem("B_weights_loaded"), 112)
            pe.wait_ge(sem("B_set_up"), 5)

            def dt_product(q, b, i):
                g2 = 2 * (2 * q + b) + i
                if i == 0:
                    pe.wait_ge(sem(f"B_dt_loaded{b}"), 16 * (q + 1))
                at_least(pe, sem("B_delta_made"), g2)
                for a in range(HC):
                    c = i * HC + a
                    ins = pe.matmul(dt_ps[a // 2][:, (a % 2) * TC:(a % 2 + 1) * TC],
                                    dt_w[:, c * P:(c + 1) * P], dtT[b], start=True, stop=True)
                ins.then_inc(sem("B_dt_multiplied"), 1)

            def sums(q, b, c):
                n = NB * CI * q + CI * b + c
                at_least(pe, sem("B_gated"), n - 1)
                for h in range(2):
                    pe.wait_ge(sem("B_c_multiplied"), 2 * n + h + 1)
                    for k in range(HN):
                        ins = pe.matmul(sum_ps[c % 2][:, 0:TC], ident, seg(hb[(2 * c + h) % 4])[:, k, 1:SEG],
                                        start=(h == 0 and k == 0), stop=(h == 1 and k == HN - 1))
                    ins.then_inc(sem("B_summed"), 1)

            def out_product(q, b, c):
                n = NB * CI * q + CI * b + c
                if c == 0:
                    at_least(pe, sem("B_residual_added"), TT * (2 * q + b))
                pe.wait_ge(sem("B_gated"), n + 1)
                for a in range(TT):
                    ins = pe.matmul(out_ps[a][:, :], yg[c % 2][:, a * P:(a + 1) * P], out_w[:, c, :],
                                    start=(c == 0), stop=(c == CI - 1))
                ins.then_inc(sem("B_out_done"), 1)

            def transpose_tn(q, b, a):
                t = TT * (2 * q + b) + a
                pe.wait_ge(sem("B_normed"), t + 1)
                at_least(pe, sem("B_tnT"), t)
                for k in range(KD):
                    ins = pe.transpose(tr_ps[:, k * P:(k + 1) * P], tn[:, a, k * P:(k + 1) * P], ident)
                ins.then_inc(sem("B_transposed"), 1)

            def logit(q, b, a):
                t = TT * (2 * q + b) + a
                pe.wait_ge(sem("B_tnT"), t + 1)
                at_least(pe, sem("B_logits_kept"), t)
                for k in range(KD):
                    ins = pe.matmul(lg_ps[:, 0:NE], tnT[:, k * P:(k + 1) * P], gate_w[:, k, :],
                                    start=(k == 0), stop=(k == KD - 1))
                ins.then_inc(sem("B_logits_done"), 1)

            def before(q, b):
                return (q, 0) if b else (q - 1, 1)

            def after(q, b):
                return (q + 1, 0) if b else (q, 1)

            def group_b(q, b, first, last):
                for c in range(CI):
                    if c in (2, 4) and not last:
                        dt_product(*after(q, b), c // 2 - 1)
                    sums(q, b, c)
                    if c > 0:
                        out_product(q, b, c - 1)
                    elif not first:
                        out_product(*before(q, b), CI - 1)
                    if not first:
                        if c in (3, 4):
                            transpose_tn(*before(q, b), c - 3)
                        if c in (4, 5):
                            logit(*before(q, b), c - 4)

            for i in range(2):
                dt_product(0, 0, i)
            for b in range(NB):
                group_b(0, b, b == 0, False)
            with pe.Fori(1, STEPS - 1) as q:
                for b in range(NB):
                    group_b(q, b, False, False)
            for b in range(NB):
                group_b(STEPS - 1, b, False, b == 1)
            out_product(STEPS - 1, 1, CI - 1)
            for a in range(TT):
                transpose_tn(STEPS - 1, 1, a)
                logit(STEPS - 1, 1, a)
            barrier(pe)

            with pe.Fori(0, 30) as i:
                pe.wait_ge(sem("C_counted"), i + 1)
                pe.matmul(bank[0][:, 0:NE], ones, cnt, start=True, stop=True).then_inc(sem("C_total"), 1)
            pe.wait_ge(sem("C_masks"), 1)
            flat2 = "p e j -> p (e j)"
            pe.matmul(bank[1][:, 0:NE * NT], below, gtm.rearrange(flat2), start=True, stop=True)
            pe.matmul(bank[2][:, 0:NE * NT], ones, gtm.rearrange(flat2), start=True, stop=True)
            pe.matmul(bank[3][:, 0:NE * NT], below, eqm.rearrange(flat2), start=True, stop=True)
            pe.matmul(bank[4][:, 0:NE * NT], ones, eqm.rearrange(flat2), start=True, stop=True)\
                .then_inc(sem("C_prefixes"), 1)
            barrier(pe)

            ND = sum(map(len, tiles_of))
            flat = [t for b in tiles_of for t in b]
            first_of = [sum(len(x_) for x_ in tiles_of[:k]) for k in range(NBLK)]
            assert (2 * NBLK) % 2 == 0

            def transposes(j, w, k):
                for i, (t0, n) in enumerate(tiles_of[k]):
                    o = w * ND + first_of[k] + i
                    pe.wait_ge(sem(f"D_gathered{o % XG}"), 16 * (j * (2 * ND // XG) + o // XG + 1))
                    at_least(pe, sem("D_xt_copied"), j * 2 * ND + o - 1)
                    for kk in range(KD):
                        ins = pe.transpose(xt_ps[o % 2][:, kk * P:kk * P + n], xg[o % XG][0:n, kk * P:(kk + 1) * P],
                                           ident[0:n, 0:n])
                    ins.then_inc(sem(f"D_transposed{o % XG}"), 1)

            def up(j, w, k):
                t0, n = blocks[k]
                e = 2 * j + w
                if k == 0:
                    pe.wait_ge(sem(f"D_w1_loaded{w}"), 48 * (j + 1))
                pe.wait_ge(sem("D_xt_copied"), ND * e + first_of[k] + len(tiles_of[k]))
                for h in range(HM):
                    at_least(pe, sem("D_gelu"), (e * NBLK + k) * HM + h - 2)
                    for kk in range(KD):
                        ins = pe.matmul(up_ps[h % 3][:, 0:n], w1_s[w][:, kk, h * P:(h + 1) * P],
                                        xgT[(w * NBLK + k) % 2][:, kk, 0:n], start=(kk == 0), stop=(kk == KD - 1))
                    ins.then_inc(sem("D_up_done"), 1)

            def down(j, w, k):
                e = 2 * j + w
                if k == 0:
                    pe.wait_ge(sem("D_w2_loaded"), 16 * (e + 1))
                pe.wait_ge(sem("D_gelu"), (e * NBLK + k + 1) * HM)
                for i, (t0, n) in enumerate(tiles_of[k]):
                    o = first_of[k] + i
                    at_least(pe, sem("D_y_made"), ND * e + o - 1)
                    c0 = t0 - blocks[k][0]
                    for h in range(HM):
                        ins = pe.matmul(dn_ps[o % 2][0:n, :], hT[:, h, c0:c0 + n], w2_s[:, h, :],
                                        start=(h == 0), stop=(h == HM - 1))
                    ins.then_inc(sem("D_down_done"), 1)

            def round_d(j, last):
                for w in range(2):
                    for k in range(NBLK):
                        up(j, w, k)
                        if k + 1 < NBLK:
                            transposes(j, w, k + 1)
                        elif w == 0:
                            transposes(j, 1, 0)
                        elif not last:
                            transposes(j + 1, 0, 0)
                        down(j, w, k)

            transposes(0, 0, 0)
            round_d(0, False)
            with pe.Fori(1, NE // 2 - 1) as j:
                round_d(j, False)
            round_d(NE // 2 - 1, True)
            barrier(pe)

        @block.vector
        def _(dve):
            dve.wait_ge(sem("A_weights_loaded"), 96)
            dve.memset(xin[:, :, :, 0:HALO], 0.0).then_inc(sem("A_halo_saved"), 1)

            def over_k(t):
                return t.rearrange("p (o t) -> p o t", o=1).broadcast_to([P, KD, W2T])

            def centre(q, s):
                dve.wait_ge(sem("A_mean_done"), q + 1)
                dve.tensor_tensor(xn[s], xn[s], over_k(mean_ps[:, :]), ALU.subtract).then_inc(sem("A_centred"), 1)

            def scale_var(q):
                dve.wait_ge(sem("A_var_done"), q + 1)
                dve.tensor_scalar(rstd, var_ps[:, :], 1.0 + EPS_MAMBA, EPS_CHANNEL * EPS_MAMBA, ALU.mult, ALU.add)\
                    .then_inc(sem("A_var_scaled"), 1)

            def scale(q, s):
                dve.wait_ge(sem("A_rooted"), q + 1)
                dve.reciprocal(rstd, rstd).then_inc(sem("A_inverted"), 1)
                dve.wait_ge(sem("A_inverted"), q + 1)
                dve.tensor_tensor(xn[s], xn[s], over_k(rstd), ALU.mult).then_inc(sem("A_scaled"), 1)

            def convolve(q, c):
                dve.wait_ge(sem("A_proj_read"), 16 * q + CI + c + 1)
                at_least(dve, sem("A_silu_done"), CI * q + c - 1)
                o = acc[c % 2]
                taps = NTAP - 1
                dve.tensor_scalar(o, xin[:, c, :, 0:TC], cw[:, c * NTAP:c * NTAP + 1], cb[:, c:c + 1], ALU.mult, ALU.add)\
                    .then_inc(sem("A_tap"), 1)
                for k in range(1, NTAP):
                    dve.wait_ge(sem("A_tap"), taps * (CI * q + c) + k)
                    i = dve.scalar_tensor_tensor(out=o, in0=xin[:, c, :, k:k + TC],
                                                 scalar=cw[:, c * NTAP + k:c * NTAP + k + 1], in1=o,
                                                 op0=ALU.mult, op1=ALU.add)
                    i.then_inc(sem("A_tap" if k < taps else "A_convolved"), 1)

            def save_halo(q):
                dve.wait_ge(sem("A_convolved"), CI * (q + 1))
                dve.tensor_copy(xin[:, :, :, 0:HALO], xin[:, :, :, TC:TC + HALO]).then_inc(sem("A_halo_saved"), 1)

            def step_a(q, s, last):
                if not last:
                    centre(q + 1, 1 - s)
                for c in range(CI):
                    convolve(q, c)
                    if c == 4 and not last:
                        scale_var(q + 1)
                    if c == 6 and not last:
                        scale(q + 1, 1 - s)
                save_halo(q)

            centre(0, 0)
            scale_var(0)
            scale(0, 0)
            step_a(0, 0, False)
            with dve.Fori(0, STEPS // 2 - 1) as j:
                step_a(2 * j + 1, 1, False)
                step_a(2 * j + 2, 0, False)
            step_a(STEPS - 1, 1, True)
            barrier(dve)

            for t in dtT:
                dve.memset(t[R:R + 1, :], 1.0).then_inc(sem("B_set_up"), 1)
            dve.memset(state, 0.0).then_inc(sem("B_set_up"), 1)
            for t in dA:
                dve.memset(seg(t)[:, :, 0], 0.0).then_inc(sem("B_set_up"), 1)
            dve.wait_ge(sem("B_weights_loaded"), 112)
            dve.wait_ge(sem("B_set_up"), 5)

            def make_delta(q, b, i):
                g2 = 2 * (2 * q + b) + i
                steps = len(LOG1P)
                dve.wait_ge(sem("B_exp"), g2 + 1)
                dve.tensor_scalar(sp_l, sp_e, LOG1P[0], LOG1P[1], ALU.mult, ALU.add).then_inc(sem("B_horner"), 1)
                for k in range(1, steps):
                    dve.wait_ge(sem("B_horner"), steps * g2 + k)
                    dve.scalar_tensor_tensor(out=sp_l, in0=sp_l, scalar=LOG1P[k] if k > 1 else 0.0, in1=sp_e,
                                             op0=ALU.add, op1=ALU.mult).then_inc(sem("B_horner"), 1)
                dve.wait_ge(sem("B_horner"), steps * (g2 + 1))
                for a in range(2):
                    o = delta[b][:, i * HC + 2 * a:i * HC + 2 * a + 2, :].rearrange("p c t -> p (c t)")
                    ins = dve.scalar_tensor_tensor(out=o, in0=dt_ps[a][:, :], scalar=0.0,
                                                   in1=sp_l[:, a * 512:(a + 1) * 512], op0=ALU.max, op1=ALU.add)
                ins.then_inc(sem("B_delta_made"), 1)

            def scan(q, b, c):
                n = NB * CI * q + CI * b + c
                r = c % RING
                if c == 0:
                    dve.wait_ge(sem("B_delta_made"), 2 * (2 * q + b + 1))
                    dve.wait_ge(sem(f"B_bc_loaded{b}"), 32 * (q + 1))
                dve.wait_ge(sem(f"B_uz_loaded{r}"), 32 * (q * (NB * CI // RING) + (CI * b + c) // RING + 1))
                at_least(dve, sem("B_scanned"), 2 * n)
                dve.tensor_tensor(du, delta[b][:, c, :], u_t[r], ALU.mult).then_inc(sem("B_du"), 1)
                for h in range(2):
                    m = 2 * n + h
                    hs = hb[(2 * c + h) % 4]
                    st = state[:, b, c, h * HN:(h + 1) * HN]
                    at_least(dve, sem("B_summed"), m - 3)
                    dve.tensor_copy(seg(hs)[:, :, 0], st).then_inc(sem("B_started"), 1)
                    if h == 0:
                        dve.wait_ge(sem("B_du"), n + 1)
                    dve.tensor_tensor(seg(hs)[:, :, 1:SEG],
                                      du.rearrange("p (o t) -> p o t", o=1).broadcast_to([P, HN, TC]),
                                      Brep[b][:, h * HN:(h + 1) * HN, :], ALU.mult).then_inc(sem("B_started"), 1)
                    dve.wait_ge(sem("B_started"), 2 * (m + 1))
                    dve.wait_ge(sem("B_decays"), m + 1)
                    dve.tensor_tensor_scan(hs, dA[h], hs, 0.0, ALU.mult, ALU.add).then_inc(sem("B_scan_out"), 1)
                    dve.wait_ge(sem("B_scan_out"), m + 1)
                    dve.tensor_copy(st, seg(hs)[:, :, TC]).then_inc(sem("B_scanned"), 1)

            def gate(q, b, c):
                n = NB * CI * q + CI * b + c
                r = c % RING
                dve.wait_ge(sem("B_summed"), 2 * (n + 1))
                at_least(dve, sem("B_gated"), n)
                dve.scalar_tensor_tensor(out=y1, in0=u_t[r], scalar=dsk[:, c:c + 1], in1=sum_ps[c % 2][:, 0:TC],
                                         op0=ALU.mult, op1=ALU.add).then_inc(sem("B_y1"), 1)
                dve.wait_ge(sem("B_y1"), n + 1)
                at_least(dve, sem("B_out_done"), n - 1)
                dve.tensor_tensor(yg[c % 2], y1, z_t[r], ALU.mult).then_inc(sem("B_gated"), 1)

            def residual(q, b):
                g = 2 * q + b
                dve.wait_ge(sem("B_out_done"), CI * (g + 1))
                dve.wait_ge(sem("B_xt_loaded"), 16 * (g + 1))
                at_least(dve, sem("B_tokens_stored"), 32 * g)
                for a in range(TT):
                    dve.tensor_tensor(x1[:, a, :], out_ps[a][:, :], x1[:, a, :], ALU.add)\
                        .then_inc(sem("B_residual_added"), 1)
                for a in range(TT):
                    dve.wait_ge(sem("B_residual_added"), TT * g + a + 1)
                    dve.bn_stats(bst[:, 6 * a:6 * a + 6], x1[:, a, :]).then_inc(sem("B_bn"), 1)
                for a in range(TT):
                    alone(dve)
                    dve.wait_ge(sem("B_bn"), TT * g + a + 1)
                    dve.bn_aggr(mv[:, 2 * a:2 * a + 2], bst[:, 6 * a:6 * a + 6]).then_inc(sem("B_aggr"), 1)
                dve.wait_ge(sem("B_aggr"), TT * (g + 1))
                v = mv.rearrange("p (a c) -> p a c", c=2)[:, :, 1]
                dve.tensor_scalar(v, v, EPS_TOKEN, None, ALU.add).then_inc(sem("B_stats"), 1)

            def normalise(q, b):
                g = 2 * q + b
                dve.wait_ge(sem("B_rs"), g + 1)
                v = mv.rearrange("p (a c) -> p a c", c=2)[:, :, 1]
                dve.tensor_tensor(newt, rs, rs, ALU.mult).then_inc(sem("B_newton"), 1)
                dve.wait_ge(sem("B_newton"), 4 * g + 1)
                dve.tensor_tensor(newt, newt, v, ALU.mult).then_inc(sem("B_newton"), 1)
                dve.wait_ge(sem("B_newton"), 4 * g + 2)
                dve.tensor_scalar(newt, newt, -0.5, 1.5, ALU.mult, ALU.add).then_inc(sem("B_newton"), 1)
                dve.wait_ge(sem("B_newton"), 4 * g + 3)
                dve.tensor_tensor(rs, rs, newt, ALU.mult).then_inc(sem("B_newton"), 1)
                dve.wait_ge(sem("B_newton"), 4 * g + 4)
                for a in range(TT):
                    dve.tensor_scalar(tn[:, a, :], x1[:, a, :], mv[:, 2 * a:2 * a + 1], rs[:, a:a + 1],
                                      ALU.subtract, ALU.mult).then_inc(sem("B_normed"), 1)

            def keep_logits(q, b, a):
                t = TT * (2 * q + b) + a
                dve.wait_ge(sem("B_logits_done"), t + 1)
                j0 = (q * TT + (b * (L // P) + a)) * NE
                dve.tensor_tensor(logits[:, bass.ds(j0, NE)], lg_ps[:, 0:NE], gate_bb, ALU.add)\
                    .then_inc(sem("B_logits_kept"), 1)

            def before(q, b):
                return (q, 0) if b else (q - 1, 1)

            def after(q, b):
                return (q + 1, 0) if b else (q, 1)

            def group_b(q, b, first, last):
                for c in range(CI):
                    scan(q, b, c)
                    if c > 0:
                        gate(q, b, c - 1)
                    elif not first:
                        gate(*before(q, b), CI - 1)
                    if c in (3, 5) and not last:
                        make_delta(*after(q, b), (c - 3) // 2)
                    if not first:
                        if c == 1:
                            residual(*before(q, b))
                        if c == 2:
                            normalise(*before(q, b))
                        if c in (5, 6):
                            keep_logits(*before(q, b), c - 5)

            for i in range(2):
                make_delta(0, 0, i)
            for b in range(NB):
                group_b(0, b, b == 0, False)
            with dve.Fori(1, STEPS - 1) as q:
                for b in range(NB):
                    group_b(q, b, False, False)
            for b in range(NB):
                group_b(STEPS - 1, b, False, b == 1)
            gate(STEPS - 1, 1, CI - 1)
            residual(STEPS - 1, 1)
            normalise(STEPS - 1, 1)
            for a in range(TT):
                keep_logits(STEPS - 1, 1, a)
            barrier(dve)

            s_chain = sem("C_chain")
            chain = [0]

            def link(ins):
                chain[0] += 1
                ins.then_inc(s_chain, 1)
                dve.wait_ge(s_chain, chain[0])

            def by_tile(t):
                return t.rearrange("p e j -> p j e")

            def over_e(t):
                return t.rearrange("p (o j) -> p o j", o=1).broadcast_to([P, NE, NT])

            def over_j(t):
                return t.rearrange("p (e o) -> p e o", o=1).broadcast_to([P, NE, NT])

            lg = logits.rearrange("p (j e) -> p j e", e=NE)
            link(dve.tensor_reduce(tmax, lg, AX_X, ALU.max))
            dve.tensor_tensor(prob, lg.rearrange("p j e -> p e j"), over_e(tmax), ALU.subtract)\
                .then_inc(sem("C_shifted"), 1)
            dve.wait_ge(sem("C_exp"), 1)
            link(dve.tensor_reduce(tsum, by_tile(prob), AX_X, ALU.add))
            link(dve.reciprocal(tsum, tsum))
            link(dve.tensor_tensor(prob, prob, over_e(tsum), ALU.mult))
            dve.wait_ge(sem("C_tables"), 2 * NE + 1)
            for s in range(1, NE):
                link(dve.tensor_tensor(tmp[:, 0:NE - s], prob[:, 0:NE - s], prob[:, s:NE], ALU.is_ge))
                link(dve.tensor_tensor(rank[:, s:NE], rank[:, s:NE], tmp[:, 0:NE - s], ALU.add))
                link(dve.tensor_tensor(rank[:, 0:NE - s], rank[:, 0:NE - s], tmp[:, 0:NE - s], ALU.subtract))
            link(dve.tensor_scalar(hit, rank, float(TOPK), None, ALU.is_lt))
            link(dve.tensor_tensor(wm, prob, hit, ALU.mult))
            link(dve.scalar_tensor_tensor(out=wm, in0=hit, scalar=1.0, in1=wm, op0=ALU.subtract, op1=ALU.add))
            link(dve.memset(thr, 0))
            link(dve.memset(bit, 1 << 29))
            with dve.Fori(0, 30) as i:
                dve.wait_ge(sem("C_bit_done"), i)
                dve.tensor_tensor(cand, thr, bit, ALU.bitwise_or).then_inc(sem("C_cand"), 1)
                dve.wait_ge(sem("C_cand"), i + 1)
                dve.tensor_tensor(hit, wm, over_j(cand.bitcast(F32)), ALU.is_ge).then_inc(sem("C_hit"), 1)
                dve.wait_ge(sem("C_hit"), i + 1)
                dve.tensor_reduce(cnt, hit, AX_X, ALU.add).then_inc(sem("C_counted"), 1)
                dve.wait_ge(sem("C_total"), i + 1)
                dve.tensor_scalar(cond, bank[0][:, 0:NE], float(CAP), None, ALU.is_ge).then_inc(sem("C_cond"), 1)
                dve.wait_ge(sem("C_cond"), i + 1)
                dve.tensor_tensor(cond, cond, bit, ALU.mult).then_inc(sem("C_gain"), 1)
                dve.wait_ge(sem("C_gain"), i + 1)
                dve.tensor_tensor(thr, thr, cond, ALU.bitwise_or).then_inc(sem("C_thr"), 1)
                dve.wait_ge(sem("C_thr"), i + 1)
                dve.tensor_scalar(bit, bit, 1, None, ALU.logical_shift_right).then_inc(sem("C_bit_done"), 1)
            dve.wait_ge(sem("C_bit_done"), 30)
            link(dve.tensor_tensor(gtm, wm, over_j(thr.bitcast(F32)), ALU.is_gt))
            dve.tensor_tensor(eqm, wm, over_j(thr.bitcast(F32)), ALU.is_equal).then_inc(sem("C_masks"), 1)
            dve.wait_ge(sem("C_prefixes"), 1)
            flat2 = "p e j -> p (e j)"

            def ps(i):
                return bank[i][:, 0:NE * NT]

            for pos, inside, total in ((posg, 1, 2), (posq, 3, 4)):
                link(dve.tensor_tensor_scan(pos.rearrange(flat2), seg0.rearrange(flat2), ps(total), 0.0,
                                            ALU.mult, ALU.add))
                if pos is posg:
                    link(dve.tensor_scalar(need, posg[:, :, NT - 1], -1.0, float(CAP), ALU.mult, ALU.add))
                link(dve.tensor_tensor(pos.rearrange(flat2), pos.rearrange(flat2), ps(total), ALU.subtract))
                link(dve.tensor_tensor(pos.rearrange(flat2), pos.rearrange(flat2), ps(inside), ALU.add))
            link(dve.tensor_tensor(tmp, posq, over_j(need), ALU.is_lt))
            link(dve.tensor_tensor(tmp, tmp, eqm, ALU.mult))
            link(dve.tensor_tensor(keep, gtm, tmp, ALU.add))
            link(dve.tensor_tensor(posq, posq, over_j(need), ALU.min))
            link(dve.tensor_tensor(posg, posg, posq, ALU.add))
            link(dve.tensor_tensor(posg, posg, over_j(base), ALU.add))
            dve.wait_ge(sem("C_token_ids"), 1)
            row_v = row_i.rearrange("p (j c) -> p j c", c=4)
            get_v = get_i.rearrange("p (j c) -> p j c", c=TOPK)
            for k in range(TOPK):
                link(dve.scalar_tensor_tensor(out=hit, in0=rank, scalar=float(k), in1=keep,
                                              op0=ALU.is_equal, op1=ALU.mult))
                link(dve.tensor_tensor(tmp, hit, prob, ALU.mult))
                link(dve.tensor_reduce(weight_v[:, k, :], by_tile(tmp), AX_X, ALU.add))
                link(dve.tensor_tensor(tmp, hit, posg, ALU.mult))
                link(dve.tensor_reduce(pick, by_tile(tmp), AX_X, ALU.add))
                link(dve.tensor_reduce(miss, by_tile(hit), AX_X, ALU.add))
                link(dve.tensor_copy(get_v[:, :, k], pick))
                link(dve.tensor_scalar(miss, miss, -float(2 * NE * CAP), float(2 * NE * CAP), ALU.mult, ALU.add))
                link(dve.tensor_tensor(miss, miss, pick, ALU.add))
                link(dve.tensor_copy(row_v[:, :, k], miss))

            with dve.Fori(0, NT // 2) as j:
                for r in range(2):
                    at_least(dve, sem(f"C_scattered{r}"), 32 * j)
                    dve.tensor_copy(scat[r][:, 0:3], row_i[:, bass.ds(j * 8 + r * 4, 3)])\
                        .then_inc(sem(f"C_row_copied{r}"), 1)
            barrier(dve)

            ND = sum(map(len, tiles_of))
            first_of = [sum(len(x_) for x_ in tiles_of[:k]) for k in range(NBLK)]

            def copy_xt(j, w, k):
                for i, (t0, n) in enumerate(tiles_of[k]):
                    o = w * ND + first_of[k] + i
                    if i == 0:
                        at_least(dve, sem("D_up_done"), HM * (2 * NBLK * j + w * NBLK + k - 1))
                    dve.wait_ge(sem(f"D_transposed{o % XG}"), j * (2 * ND // XG) + o // XG + 1)
                    c0 = t0 - blocks[k][0]
                    dve.tensor_copy(xgT[(w * NBLK + k) % 2][:, :, c0:c0 + n],
                                    xt_ps[o % 2][:, :].rearrange("p (k t) -> p k t", k=KD)[:, :, 0:n])\
                        .then_inc(sem("D_xt_copied"), 1)

            def add_b2(j, w, k):
                e = 2 * j + w
                if k == 0:
                    dve.wait_ge(sem(f"D_w1_loaded{w}"), 48 * (j + 1))
                for i, (t0, n) in enumerate(tiles_of[k]):
                    o = first_of[k] + i
                    dve.wait_ge(sem("D_down_done"), ND * e + o + 1)
                    at_least(dve, sem(f"D_y_stored{o % 2}"), 16 * ((ND // 2) * e + o // 2))
                    dve.tensor_tensor(ye[o % 2][0:n, :], dn_ps[o % 2][0:n, :], b2_s[w][0:n, :], ALU.add)\
                        .then_inc(sem("D_y_made"), 1)

            def round_d(j, last):
                for w in range(2):
                    for k in range(NBLK):
                        if k + 1 < NBLK:
                            copy_xt(j, w, k + 1)
                        elif w == 0:
                            copy_xt(j, 1, 0)
                        elif not last:
                            copy_xt(j + 1, 0, 0)
                        add_b2(j, w, k)

            copy_xt(0, 0, 0)
            round_d(0, False)
            with dve.Fori(1, NE // 2 - 1) as j:
                round_d(j, False)
            round_d(NE // 2 - 1, True)
            barrier(dve)

            def index(j, r):
                at_least(dve, sem(f"E_rows{r}"), 32 * j)
                dve.tensor_copy(e_i[r], get_i[:, bass.ds(j * (ER * TOPK) + r * TOPK, TOPK)]).then_inc(sem(f"E_index_copied{r}"), 1)

            def combine(j, r):
                dve.wait_ge(sem(f"E_x1_loaded{r}"), 16 * (j + 1))
                dve.wait_ge(sem(f"E_rows{r}"), 32 * (j + 1))
                at_least(dve, sem(f"E_stored{r}"), 16 * j)
                for k in range(TOPK):
                    dve.tensor_copy(e_w[r][:, k:k + 1], weight[:, bass.ds(j * ER + (k * NT + r), 1)]).then_inc(sem(f"E_w{r}"), 1)
                dve.wait_ge(sem(f"E_w{r}"), TOPK * (j + 1))
                dve.scalar_tensor_tensor(out=e_o[r], in0=e_y[r][0], scalar=e_w[r][:, 0:1], in1=e_x1[r],
                                         op0=ALU.mult, op1=ALU.add).then_inc(sem(f"E_first{r}"), 1)
                dve.wait_ge(sem(f"E_first{r}"), j + 1)
                dve.scalar_tensor_tensor(out=e_o[r], in0=e_y[r][1], scalar=e_w[r][:, 1:2], in1=e_o[r],
                                         op0=ALU.mult, op1=ALU.add).then_inc(sem(f"E_summed{r}"), 1)

            for r in range(ER):
                index(0, r)
            with dve.Fori(0, NT // ER - 1) as j:
                for r in range(ER):
                    combine(j, r)
                    index(j + 1, r)
            for r in range(ER):
                combine(NT // ER - 1, r)


def kernel(x, L0_conv_ln_w, L0_conv_ln_b, L0_conv_in_proj_w, L0_conv_conv_w, L0_conv_conv_b, L0_conv_x_proj_w,
           L0_conv_dt_proj_w, L0_conv_dt_proj_b, L0_conv_A_log, L0_conv_D_skip, L0_conv_out_proj_w,
           L0_ffn_gate_w, L0_ffn_gate_b, L0_ffn_w1, L0_ffn_b1, L0_ffn_w2, L0_ffn_b2):
    import numpy as np
    import concourse.bacc as bacc
    from concourse.bass_utils import run_bass_kernel_spmd as run

    x = np.asarray(x)
    NB, DIM, H, W = x.shape

    def tiles(a):
        a = np.asarray(a)
        a = a.reshape(a.shape[0] // 128, 128, -1)
        return a.transpose(1, 0, 2).reshape(128, -1)

    b1 = np.asarray(L0_ffn_b1)
    arrays = {
        "x": x.reshape(NB, DIM, H * W),
        "x_tok": x.reshape(NB, DIM, H * W).transpose(0, 2, 1).reshape(NB * H * W, DIM),
        "ln_w": tiles(L0_conv_ln_w),
        "ln_b": tiles(L0_conv_ln_b),
        "in_wT": np.asarray(L0_conv_in_proj_w).T,
        "conv_w": tiles(L0_conv_conv_w),
        "conv_b": tiles(L0_conv_conv_b),
        "xp_wT": np.asarray(L0_conv_x_proj_w).T,
        "dt_wT": np.asarray(L0_conv_dt_proj_w).T,
        "dt_b": np.asarray(L0_conv_dt_proj_b).reshape(1, -1),
        "A_log": tiles(L0_conv_A_log),
        "D_skip": tiles(L0_conv_D_skip),
        "out_wT": np.asarray(L0_conv_out_proj_w).T,
        "gate_wT": np.asarray(L0_ffn_gate_w).T,
        "gate_b": np.asarray(L0_ffn_gate_b).reshape(1, -1),
        "w1": np.asarray(L0_ffn_w1),
        "b1": b1.reshape(b1.shape[0], -1, 128).transpose(0, 2, 1),
        "w2": np.asarray(L0_ffn_w2),
        "b2": np.asarray(L0_ffn_b2),
    }
    arrays = {f"in_{k}": np.ascontiguousarray(a) for k, a in arrays.items()}
    nc = bacc.Bacc("TRN2", target_bir_lowering=False, num_devices=1)
    args = [nc.dram_tensor(k, a.shape, mybir.dt.from_np(a.dtype), kind="ExternalInput").ap()
            for k, a in arrays.items()]
    out = nc.dram_tensor("out_dram", (NB * H * W, DIM), F32, kind="ExternalOutput").ap()
    metaformer_layer(nc, *args, out)
    r = run(nc, [arrays], core_ids=[0])
    y = r.results[0]["out_dram"]
    return np.ascontiguousarray(y.reshape(NB, H * W, DIM).transpose(0, 2, 1)).reshape(NB, DIM, H, W)
```

```python
from contextlib import ExitStack

import concourse.bass as bass
from concourse import mybir

F32 = mybir.dt.float32
I32 = mybir.dt.int32
ALU = mybir.AluOpType
ACT = mybir.ActivationFunctionType
AX_X = mybir.AxisListType.X

P = 128
EPS_CHANNEL = 1e-6
EPS_MAMBA = 1e-5
EPS_TOKEN = 1e-5
TC = 256
TOPK = 2
CAPACITY_FACTOR = 1.2
NPOOL = 4
ARENA = 48 * 1024


LOG_LEAD = -0.0085392045
LOG_ROOT = 2.4858158
LOG_SQUARES = ((-1.8699235, 1.9141982), (-0.41215122, 3.5825396), (0.94338274, 1.4303126))


class Arena:

    def __init__(self, tensor, width):
        self.tensor, self.width, self.at = tensor, width, 0

    def take(self, cols, partitions=P):
        view = self.tensor[0:partitions, self.at:self.at + cols]
        self.at += cols
        assert self.at <= self.width, (self.at, self.width)
        return view


def at_least(eng, sem, value):
    if isinstance(value, int) and value <= 0:
        return
    eng.wait_ge(sem, value)


def metaformer_layer(nc, x, x_tok, ln_w, ln_b, in_wT, conv_w, conv_b, xp_wT, dt_wT, dt_b, A_log, D_skip,
                     out_wT, gate_wT, gate_b, w1, b1, w2, b2, out):
    NB, DIM, L = x.shape
    T = NB * L
    KD = DIM // P
    DI = in_wT.shape[1] // 2
    CI = DI // P
    NTAP = conv_w.shape[1] // CI
    HALO = NTAP - 1
    NS = A_log.shape[1] // CI
    R = dt_wT.shape[0]
    XD = xp_wT.shape[1]
    NE, _, HID = w1.shape
    HM = HID // P
    CAP = int(CAPACITY_FACTOR * T / NE)
    TILES = -(-CAP // P)
    NT = T // P
    STEPS = L // TC
    W2T = NB * TC
    HN = NS // 2
    SEG = TC + 1
    TT = TC // P
    assert NB == 2 and STEPS % 2 == 0 and STEPS >= 4 and W2T == 512 and DIM == 512

    u_d = nc.dram_tensor("u_d", [DI, T], F32).ap()
    z_d = nc.dram_tensor("z_d", [DI, T], F32).ap()
    xdbl_d = nc.dram_tensor("xdbl_d", [XD, T], F32).ap()
    tn_d = nc.dram_tensor("tn_d", [T, DIM], F32).ap()

    with ExitStack() as ctx:
        sems = {}

        def sem(name):
            if name not in sems:
                sems[name] = ctx.enter_context(nc.semaphore(name))
            return sems[name]

        arena = Arena(ctx.enter_context(nc.sbuf_tensor("arena", [P, ARENA], F32)), ARENA)
        bank = [ctx.enter_context(nc.psum_tensor(f"bank{i}", [P, 512], F32)) for i in range(8)]

        ident = arena.take(P)
        mean_w = arena.take(P)
        ones = arena.take(P)
        below = arena.take(P)
        logits = arena.take(NT * NE)
        slot_get = arena.take(NE * TILES).bitcast(I32)
        slot_put = arena.take(NE * TILES).bitcast(I32)
        slot_w = arena.take(NE * TILES)
        LASTING = arena.at

        s_const = sem("constants_made")
        s_phase = sem("engines_through_phase")
        phase_count = {}

        in_w = arena.take(KD * 2 * DI).rearrange("p (k m) -> p k m", k=KD)
        xp_w = arena.take(CI * XD).rearrange("p (c m) -> p c m", c=CI)
        cw = arena.take(CI * NTAP)
        cb = arena.take(CI)
        lw = arena.take(KD)
        lb = arena.take(KD)
        xn = [arena.take(KD * W2T).rearrange("p (k t) -> p k t", k=KD) for _ in range(2)]
        sq = arena.take(KD * W2T).rearrange("p (k t) -> p k t", k=KD)
        rstd = arena.take(W2T)
        xin = arena.take(CI * NB * (TC + HALO)).rearrange("p (c b t) -> p c b t", c=CI, b=NB)
        acc = [arena.take(W2T).rearrange("p (b t) -> p b t", b=NB) for _ in range(2)]
        ub = [arena.take(CI * W2T).rearrange("p (c b t) -> p c b t", c=CI, b=NB) for _ in range(2)]
        zb = [arena.take(CI * W2T).rearrange("p (c b t) -> p c b t", c=CI, b=NB) for _ in range(2)]
        xd = arena.take(W2T, XD)
        proj_ps = bank[0:4]
        mean_ps, var_ps, xd_ps = bank[4], bank[5], bank[6]

        def tok(q, b):
            return bass.ds(q * TC + b * L, TC)

        arena.at = LASTING
        out_w = arena.take(CI * DIM).rearrange("p (c m) -> p c m", c=CI)
        dt_w = arena.take(DI, R + 1)
        A_neg = arena.take(CI * NS)
        dsk = arena.take(CI)
        gate_w = arena.take(KD * NE).rearrange("p (k e) -> p k e", k=KD)
        gate_bb = arena.take(NE)
        state = arena.take(NB * CI * NS).rearrange("p (b c n) -> p b c n", b=NB, c=CI)
        dtT = [arena.take(TC, R + 1) for _ in range(2)]
        Brep = [arena.take(NS * TC).rearrange("p (n t) -> p n t", n=NS) for _ in range(2)]
        Crep = [arena.take(NS * TC).rearrange("p (n t) -> p n t", n=NS) for _ in range(2)]
        delta = [arena.take(CI * TC).rearrange("p (c t) -> p c t", c=CI) for _ in range(2)]
        HC = CI // 2
        sp_e = arena.take(HC * TC)
        sp_l = arena.take(HC * TC)
        sp_q = arena.take(HC * TC)
        log_a = arena.take(len(LOG_SQUARES))
        RING = 4
        u_t = [arena.take(TC) for _ in range(RING)]
        z_t = [arena.take(TC) for _ in range(RING)]
        du = [arena.take(TC) for _ in range(2)]
        dA = [arena.take(HN * SEG) for _ in range(2)]
        hb = [arena.take(HN * SEG) for _ in range(4)]
        yg = [arena.take(TC) for _ in range(2)]
        x1 = arena.take(TT * DIM).rearrange("p (a m) -> p a m", a=TT)
        tn = arena.take(TT * DIM).rearrange("p (a m) -> p a m", a=TT)
        tnT = arena.take(DIM)
        bst = arena.take(TT * 6)
        mv = arena.take(TT * 2)
        rs = arena.take(TT)
        newt = arena.take(TT)
        sum_ps = bank[0:2]
        dt_ps = bank[2:4]
        out_ps = bank[4:6]
        tr_ps, lg_ps = bank[6], bank[7]

        PE_DT = (0, 2)
        ACT_RELU = (4, 8)
        ACT_EXP = (4, 10)
        ACT_SQUARE = (5, 7, 9, 11, 13, 15)
        DVE_LOG = (5, 5, 7, 9, 10, 11, 11, 13, 15, 15)
        LOG_STEPS = len(LOG_SQUARES) + 2

        def seg(t):
            return t.rearrange("p (n t) -> p n t", n=HN)

        arena.at = LASTING
        w1_s = [arena.take(KD * HID).rearrange("p (k m) -> p k m", k=KD) for _ in range(2)]
        w2_s = arena.take(HM * DIM).rearrange("p (h m) -> p h m", h=HM)
        b1_s = [arena.take(HM) for _ in range(2)]
        b2_s = [arena.take(DIM) for _ in range(2)]
        EXPERT_WEIGHTS = arena.at


        def table():
            return arena.take(NE * NT).rearrange("p (e j) -> p e j", e=NE)

        prob, rank, wm, hit, gtm, eqm, posg, posq, tmp, keep = (table() for _ in range(10))
        seg0 = table()
        tmax = arena.take(NT)
        tsum = arena.take(NT)
        pick = arena.take(NT)
        miss = arena.take(NT)
        thr = arena.take(NE).bitcast(I32)
        cand = arena.take(NE).bitcast(I32)
        bit = arena.take(NE).bitcast(I32)
        cnt = arena.take(NE)
        cond = arena.take(NE).bitcast(I32)
        need = arena.take(NE)
        base = arena.take(NE)
        word = arena.take(TOPK * NT).bitcast(I32)
        NCOL = 1 + 3 * TOPK
        cols = arena.take(NT * NCOL)
        cols_v = cols.rearrange("p (j c) -> p j c", c=NCOL)
        tile_cols = [arena.take(NCOL) for _ in range(2)]
        count_i = arena.take(P).bitcast(I32)
        count = arena.take(P)
        token_i = arena.take(NT).bitcast(I32)
        ROWS = NE * TILES
        lo_hot = [arena.take(P) for _ in range(2 * TOPK)]
        hi_hot = [arena.take(2 * ROWS) for _ in range(2 * TOPK)]
        zeros = arena.take(max(P, 2 * ROWS))
        found = arena.take(ROWS)
        table_ps = bank[5][:, 0:2 * ROWS]

        arena.at = EXPERT_WEIGHTS
        BLK = 512
        blocks = [(t0, min(BLK, CAP - t0)) for t0 in range(0, CAP, BLK)]
        NBLK = len(blocks)
        BT = BLK // P
        tiles_of = [[(t0 + i, min(P, n - i)) for i in range(0, n, P)] for t0, n in blocks]
        hT = arena.take(HM * BLK).rearrange("p (h t) -> p h t", h=HM)
        xgT = [arena.take(KD * BLK).rearrange("p (k t) -> p k t", k=KD) for _ in range(2)]
        XG = 4
        xg = [arena.take(DIM) for _ in range(XG)]
        get = [arena.take(1).bitcast(I32) for _ in range(XG)]
        put = [arena.take(1).bitcast(I32) for _ in range(2)]
        put_w = [arena.take(1) for _ in range(2)]
        ye = [arena.take(DIM) for _ in range(2)]
        up_ps = bank[0:3]
        dn_ps = bank[3:5]
        xt_ps = bank[5:7]

        ND = TILES
        flat = [t for b in tiles_of for t in b]
        first_of = [sum(len(x_) for x_ in tiles_of[:k]) for k in range(NBLK)]
        assert len(flat) == ND and ND % 2 == 0 and 2 * ND % XG == 0 and (XG <= ND)

        def carry(eng, register):
            eng.reg_add(register, register, 1)
            eng.reg_sub(register, register, 1)

        def alone(eng):
            eng.wait_ge(s_const, 1)

        def barrier(eng):
            n = phase_count[eng] = phase_count.get(eng, 0) + 1
            eng.drain().then_inc(s_phase, 1)
            eng.wait_ge(s_phase, 5 * n)

        block = ctx.enter_context(nc.Block())

        @block.sync
        def _(sp):
            s_w = sem("A_weights_loaded")
            sp.dma_start(in_w, in_wT.rearrange("(k p) m -> p k m", p=P)).then_inc(s_w, 16)
            sp.dma_start(xp_w, xp_wT.rearrange("(c p) m -> p c m", p=P)).then_inc(s_w, 16)
            for dst, src in ((cw, conv_w), (cb, conv_b), (lw, ln_w), (lb, ln_b)):
                sp.dma_start(dst, src).then_inc(s_w, 16)
            x_v = x.rearrange("b (k p) t -> b p k t", p=P)
            u_v = u_d.rearrange("(c p) t -> p c t", p=P)
            z_v = z_d.rearrange("(c p) t -> p c t", p=P)

            def load_x(q, s):
                at_least(sp, sem("A_projected"), 16 * (q - 1))
                for b in range(NB):
                    sp.dma_start(xn[s][:, :, b * TC:(b + 1) * TC],
                                 x_v[b][:, :, bass.ds(q * TC, TC)]).then_inc(sem(f"A_x_loaded{s}"), 16)

            def store_xdbl(q):
                sp.wait_ge(sem("A_xdbl_copied"), q + 1)
                for b in range(NB):
                    sp.dma_start(xdbl_d[:, tok(q, b)], xd[:, b * TC:(b + 1) * TC]).then_inc(sem("A_xdbl_stored"), 16)

            def step_a(q, s, first, last):
                if not last:
                    load_x(q + 1, 1 - s)
                if not first:
                    store_xdbl(q - 1)
                sp.wait_ge(sem("A_proj_read"), 16 * q + CI)
                for b in range(NB):
                    sp.dma_start(z_v[:, :, tok(q, b)], zb[s][:, :, b, :]).then_inc(sem(f"A_z_stored{s}"), 16)
                sp.wait_ge(sem("A_silu_done"), CI * (q + 1))
                for b in range(NB):
                    sp.dma_start(u_v[:, :, tok(q, b)], ub[s][:, :, b, :]).then_inc(sem(f"A_u_stored{s}"), 16)

            load_x(0, 0)
            step_a(0, 0, True, False)
            step_a(1, 1, False, False)
            with sp.Fori(1, STEPS // 2 - 1) as j:
                step_a(2 * j, 0, False, False)
                step_a(2 * j + 1, 1, False, False)
            step_a(STEPS - 2, 0, False, False)
            step_a(STEPS - 1, 1, False, True)
            store_xdbl(STEPS - 1)
            for name in ("A_z_stored", "A_u_stored"):
                for s in range(2):
                    sp.wait_ge(sem(f"{name}{s}"), 16 * STEPS)
            sp.wait_ge(sem("A_xdbl_stored"), 32 * STEPS)
            barrier(sp)

            s_w = sem("B_weights_loaded")
            sp.dma_start(out_w, out_wT.rearrange("(c p) m -> p c m", p=P)).then_inc(s_w, 16)
            sp.dma_start(dt_w[0:R, :], dt_wT).then_inc(s_w, 16)
            sp.dma_start(dt_w[R:R + 1, :], dt_b).then_inc(s_w, 16)
            sp.dma_start(A_neg, A_log).then_inc(s_w, 16)
            sp.dma_start(dsk, D_skip).then_inc(s_w, 16)
            sp.dma_start(gate_w, gate_wT.rearrange("(k p) e -> p k e", p=P)).then_inc(s_w, 16)
            sp.dma_start(gate_bb, gate_b.broadcast_to([P, NE])).then_inc(s_w, 16)

            def load_dt(q, b):
                at_least(sp, sem("B_dt_multiplied"), 2 * (2 * q + b - 1))
                sp.dma_start(dtT[b][0:R, :], xdbl_d[0:R, tok(q, b)]).then_inc(sem(f"B_dt_loaded{b}"), 16)

            def load_bc(q, b):
                n = NB * CI * q + CI * b
                at_least(sp, sem("B_scanned"), 2 * (n - CI))
                at_least(sp, sem("B_c_multiplied"), 2 * (n - CI))
                for rep, r0 in ((Brep, R), (Crep, R + NS)):
                    src = xdbl_d[r0:r0 + NS, tok(q, b)].rearrange("(a n) t -> a n t", a=1)
                    sp.dma_start(rep[b], src.broadcast_to([P, NS, TC])).then_inc(sem(f"B_bc_loaded{b}"), 16)

            def load_unit(q, b, c):
                n = NB * CI * q + CI * b + c
                at_least(sp, sem("B_gated"), n - RING + 1)
                r = c % RING
                for t, d in ((u_t, u_d), (z_t, z_d)):
                    sp.dma_start(t[r], d[c * P:(c + 1) * P, tok(q, b)]).then_inc(sem(f"B_uz_loaded{r}"), 16)

            def tile_rows(q, b):
                return bass.ds(q * TC + b * L, TC)

            def store_group(q, b):
                g = 2 * q + b
                sp.wait_ge(sem("B_normed"), TT * (g + 1))
                for t, d in ((x1, out), (tn, tn_d)):
                    sp.dma_start(d[tile_rows(q, b), :].rearrange("(a p) m -> p a m", p=P), t)\
                        .then_inc(sem("B_tokens_stored"), 16)

            def load_xt(q, b):
                at_least(sp, sem("B_tokens_stored"), 32 * (2 * q + b))
                sp.dma_start(x1, x_tok[tile_rows(q, b), :].rearrange("(a p) m -> p a m", p=P))\
                    .then_inc(sem("B_xt_loaded"), 16)

            def before(q, b):
                return (q, 0) if b else (q - 1, 1)

            def after(q, b):
                return (q + 1, 0) if b else (q, 1)

            def group_b(q, b, first, last):
                for c in range(CI):
                    load_unit(q, b, c)
                    if c == 0 and not last:
                        load_dt(*after(q, b))
                    if c == 4 and not last:
                        load_bc(*after(q, b))
                    if c == 6 and not first:
                        store_group(*before(q, b))
                    if c == 7:
                        load_xt(q, b)

            load_dt(0, 0)
            load_bc(0, 0)
            for b in range(NB):
                group_b(0, b, b == 0, False)
            with sp.Fori(1, STEPS - 1) as q:
                for b in range(NB):
                    group_b(q, b, False, False)
            for b in range(NB):
                group_b(STEPS - 1, b, False, b == 1)
            store_group(STEPS - 1, 1)
            sp.wait_ge(sem("B_tokens_stored"), 32 * NB * STEPS)
            barrier(sp)

            def load_expert(e, r):
                at_least(sp, sem("D_down_done"), ND * (e - 1))
                at_least(sp, sem("D_biased"), ND * (e - 1))
                sp.dma_start(w1_s[r], w1[bass.ds(e, 1)].rearrange("e (k p) m -> p (e k) m", p=P)).then_inc(sem(f"D_w1_loaded{r}"), 16)
                sp.dma_start(b1_s[r], b1[bass.ds(e, 1)].rearrange("e p h -> p (e h)")).then_inc(sem(f"D_w1_loaded{r}"), 16)
                sp.dma_start(b2_s[r], b2[bass.ds(e, 1)].broadcast_to([P, DIM])).then_inc(sem(f"D_w1_loaded{r}"), 16)

            def load_w2(e):
                at_least(sp, sem("D_down_done"), ND * e)
                sp.dma_start(w2_s, w2[bass.ds(e, 1)].rearrange("e (h p) m -> p (e h) m", p=P)).then_inc(sem("D_w2_loaded"), 16)

            load_expert(0, 0)
            load_w2(0)
            load_expert(1, 1)
            barrier(sp)

            with sp.Fori(0, NE // 2 - 1) as j:
                for r in range(2):
                    load_w2(2 * j + r + 1)
                    load_expert(2 * j + r + 2, r)
            load_w2(NE - 1)
            barrier(sp)

        @block.gpsimd
        def _(pool):
            pool.memset(ident, 0.0).then_inc(sem("pool_const"), 1)
            pool.memset(below, 1.0).then_inc(sem("pool_const"), 1)
            pool.memset(ones, 1.0).then_inc(s_const, 1)
            pool.memset(mean_w, 1.0 / DIM).then_inc(s_const, 1)
            pool.wait_ge(sem("pool_const"), 2)
            pool.affine_select(out=ident, in_=ident, compare_op=ALU.not_equal, fill=1.0, base=0,
                               pattern=[[-1, P]], channel_multiplier=1).then_inc(s_const, 1)
            pool.affine_select(out=below, in_=below, compare_op=ALU.is_gt, fill=0.0, base=0,
                               pattern=[[1, P]], channel_multiplier=-1).then_inc(s_const, 1)
            barrier(pool)

            def m_slot(c, h):
                return (2 * c + h) % 4

            def inputs(q, b, c):
                n = NB * CI * q + CI * b + c
                pool.wait_ge(sem("B_du"), n + 1)
                at_least(pool, sem("B_summed"), 2 * n + 1 - 3)
                if c == 0:
                    pool.wait_ge(sem(f"B_bc_loaded{b}"), 32 * (q + 1))
                pool.tensor_tensor(seg(hb[m_slot(c, 1)])[:, HN - NPOOL:, 1:SEG],
                                   du[c % 2].rearrange("p (o t) -> p o t", o=1).broadcast_to([P, NPOOL, TC]),
                                   Brep[b][:, NS - NPOOL:, :], ALU.mult).then_inc(sem("B_pool_started"), 1)

            def times_c(q, b, c, h):
                m = 2 * (NB * CI * q + CI * b + c) + h
                pool.wait_ge(sem("B_state_kept"), m + 1)
                hv = seg(hb[m_slot(c, h)])[:, :, 1:SEG]
                pool.tensor_tensor(hv, hv, Crep[b][:, h * HN:(h + 1) * HN, :], ALU.mult)\
                    .then_inc(sem("B_c_multiplied"), 1)

            def group_b(q, b, first):
                for c in range(CI):
                    inputs(q, b, c)
                    if c > 0:
                        times_c(q, b, c - 1, 1)
                    elif not first:
                        times_c(*((q, 0) if b else (q - 1, 1)), CI - 1, 1)
                    times_c(q, b, c, 0)

            for b in range(NB):
                group_b(0, b, b == 0)
            with pool.Fori(1, STEPS) as q:
                for b in range(NB):
                    group_b(q, b, False)
            times_c(STEPS - 1, 1, CI - 1, 1)
            barrier(pool)

            pool.iota(token_i, pattern=[[P, NT]], base=1, channel_multiplier=1).then_inc(sem("C_tables"), 1)
            pool.iota(count_i, pattern=[[1, P]], base=0, channel_multiplier=0).then_inc(sem("C_tables"), 1)
            for e in range(NE):
                pool.memset(rank[:, e, :], float(NE - 1 - e)).then_inc(sem("C_tables"), 1)
                pool.memset(base[:, e:e + 1], float(e * TILES * P)).then_inc(sem("C_tables"), 1)
            pool.memset(zeros, 0.0).then_inc(sem("C_zeros"), 1)
            pool.memset(seg0, 1.0).then_inc(sem("C_seg"), 1)
            pool.wait_ge(sem("C_seg"), 1)
            pool.memset(seg0[:, :, 0], 0.0).then_inc(sem("C_tables"), 1)
            last_token = pool.alloc_register("last_token")
            pool.reg_mov(last_token, T - 1)
            barrier(pool)

            def gather(j, w, i):
                o = w * ND + i
                n = flat[i][1]
                at_least(pool, sem(f"D_transposed{o % XG}"), j * (2 * ND // XG) + o // XG)
                pool.wait_ge(sem("D_get_ready"), 2 * ND * j + o + 1)
                carry(pool, last_token)
                pool.indirect_dma_start(xg[o % XG][0:n, :], None, tn_d,
                                        bass.IndirectOffsetOnAxis(get[o % XG][0:n, :], 0),
                                        bounds_check=last_token, oob_is_err=False)\
                    .then_inc(sem(f"D_gathered{o % XG}"), 16)

            def gathers(j, w, k):
                for i in range(len(tiles_of[k])):
                    gather(j, w, first_of[k] + i)

            def adds(j, w, k):
                e = 2 * j + w
                if k == 0:
                    for p in range(2):
                        at_least(pool, sem(f"D_added{p}"), 16 * (ND // 2) * e)
                for i in range(first_of[k], first_of[k] + len(tiles_of[k])):
                    n = flat[i][1]
                    pool.wait_ge(sem("D_weighted"), ND * e + i + 1)
                    carry(pool, last_token)
                    pool.indirect_dma_start(out, bass.IndirectOffsetOnAxis(put[i % 2][0:n, :], 0),
                                            ye[i % 2][0:n, :], None, bounds_check=last_token,
                                            oob_is_err=False, compute_op=ALU.add)\
                        .then_inc(sem(f"D_added{i % 2}"), 16)

            def round_d(j, last):
                for w in range(2):
                    for k in range(NBLK):
                        if k + 1 < NBLK:
                            gathers(j, w, k + 1)
                        elif w == 0:
                            gathers(j, 1, 0)
                        elif not last:
                            gathers(j + 1, 0, 0)
                        adds(j, w, k)

            gathers(0, 0, 0)
            round_d(0, False)
            with pool.Fori(1, NE // 2 - 1) as j:
                round_d(j, False)
            round_d(NE // 2 - 1, True)
            for p in range(2):
                pool.wait_ge(sem(f"D_added{p}"), 16 * (ND // 2) * NE)
            barrier(pool)

        @block.scalar
        def _(act):
            act.wait_ge(sem("A_weights_loaded"), 96)

            def square(q, s):
                act.wait_ge(sem("A_centred"), q + 1)
                at_least(act, sem("A_var_done"), q)
                act.activation(sq, xn[s], ACT.Square).then_inc(sem("A_squared"), 1)

            def root(q):
                act.wait_ge(sem("A_var_scaled"), q + 1)
                act.activation(rstd, rstd, ACT.Sqrt).then_inc(sem("A_rooted"), 1)

            def affine(q, s):
                act.wait_ge(sem("A_scaled"), q + 1)
                for k in range(KD):
                    i = act.activation(xn[s][:, k, :], xn[s][:, k, :], ACT.Identity,
                                       bias=lb[:, k:k + 1], scale=lw[:, k:k + 1])
                i.then_inc(sem("A_xn_ready"), 1)

            def copy_z(q, s, i):
                act.wait_ge(sem("A_projected"), 16 * q + i + 1)
                act.activation(zb[s][:, i], proj_ps[i % 4][:, :].rearrange("p (b t) -> p b t", b=NB), ACT.Silu)\
                    .then_inc(sem("A_proj_read"), 1)

            def copy_xin(q, c):
                act.wait_ge(sem("A_projected"), 16 * q + CI + c + 1)
                if c == 0:
                    at_least(act, sem("A_halo_saved"), q + 1)
                act.activation(xin[:, c, :, HALO:], proj_ps[c % 4][:, :].rearrange("p (b t) -> p b t", b=NB),
                               ACT.Copy).then_inc(sem("A_proj_read"), 1)

            def silu_u(q, s, c):
                act.wait_ge(sem("A_convolved"), CI * q + c + 1)
                act.activation(ub[s][:, c], acc[c % 2], ACT.Silu).then_inc(sem("A_silu_done"), 1)

            def copy_xdbl(q):
                act.wait_ge(sem("A_xdbl_done"), q + 1)
                at_least(act, sem("A_xdbl_stored"), 32 * q)
                act.activation(xd, xd_ps[0:XD, :], ACT.Copy).then_inc(sem("A_xdbl_copied"), 1)

            def step_a(q, s, half, first, last):
                at_least(act, sem(f"A_z_stored{s}"), 32 * half)
                for i in range(4):
                    copy_z(q, s, i)
                if not first:
                    copy_xdbl(q - 1)
                for i in range(4, CI):
                    copy_z(q, s, i)
                at_least(act, sem(f"A_u_stored{s}"), 32 * half)
                for c in range(CI):
                    copy_xin(q, c)
                    if c >= 1:
                        silu_u(q, s, c - 1)
                    if c == 3 and not last:
                        square(q + 1, 1 - s)
                    if c == 6 and not last:
                        root(q + 1)
                silu_u(q, s, CI - 1)
                if not last:
                    affine(q + 1, 1 - s)

            square(0, 0)
            root(0)
            affine(0, 0)
            step_a(0, 0, 0, True, False)
            step_a(1, 1, 0, False, False)
            with act.Fori(1, STEPS // 2 - 1) as j:
                step_a(2 * j, 0, j, False, False)
                step_a(2 * j + 1, 1, j, False, False)
            step_a(STEPS - 2, 0, STEPS // 2 - 1, False, False)
            step_a(STEPS - 1, 1, STEPS // 2 - 1, False, True)
            copy_xdbl(STEPS - 1)
            barrier(act)

            act.wait_ge(sem("B_weights_loaded"), 112)
            nc.scalar.preload_act_table_set("natural_log_exp_and_others")
            act.activation(A_neg, A_neg, ACT.Exp).then_inc(sem("B_a_exp"), 1)
            act.wait_ge(sem("B_a_exp"), 1)
            act.activation(A_neg, A_neg, ACT.Copy, scale=-1.0).then_inc(sem("B_a_ready"), 1)
            act.wait_ge(sem("B_a_ready"), 1)
            act.wait_ge(sem("B_set_up"), 5 + len(LOG_SQUARES))

            def relu_v(q, b, i):
                g2 = 2 * (2 * q + b) + i
                act.wait_ge(sem("B_dt_multiplied"), g2 + 1)
                for a in range(2):
                    o = delta[b][:, i * HC + 2 * a:i * HC + 2 * a + 2, :].rearrange("p c t -> p (c t)")
                    act.activation(o, dt_ps[a][:, :], ACT.Relu).then_inc(sem("B_relu"), 1)

            def exp_v(q, b, i):
                g2 = 2 * (2 * q + b) + i
                at_least(act, sem("B_product_started"), g2)
                at_least(act, sem("B_squared"), len(LOG_SQUARES) * g2)
                for a in range(2):
                    ins = act.activation(sp_e[:, a * 512:(a + 1) * 512], dt_ps[a][:, :], ACT.Abs)
                ins.then_inc(sem("B_abs"), 1)
                act.wait_ge(sem("B_abs"), g2 + 1)
                act.activation(sp_e, sp_e, ACT.Exp, scale=-1.0).then_inc(sem("B_exp"), 1)

            def square(q, b, i, k):
                g2 = 2 * (2 * q + b) + i
                if k == 0:
                    act.wait_ge(sem("B_exp"), g2 + 1)
                at_least(act, sem("B_square_used"), len(LOG_SQUARES) * g2 + k)
                act.activation(sp_q, sp_e, ACT.Square, bias=log_a[:, k:k + 1]).then_inc(sem("B_squared"), 1)

            def keep_state(q, b, c, h):
                m = 2 * (NB * CI * q + CI * b + c) + h
                act.wait_ge(sem("B_scanned"), m + 1)
                act.activation(state[:, b, c, h * HN:(h + 1) * HN], seg(hb[(2 * c + h) % 4])[:, :, TC], ACT.Copy)\
                    .then_inc(sem("B_state_kept"), 1)

            def decays(q, b, c, h):
                m = 2 * (NB * CI * q + CI * b + c) + h
                if c in (0, HC) and h == 0:
                    act.wait_ge(sem("B_delta_made"), 2 * (2 * q + b) + 1 + c // HC)
                for n in range(HN):
                    act.activation(seg(dA[h])[:, n, 1:SEG], delta[b][:, c, :], ACT.Exp,
                                   scale=A_neg[:, c * NS + h * HN + n:c * NS + h * HN + n + 1])
                at_least(act, sem("B_summed"), m - 3)
                at_least(act, sem("B_state_kept"), m + 1 - 2 * NB * CI)
                act.activation(seg(hb[(2 * c + h) % 4])[:, :, 0], state[:, b, c, h * HN:(h + 1) * HN], ACT.Copy)\
                    .then_inc(sem("B_decays"), 1)

            def skip(q, b, c):
                n = NB * CI * q + CI * b + c
                act.wait_ge(sem("B_du"), n + 1)
                act.activation(u_t[c % RING], u_t[c % RING], ACT.Identity, scale=dsk[:, c:c + 1])\
                    .then_inc(sem("B_skip"), 1)

            def token_rstd(q, b):
                g = 2 * q + b
                act.wait_ge(sem("B_stats"), g + 1)
                act.activation(rs, mv.rearrange("p (a c) -> p a c", c=2)[:, :, 1], ACT.Ln).then_inc(sem("B_rs_log"), 1)
                act.wait_ge(sem("B_rs_log"), g + 1)
                act.activation(rs, rs, ACT.Exp, scale=-0.5).then_inc(sem("B_rs"), 1)

            def copy_tnT(q, b, a):
                act.wait_ge(sem("B_transposed"), TT * (2 * q + b) + a + 1)
                at_least(act, sem("B_logits_done"), TT * (2 * q + b) + a)
                act.activation(tnT, tr_ps[:, :], ACT.Copy).then_inc(sem("B_tnT"), 1)

            def before(q, b):
                return (q, 0) if b else (q - 1, 1)

            def after(q, b):
                return (q + 1, 0) if b else (q, 1)

            def group_b(q, b, first, last):
                for c in range(CI):
                    for h in range(2):
                        if c > 0:
                            keep_state(q, b, c - 1, h)
                        elif not first:
                            keep_state(*before(q, b), CI - 1, h)
                        decays(q, b, c, h)
                        if h == 0:
                            skip(q, b, c)
                        if not last:
                            if 2 * c + h in ACT_RELU:
                                relu_v(*after(q, b), ACT_RELU.index(2 * c + h))
                            if 2 * c + h in ACT_EXP:
                                exp_v(*after(q, b), ACT_EXP.index(2 * c + h))
                            if 2 * c + h in ACT_SQUARE:
                                square(*after(q, b), *divmod(ACT_SQUARE.index(2 * c + h), len(LOG_SQUARES)))
                    if not first:
                        if c == 3:
                            token_rstd(*before(q, b))
                        if c in (5, 6):
                            copy_tnT(*before(q, b), c - 5)

            for i in range(2):
                relu_v(0, 0, i)
                exp_v(0, 0, i)
                for k in range(len(LOG_SQUARES)):
                    square(0, 0, i, k)
            for b in range(NB):
                group_b(0, b, b == 0, False)
            with act.Fori(1, STEPS - 1) as q:
                for b in range(NB):
                    group_b(q, b, False, False)
            for b in range(NB):
                group_b(STEPS - 1, b, False, b == 1)
            for h in range(2):
                keep_state(STEPS - 1, 1, CI - 1, h)
            token_rstd(STEPS - 1, 1)
            for a in range(TT):
                copy_tnT(STEPS - 1, 1, a)
            barrier(act)

            act.wait_ge(sem("C_shifted"), 1)
            act.activation(prob, prob, ACT.Exp).then_inc(sem("C_exp"), 1)
            barrier(act)

            def gelu(j, r, k, h):
                t0, n = blocks[k]
                up = ((2 * j + r) * NBLK + k) * HM + h
                if k == 0 and h == 0:
                    act.wait_ge(sem(f"D_w1_loaded{r}"), 48 * (j + 1))
                act.wait_ge(sem("D_up_done"), up + 1)
                act.activation(hT[:, h, 0:n], up_ps[h % 3][:, 0:n], ACT.Gelu,
                               bias=b1_s[r][:, h:h + 1]).then_inc(sem("D_gelu"), 1)

            with act.Fori(0, NE // 2) as j:
                for r in range(2):
                    for k in range(NBLK):
                        for h in range(HM):
                            gelu(j, r, k, h)
            barrier(act)

        @block.tensor
        def _(pe):
            pe.wait_ge(s_const, 4)
            pe.wait_ge(sem("A_weights_loaded"), 96)

            def mean(q, s, half):
                pe.wait_ge(sem(f"A_x_loaded{s}"), 32 * (half + 1))
                at_least(pe, sem("A_centred"), q)
                for k in range(KD):
                    i = pe.matmul(mean_ps[:, :], mean_w, xn[s][:, k, :], start=(k == 0), stop=(k == KD - 1))
                i.then_inc(sem("A_mean_done"), 1)

            def var(q):
                pe.wait_ge(sem("A_squared"), q + 1)
                at_least(pe, sem("A_var_scaled"), q)
                for k in range(KD):
                    i = pe.matmul(var_ps[:, :], mean_w, sq[:, k, :], start=(k == 0), stop=(k == KD - 1))
                i.then_inc(sem("A_var_done"), 1)

            def project(q, s, i):
                at_least(pe, sem("A_proj_read"), 16 * q + i - 3)
                m = (CI + i) % (2 * CI)
                for k in range(KD):
                    ins = pe.matmul(proj_ps[i % 4][:, :], in_w[:, k, m * P:(m + 1) * P], xn[s][:, k, :],
                                    start=(k == 0), stop=(k == KD - 1))
                ins.then_inc(sem("A_projected"), 1)

            def xdbl(q, s):
                pe.wait_ge(sem("A_silu_done"), CI * (q + 1))
                at_least(pe, sem("A_xdbl_copied"), q)
                for c in range(CI):
                    i = pe.matmul(xd_ps[0:XD, :], xp_w[:, c, :], ub[s][:, c].rearrange("p b t -> p (b t)"),
                                  start=(c == 0), stop=(c == CI - 1))
                i.then_inc(sem("A_xdbl_done"), 1)

            def step_a(q, s, half, first, last):
                pe.wait_ge(sem("A_xn_ready"), q + 1)
                for i in range(16):
                    if i == 4 and not first:
                        xdbl(q - 1, 1 - s)
                    if i == 8 and not last:
                        mean(q + 1, 1 - s, half + s)
                    if i == 12 and not last:
                        var(q + 1)
                    project(q, s, i)

            mean(0, 0, 0)
            var(0)
            step_a(0, 0, 0, True, False)
            step_a(1, 1, 0, False, False)
            with pe.Fori(1, STEPS // 2 - 1) as j:
                step_a(2 * j, 0, j, False, False)
                step_a(2 * j + 1, 1, j, False, False)
            step_a(STEPS - 2, 0, STEPS // 2 - 1, False, False)
            step_a(STEPS - 1, 1, STEPS // 2 - 1, False, True)
            xdbl(STEPS - 1, 1)
            barrier(pe)

            pe.wait_ge(sem("B_weights_loaded"), 112)
            pe.wait_ge(sem("B_set_up"), 5 + len(LOG_SQUARES))

            def dt_product(q, b, i):
                g2 = 2 * (2 * q + b) + i
                if i == 0:
                    pe.wait_ge(sem(f"B_dt_loaded{b}"), 16 * (q + 1))
                at_least(pe, sem("B_abs"), g2)
                for a in range(HC):
                    c = i * HC + a
                    ins = pe.matmul(dt_ps[a // 2][:, (a % 2) * TC:(a % 2 + 1) * TC],
                                    dt_w[:, c * P:(c + 1) * P], dtT[b], start=True, stop=True)
                ins.then_inc(sem("B_dt_multiplied"), 1)

            def sums(q, b, c):
                n = NB * CI * q + CI * b + c
                at_least(pe, sem("B_gated"), n - 1)
                o = sum_ps[c % 2][:, 0:TC]
                pe.wait_ge(sem("B_skip"), n + 1)
                pe.matmul(o, ident, u_t[c % RING], start=True, stop=False)
                for h in range(2):
                    pe.wait_ge(sem("B_c_multiplied"), 2 * n + h + 1)
                    for k in range(HN):
                        ins = pe.matmul(o, ident, seg(hb[(2 * c + h) % 4])[:, k, 1:SEG],
                                        start=False, stop=(h == 1 and k == HN - 1))
                    ins.then_inc(sem("B_summed"), 1)

            def out_product(q, b, c):
                n = NB * CI * q + CI * b + c
                if c == 0:
                    at_least(pe, sem("B_residual_added"), TT * (2 * q + b))
                pe.wait_ge(sem("B_gated"), n + 1)
                for a in range(TT):
                    ins = pe.matmul(out_ps[a][:, :], yg[c % 2][:, a * P:(a + 1) * P], out_w[:, c, :],
                                    start=(c == 0), stop=(c == CI - 1))
                ins.then_inc(sem("B_out_done"), 1)

            def transpose_tn(q, b, a):
                t = TT * (2 * q + b) + a
                pe.wait_ge(sem("B_normed"), t + 1)
                at_least(pe, sem("B_tnT"), t)
                for k in range(KD):
                    ins = pe.transpose(tr_ps[:, k * P:(k + 1) * P], tn[:, a, k * P:(k + 1) * P], ident)
                ins.then_inc(sem("B_transposed"), 1)

            def logit(q, b, a):
                t = TT * (2 * q + b) + a
                pe.wait_ge(sem("B_tnT"), t + 1)
                at_least(pe, sem("B_logits_kept"), t)
                for k in range(KD):
                    ins = pe.matmul(lg_ps[:, 0:NE], tnT[:, k * P:(k + 1) * P], gate_w[:, k, :],
                                    start=(k == 0), stop=(k == KD - 1))
                ins.then_inc(sem("B_logits_done"), 1)

            def before(q, b):
                return (q, 0) if b else (q - 1, 1)

            def after(q, b):
                return (q + 1, 0) if b else (q, 1)

            def group_b(q, b, first, last):
                for c in range(CI):
                    if c in PE_DT and not last:
                        dt_product(*after(q, b), PE_DT.index(c))
                    sums(q, b, c)
                    if c > 0:
                        out_product(q, b, c - 1)
                    elif not first:
                        out_product(*before(q, b), CI - 1)
                    if not first:
                        if c in (4, 5):
                            logit(*before(q, b), c - 4)
                        if c in (3, 4):
                            transpose_tn(*before(q, b), c - 3)

            for i in range(2):
                dt_product(0, 0, i)
            for b in range(NB):
                group_b(0, b, b == 0, False)
            with pe.Fori(1, STEPS - 1) as q:
                for b in range(NB):
                    group_b(q, b, False, False)
            for b in range(NB):
                group_b(STEPS - 1, b, False, b == 1)
            out_product(STEPS - 1, 1, CI - 1)
            for a in range(TT):
                transpose_tn(STEPS - 1, 1, a)
                logit(STEPS - 1, 1, a)
            barrier(pe)

            with pe.Fori(0, 30) as i:
                pe.wait_ge(sem("C_counted"), i + 1)
                pe.matmul(bank[0][:, 0:NE], ones, cnt, start=True, stop=True).then_inc(sem("C_total"), 1)
            pe.wait_ge(sem("C_masks"), 1)
            flat2 = "p e j -> p (e j)"
            pe.matmul(bank[1][:, 0:NE * NT], below, gtm.rearrange(flat2), start=True, stop=True)
            pe.matmul(bank[2][:, 0:NE * NT], ones, gtm.rearrange(flat2), start=True, stop=True)
            pe.matmul(bank[3][:, 0:NE * NT], below, eqm.rearrange(flat2), start=True, stop=True)
            pe.matmul(bank[4][:, 0:NE * NT], ones, eqm.rearrange(flat2), start=True, stop=True)\
                .then_inc(sem("C_prefixes"), 1)
            pe.wait_ge(sem("C_zeros"), 1)
            pe.matmul(table_ps, zeros[:, 0:P], zeros[:, 0:2 * ROWS], start=True, stop=False)
            with pe.Fori(0, NT // 2) as j:
                for r in range(2):
                    for k in range(TOPK):
                        pe.wait_ge(sem("C_hot"), TOPK * (2 * j + r) + k + 1)
                        pe.matmul(table_ps, lo_hot[2 * r + k], hi_hot[2 * r + k], start=False, stop=False)\
                            .then_inc(sem("C_hot_used"), 1)
            pe.matmul(table_ps, zeros[:, 0:P], zeros[:, 0:2 * ROWS], start=False, stop=True).then_inc(sem("C_table"), 1)
            barrier(pe)


            def transposes(j, w, k):
                for i, (t0, n) in enumerate(tiles_of[k]):
                    o = w * ND + first_of[k] + i
                    pe.wait_ge(sem(f"D_gathered{o % XG}"), 16 * (j * (2 * ND // XG) + o // XG + 1))
                    at_least(pe, sem("D_xt_copied"), j * 2 * ND + o - 1)
                    for kk in range(KD):
                        ins = pe.transpose(xt_ps[o % 2][:, kk * P:kk * P + n], xg[o % XG][0:n, kk * P:(kk + 1) * P],
                                           ident[0:n, 0:n])
                    ins.then_inc(sem(f"D_transposed{o % XG}"), 1)

            def up(j, w, k):
                t0, n = blocks[k]
                e = 2 * j + w
                if k == 0:
                    pe.wait_ge(sem(f"D_w1_loaded{w}"), 48 * (j + 1))
                pe.wait_ge(sem("D_xt_copied"), ND * e + first_of[k] + len(tiles_of[k]))
                for h in range(HM):
                    at_least(pe, sem("D_gelu"), (e * NBLK + k) * HM + h - 2)
                    for kk in range(KD):
                        ins = pe.matmul(up_ps[h % 3][:, 0:n], w1_s[w][:, kk, h * P:(h + 1) * P],
                                        xgT[(w * NBLK + k) % 2][:, kk, 0:n], start=(kk == 0), stop=(kk == KD - 1))
                    ins.then_inc(sem("D_up_done"), 1)

            def down(j, w, k):
                e = 2 * j + w
                if k == 0:
                    pe.wait_ge(sem("D_w2_loaded"), 16 * (e + 1))
                pe.wait_ge(sem("D_gelu"), (e * NBLK + k + 1) * HM)
                for i, (t0, n) in enumerate(tiles_of[k]):
                    o = first_of[k] + i
                    at_least(pe, sem("D_biased"), ND * e + o - 1)
                    c0 = t0 - blocks[k][0]
                    for h in range(HM):
                        ins = pe.matmul(dn_ps[o % 2][0:n, :], hT[:, h, c0:c0 + n], w2_s[:, h, :],
                                        start=(h == 0), stop=(h == HM - 1))
                    ins.then_inc(sem("D_down_done"), 1)

            def round_d(j, last):
                for w in range(2):
                    for k in range(NBLK):
                        up(j, w, k)
                        if k + 1 < NBLK:
                            transposes(j, w, k + 1)
                        elif w == 0:
                            transposes(j, 1, 0)
                        elif not last:
                            transposes(j + 1, 0, 0)
                        down(j, w, k)

            transposes(0, 0, 0)
            round_d(0, False)
            with pe.Fori(1, NE // 2 - 1) as j:
                round_d(j, False)
            round_d(NE // 2 - 1, True)
            barrier(pe)

        @block.vector
        def _(dve):
            dve.wait_ge(sem("A_weights_loaded"), 96)
            dve.memset(xin[:, :, :, 0:HALO], 0.0).then_inc(sem("A_halo_saved"), 1)

            def over_k(t):
                return t.rearrange("p (o t) -> p o t", o=1).broadcast_to([P, KD, W2T])

            def centre(q, s):
                dve.wait_ge(sem("A_mean_done"), q + 1)
                dve.tensor_tensor(xn[s], xn[s], over_k(mean_ps[:, :]), ALU.subtract).then_inc(sem("A_centred"), 1)

            def scale_var(q):
                dve.wait_ge(sem("A_var_done"), q + 1)
                dve.tensor_scalar(rstd, var_ps[:, :], 1.0 + EPS_MAMBA, EPS_CHANNEL * EPS_MAMBA, ALU.mult, ALU.add)\
                    .then_inc(sem("A_var_scaled"), 1)

            def scale(q, s):
                dve.wait_ge(sem("A_rooted"), q + 1)
                dve.reciprocal(rstd, rstd).then_inc(sem("A_inverted"), 1)
                dve.wait_ge(sem("A_inverted"), q + 1)
                dve.tensor_tensor(xn[s], xn[s], over_k(rstd), ALU.mult).then_inc(sem("A_scaled"), 1)

            def convolve(q, c):
                dve.wait_ge(sem("A_proj_read"), 16 * q + CI + c + 1)
                at_least(dve, sem("A_silu_done"), CI * q + c - 1)
                o = acc[c % 2]
                taps = NTAP - 1
                dve.tensor_scalar(o, xin[:, c, :, 0:TC], cw[:, c * NTAP:c * NTAP + 1], cb[:, c:c + 1], ALU.mult, ALU.add)\
                    .then_inc(sem("A_tap"), 1)
                for k in range(1, NTAP):
                    dve.wait_ge(sem("A_tap"), taps * (CI * q + c) + k)
                    i = dve.scalar_tensor_tensor(out=o, in0=xin[:, c, :, k:k + TC],
                                                 scalar=cw[:, c * NTAP + k:c * NTAP + k + 1], in1=o,
                                                 op0=ALU.mult, op1=ALU.add)
                    i.then_inc(sem("A_tap" if k < taps else "A_convolved"), 1)

            def save_halo(q):
                dve.wait_ge(sem("A_convolved"), CI * (q + 1))
                dve.tensor_copy(xin[:, :, :, 0:HALO], xin[:, :, :, TC:TC + HALO]).then_inc(sem("A_halo_saved"), 1)

            def step_a(q, s, last):
                if not last:
                    centre(q + 1, 1 - s)
                for c in range(CI):
                    convolve(q, c)
                    if c == 4 and not last:
                        scale_var(q + 1)
                    if c == 6 and not last:
                        scale(q + 1, 1 - s)
                save_halo(q)

            centre(0, 0)
            scale_var(0)
            scale(0, 0)
            step_a(0, 0, False)
            step_a(1, 1, False)
            with dve.Fori(1, STEPS // 2 - 1) as j:
                step_a(2 * j, 0, False)
                step_a(2 * j + 1, 1, False)
            step_a(STEPS - 2, 0, False)
            step_a(STEPS - 1, 1, True)
            barrier(dve)

            for t in dtT:
                dve.memset(t[R:R + 1, :], 1.0).then_inc(sem("B_set_up"), 1)
            dve.memset(state, 0.0).then_inc(sem("B_set_up"), 1)
            for k, (a, _) in enumerate(LOG_SQUARES):
                dve.memset(log_a[:, k:k + 1], a).then_inc(sem("B_set_up"), 1)
            for t in dA:
                dve.memset(seg(t)[:, :, 0], 0.0).then_inc(sem("B_set_up"), 1)
            dve.wait_ge(sem("B_weights_loaded"), 112)
            dve.wait_ge(sem("B_set_up"), 5 + len(LOG_SQUARES))

            def log_step(q, b, i, k):
                g2 = 2 * (2 * q + b) + i
                if k == 0:
                    dve.wait_ge(sem("B_exp"), g2 + 1)
                    at_least(dve, sem("B_delta_made"), g2)
                    dve.scalar_tensor_tensor(out=sp_l, in0=sp_e, scalar=LOG_ROOT, in1=sp_e,
                                             op0=ALU.subtract, op1=ALU.mult).then_inc(sem("B_product_started"), 1)
                elif k < LOG_STEPS - 1:
                    if k == 1:
                        dve.wait_ge(sem("B_product_started"), g2 + 1)
                    else:
                        dve.wait_ge(sem("B_square_used"), len(LOG_SQUARES) * g2 + k - 1)
                    dve.wait_ge(sem("B_squared"), len(LOG_SQUARES) * g2 + k)
                    dve.scalar_tensor_tensor(out=sp_l, in0=sp_q, scalar=LOG_SQUARES[k - 1][1], in1=sp_l,
                                             op0=ALU.add, op1=ALU.mult).then_inc(sem("B_square_used"), 1)
                else:
                    dve.wait_ge(sem("B_square_used"), len(LOG_SQUARES) * (g2 + 1))
                    dve.wait_ge(sem("B_relu"), 2 * (g2 + 1))
                    o = delta[b][:, i * HC:(i + 1) * HC, :].rearrange("p c t -> p (c t)")
                    dve.scalar_tensor_tensor(out=o, in0=sp_l, scalar=LOG_LEAD, in1=o, op0=ALU.mult, op1=ALU.add)\
                        .then_inc(sem("B_delta_made"), 1)

            def input_u(q, b, c):
                n = NB * CI * q + CI * b + c
                r = c % RING
                if c in (0, HC):
                    dve.wait_ge(sem("B_delta_made"), 2 * (2 * q + b) + 1 + c // HC)
                dve.wait_ge(sem(f"B_uz_loaded{r}"), 32 * (q * (NB * CI // RING) + (CI * b + c) // RING + 1))
                at_least(dve, sem("B_pool_started"), n - 1)
                dve.tensor_tensor(du[c % 2], delta[b][:, c, :], u_t[r], ALU.mult).then_inc(sem("B_du"), 1)

            def scan(q, b, c, h):
                n = NB * CI * q + CI * b + c
                m = 2 * n + h
                own = HN - h * NPOOL
                hs = hb[(2 * c + h) % 4]
                if c == 0 and h == 0:
                    dve.wait_ge(sem(f"B_bc_loaded{b}"), 32 * (q + 1))
                at_least(dve, sem("B_summed"), m - 3)
                if h == 0:
                    dve.wait_ge(sem("B_du"), n + 1)
                dve.tensor_tensor(seg(hs)[:, 0:own, 1:SEG],
                                  du[c % 2].rearrange("p (o t) -> p o t", o=1).broadcast_to([P, own, TC]),
                                  Brep[b][:, h * HN:h * HN + own, :], ALU.mult).then_inc(sem("B_started"), 1)
                dve.wait_ge(sem("B_started"), m + 1)
                if h == 1:
                    dve.wait_ge(sem("B_pool_started"), n + 1)
                dve.wait_ge(sem("B_decays"), m + 1)
                dve.tensor_tensor_scan(hs, dA[h], hs, 0.0, ALU.mult, ALU.add).then_inc(sem("B_scanned"), 1)

            def gate(q, b, c):
                n = NB * CI * q + CI * b + c
                r = c % RING
                dve.wait_ge(sem("B_summed"), 2 * (n + 1))
                at_least(dve, sem("B_out_done"), n - 1)
                dve.tensor_tensor(yg[c % 2], sum_ps[c % 2][:, 0:TC], z_t[r], ALU.mult).then_inc(sem("B_gated"), 1)

            def residual(q, b):
                g = 2 * q + b
                dve.wait_ge(sem("B_out_done"), CI * (g + 1))
                dve.wait_ge(sem("B_xt_loaded"), 16 * (g + 1))
                at_least(dve, sem("B_tokens_stored"), 32 * g)
                for a in range(TT):
                    dve.tensor_tensor(x1[:, a, :], out_ps[a][:, :], x1[:, a, :], ALU.add)\
                        .then_inc(sem("B_residual_added"), 1)
                for a in range(TT):
                    dve.wait_ge(sem("B_residual_added"), TT * g + a + 1)
                    dve.bn_stats(bst[:, 6 * a:6 * a + 6], x1[:, a, :]).then_inc(sem("B_bn"), 1)
                for a in range(TT):
                    alone(dve)
                    dve.wait_ge(sem("B_bn"), TT * g + a + 1)
                    dve.bn_aggr(mv[:, 2 * a:2 * a + 2], bst[:, 6 * a:6 * a + 6]).then_inc(sem("B_aggr"), 1)
                dve.wait_ge(sem("B_aggr"), TT * (g + 1))
                v = mv.rearrange("p (a c) -> p a c", c=2)[:, :, 1]
                dve.tensor_scalar(v, v, EPS_TOKEN, None, ALU.add).then_inc(sem("B_stats"), 1)

            def normalise(q, b):
                g = 2 * q + b
                dve.wait_ge(sem("B_rs"), g + 1)
                v = mv.rearrange("p (a c) -> p a c", c=2)[:, :, 1]
                dve.tensor_tensor(newt, rs, rs, ALU.mult).then_inc(sem("B_newton"), 1)
                dve.wait_ge(sem("B_newton"), 4 * g + 1)
                dve.tensor_tensor(newt, newt, v, ALU.mult).then_inc(sem("B_newton"), 1)
                dve.wait_ge(sem("B_newton"), 4 * g + 2)
                dve.tensor_scalar(newt, newt, -0.5, 1.5, ALU.mult, ALU.add).then_inc(sem("B_newton"), 1)
                dve.wait_ge(sem("B_newton"), 4 * g + 3)
                dve.tensor_tensor(rs, rs, newt, ALU.mult).then_inc(sem("B_newton"), 1)
                dve.wait_ge(sem("B_newton"), 4 * g + 4)
                for a in range(TT):
                    dve.tensor_scalar(tn[:, a, :], x1[:, a, :], mv[:, 2 * a:2 * a + 1], rs[:, a:a + 1],
                                      ALU.subtract, ALU.mult).then_inc(sem("B_normed"), 1)

            def keep_logits(q, b, a):
                t = TT * (2 * q + b) + a
                dve.wait_ge(sem("B_logits_done"), t + 1)
                j0 = (q * TT + (b * (L // P) + a)) * NE
                dve.tensor_tensor(logits[:, bass.ds(j0, NE)], lg_ps[:, 0:NE], gate_bb, ALU.add)\
                    .then_inc(sem("B_logits_kept"), 1)

            def before(q, b):
                return (q, 0) if b else (q - 1, 1)

            def after(q, b):
                return (q + 1, 0) if b else (q, 1)

            def group_b(q, b, first, last):
                for c in range(CI):
                    for h in range(2):
                        scan(q, b, c, h)
                        if h == 0:
                            if c < CI - 1:
                                input_u(q, b, c + 1)
                            elif not last:
                                input_u(*after(q, b), 0)
                            if c >= 2:
                                gate(q, b, c - 2)
                            elif not first:
                                gate(*before(q, b), CI - 2 + c)
                        if not last:
                            for k, at in enumerate(DVE_LOG):
                                if at == 2 * c + h:
                                    log_step(*after(q, b), *divmod(k, LOG_STEPS))
                    if not first:
                        if c == 2:
                            residual(*before(q, b))
                        if c == 3:
                            normalise(*before(q, b))
                        if c in (6, 7):
                            keep_logits(*before(q, b), c - 6)

            for i in range(2):
                for k in range(LOG_STEPS):
                    log_step(0, 0, i, k)
            input_u(0, 0, 0)
            for b in range(NB):
                group_b(0, b, b == 0, False)
            with dve.Fori(1, STEPS - 1) as q:
                for b in range(NB):
                    group_b(q, b, False, False)
            for b in range(NB):
                group_b(STEPS - 1, b, False, b == 1)
            for c in (CI - 2, CI - 1):
                gate(STEPS - 1, 1, c)
            residual(STEPS - 1, 1)
            normalise(STEPS - 1, 1)
            for a in range(TT):
                keep_logits(STEPS - 1, 1, a)
            barrier(dve)

            s_chain = sem("C_chain")
            chain = [0]

            def link(ins):
                chain[0] += 1
                ins.then_inc(s_chain, 1)
                dve.wait_ge(s_chain, chain[0])

            def by_tile(t):
                return t.rearrange("p e j -> p j e")

            def over_e(t):
                return t.rearrange("p (o j) -> p o j", o=1).broadcast_to([P, NE, NT])

            def over_j(t):
                return t.rearrange("p (e o) -> p e o", o=1).broadcast_to([P, NE, NT])

            lg = logits.rearrange("p (j e) -> p j e", e=NE)
            link(dve.tensor_reduce(tmax, lg, AX_X, ALU.max))
            dve.tensor_tensor(prob, lg.rearrange("p j e -> p e j"), over_e(tmax), ALU.subtract)\
                .then_inc(sem("C_shifted"), 1)
            dve.wait_ge(sem("C_exp"), 1)
            link(dve.tensor_reduce(tsum, by_tile(prob), AX_X, ALU.add))
            link(dve.reciprocal(tsum, tsum))
            link(dve.tensor_tensor(prob, prob, over_e(tsum), ALU.mult))
            dve.wait_ge(sem("C_tables"), 2 * NE + 3)
            for s in range(1, NE):
                link(dve.tensor_tensor(tmp[:, 0:NE - s], prob[:, 0:NE - s], prob[:, s:NE], ALU.is_ge))
                link(dve.tensor_tensor(rank[:, s:NE], rank[:, s:NE], tmp[:, 0:NE - s], ALU.add))
                link(dve.tensor_tensor(rank[:, 0:NE - s], rank[:, 0:NE - s], tmp[:, 0:NE - s], ALU.subtract))
            link(dve.tensor_scalar(hit, rank, float(TOPK), None, ALU.is_lt))
            link(dve.tensor_tensor(wm, prob, hit, ALU.mult))
            link(dve.scalar_tensor_tensor(out=wm, in0=hit, scalar=1.0, in1=wm, op0=ALU.subtract, op1=ALU.add))
            link(dve.memset(thr, 0))
            link(dve.memset(bit, 1 << 29))
            with dve.Fori(0, 30) as i:
                dve.tensor_tensor(cand, thr, bit, ALU.bitwise_or).then_inc(sem("C_cand"), 1)
                dve.wait_ge(sem("C_cand"), i + 1)
                dve.tensor_tensor(hit, wm, over_j(cand.bitcast(F32)), ALU.is_ge).then_inc(sem("C_hit"), 1)
                dve.wait_ge(sem("C_hit"), i + 1)
                dve.tensor_reduce(cnt, hit, AX_X, ALU.add).then_inc(sem("C_counted"), 1)
                dve.wait_ge(sem("C_total"), i + 1)
                dve.tensor_scalar(cond, bank[0][:, 0:NE], float(CAP), None, ALU.is_ge).then_inc(sem("C_cond"), 1)
                dve.wait_ge(sem("C_cond"), i + 1)
                dve.tensor_tensor(cond, cond, bit, ALU.mult).then_inc(sem("C_gain"), 1)
                dve.wait_ge(sem("C_gain"), i + 1)
                dve.tensor_tensor(thr, thr, cond, ALU.bitwise_or).then_inc(sem("C_thr"), 1)
                dve.wait_ge(sem("C_thr"), i + 1)
                dve.tensor_scalar(bit, bit, 1, None, ALU.logical_shift_right).then_inc(sem("C_bit_done"), 1)
                dve.wait_ge(sem("C_bit_done"), i + 1)
            link(dve.tensor_tensor(gtm, wm, over_j(thr.bitcast(F32)), ALU.is_gt))
            dve.tensor_tensor(eqm, wm, over_j(thr.bitcast(F32)), ALU.is_equal).then_inc(sem("C_masks"), 1)
            dve.wait_ge(sem("C_prefixes"), 1)
            flat2 = "p e j -> p (e j)"

            def ps(i):
                return bank[i][:, 0:NE * NT]

            for pos, inside, total in ((posg, 1, 2), (posq, 3, 4)):
                link(dve.tensor_tensor_scan(pos.rearrange(flat2), seg0.rearrange(flat2), ps(total), 0.0,
                                            ALU.mult, ALU.add))
                if pos is posg:
                    link(dve.tensor_scalar(need, posg[:, :, NT - 1], -1.0, float(CAP), ALU.mult, ALU.add))
                link(dve.tensor_tensor(pos.rearrange(flat2), pos.rearrange(flat2), ps(total), ALU.subtract))
                link(dve.tensor_tensor(pos.rearrange(flat2), pos.rearrange(flat2), ps(inside), ALU.add))
            link(dve.tensor_tensor(tmp, posq, over_j(need), ALU.is_lt))
            link(dve.tensor_tensor(tmp, tmp, eqm, ALU.mult))
            link(dve.tensor_tensor(keep, gtm, tmp, ALU.add))
            link(dve.tensor_tensor(posq, posq, over_j(need), ALU.min))
            link(dve.tensor_tensor(posg, posg, posq, ALU.add))
            link(dve.tensor_tensor(posg, posg, over_j(base), ALU.add))
            link(dve.tensor_copy(count, count_i))
            link(dve.tensor_copy(cols_v[:, :, 0], token_i))
            for k in range(TOPK):
                link(dve.scalar_tensor_tensor(out=hit, in0=rank, scalar=float(k), in1=keep,
                                              op0=ALU.is_equal, op1=ALU.mult))
                link(dve.tensor_tensor(tmp, hit, prob, ALU.mult))
                link(dve.tensor_reduce(cols_v[:, :, 5 + k], by_tile(tmp), AX_X, ALU.add))
                link(dve.tensor_tensor(tmp, hit, posg, ALU.mult))
                link(dve.tensor_reduce(pick, by_tile(tmp), AX_X, ALU.add))
                link(dve.tensor_reduce(miss, by_tile(hit), AX_X, ALU.add))
                none = float(2 * ROWS * P)
                link(dve.tensor_scalar(miss, miss, -none, none, ALU.mult, ALU.add))
                link(dve.tensor_tensor(miss, miss, pick, ALU.add))
                link(dve.tensor_copy(word[:, 0:NT], miss))
                log2p = P.bit_length() - 1
                link(dve.tensor_scalar(word[:, NT:2 * NT], word[:, 0:NT], P - 1, None, ALU.bitwise_and))
                link(dve.tensor_scalar(word[:, 0:NT], word[:, 0:NT], log2p, None, ALU.logical_shift_right))
                link(dve.tensor_copy(cols_v[:, :, 1 + k], word[:, NT:2 * NT]))
                link(dve.tensor_copy(cols_v[:, :, 3 + k], word[:, 0:NT]))

            def one_hots(j, r, first):
                t = 2 * j + r
                if not first:
                    dve.wait_ge(sem("C_hot_used"), TOPK * (t - 1))
                    dve.wait_ge(sem("C_hot"), TOPK * (t - 1))
                dve.tensor_copy(tile_cols[r], cols[:, bass.ds(t * NCOL, NCOL)]).then_inc(sem("C_cols"), 1)
                dve.wait_ge(sem("C_cols"), t + 1)
                c = tile_cols[r]
                for k in range(TOPK):
                    o = 2 * r + k
                    hi = c[:, 3 + k:4 + k]
                    dve.tensor_scalar(lo_hot[o], count, c[:, 1 + k:2 + k], None, ALU.is_equal)
                    dve.tensor_scalar(hi_hot[o][:, 0:ROWS], count[:, 0:ROWS], hi, c[:, 0:1],
                                      ALU.is_equal, ALU.mult)
                    dve.tensor_scalar(hi_hot[o][:, ROWS:], count[:, 0:ROWS], hi, c[:, 5 + k:6 + k],
                                      ALU.is_equal, ALU.mult).then_inc(sem("C_hot"), 1)

            for r in range(2):
                one_hots(0, r, True)
            with dve.Fori(1, NT // 2) as j:
                for r in range(2):
                    one_hots(j, r, False)
            dve.wait_ge(sem("C_table"), 1)
            link(dve.tensor_copy(slot_w, table_ps[:, ROWS:]))
            link(dve.tensor_scalar(found, table_ps[:, 0:ROWS], -1.0, 0.0, ALU.add, ALU.max))
            link(dve.tensor_copy(slot_get, found))
            link(dve.tensor_scalar(found, table_ps[:, 0:ROWS], 0.0, float(2 * T), ALU.is_equal, ALU.mult))
            link(dve.scalar_tensor_tensor(out=found, in0=table_ps[:, 0:ROWS], scalar=-1.0, in1=found,
                                          op0=ALU.add, op1=ALU.add))
            link(dve.tensor_copy(slot_put, found))
            barrier(dve)

            def ready_get(j, w, k):
                for i in range(first_of[k], first_of[k] + len(tiles_of[k])):
                    o = w * ND + i
                    at_least(dve, sem(f"D_gathered{o % XG}"), 16 * (j * (2 * ND // XG) + o // XG))
                    dve.tensor_copy(get[o % XG], slot_get[:, bass.ds(2 * ND * j + o, 1)])\
                        .then_inc(sem("D_get_ready"), 1)

            def copy_xt(j, w, k):
                for i, (t0, n) in enumerate(tiles_of[k]):
                    o = w * ND + first_of[k] + i
                    if i == 0:
                        at_least(dve, sem("D_up_done"), HM * (2 * NBLK * j + w * NBLK + k - 1))
                    dve.wait_ge(sem(f"D_transposed{o % XG}"), j * (2 * ND // XG) + o // XG + 1)
                    c0 = t0 - blocks[k][0]
                    dve.tensor_copy(xgT[(w * NBLK + k) % 2][:, :, c0:c0 + n],
                                    xt_ps[o % 2][:, :].rearrange("p (k t) -> p k t", k=KD)[:, :, 0:n])\
                        .then_inc(sem("D_xt_copied"), 1)

            def weigh(j, w, k):
                e = 2 * j + w
                if k == 0:
                    dve.wait_ge(sem(f"D_w1_loaded{w}"), 48 * (j + 1))
                for i, (t0, n) in enumerate(tiles_of[k]):
                    o = first_of[k] + i
                    g = ND * e + o
                    at_least(dve, sem(f"D_added{o % 2}"), 16 * ((ND // 2) * e + o // 2))
                    dve.tensor_copy(put[o % 2], slot_put[:, bass.ds(2 * ND * j + w * ND + o, 1)])\
                        .then_inc(sem("D_put_ready"), 1)
                    dve.tensor_copy(put_w[o % 2], slot_w[:, bass.ds(2 * ND * j + w * ND + o, 1)])\
                        .then_inc(sem("D_put_ready"), 1)
                    dve.wait_ge(sem("D_down_done"), g + 1)
                    dve.tensor_tensor(ye[o % 2][0:n, :], dn_ps[o % 2][0:n, :], b2_s[w][0:n, :], ALU.add)\
                        .then_inc(sem("D_biased"), 1)
                    dve.wait_ge(sem("D_biased"), g + 1)
                    dve.wait_ge(sem("D_put_ready"), 2 * (g + 1))
                    dve.tensor_scalar(ye[o % 2][0:n, :], ye[o % 2][0:n, :], put_w[o % 2][0:n, :], None,
                                      ALU.mult).then_inc(sem("D_weighted"), 1)

            def round_d(j, last):
                for w in range(2):
                    for k in range(NBLK):
                        nxt = (j, w, k + 1) if k + 1 < NBLK else (j, 1, 0) if w == 0 else (j + 1, 0, 0)
                        if not (last and w == 1 and k == NBLK - 1):
                            ready_get(*nxt)
                            copy_xt(*nxt)
                        weigh(j, w, k)

            ready_get(0, 0, 0)
            copy_xt(0, 0, 0)
            round_d(0, False)
            with dve.Fori(1, NE // 2 - 1) as j:
                round_d(j, False)
            round_d(NE // 2 - 1, True)
            barrier(dve)


def kernel(x, L0_conv_ln_w, L0_conv_ln_b, L0_conv_in_proj_w, L0_conv_conv_w, L0_conv_conv_b, L0_conv_x_proj_w,
           L0_conv_dt_proj_w, L0_conv_dt_proj_b, L0_conv_A_log, L0_conv_D_skip, L0_conv_out_proj_w,
           L0_ffn_gate_w, L0_ffn_gate_b, L0_ffn_w1, L0_ffn_b1, L0_ffn_w2, L0_ffn_b2):
    import numpy as np
    import concourse.bacc as bacc
    from concourse.bass_utils import run_bass_kernel_spmd as run

    x = np.asarray(x)
    NB, DIM, H, W = x.shape

    def tiles(a):
        a = np.asarray(a)
        a = a.reshape(a.shape[0] // 128, 128, -1)
        return a.transpose(1, 0, 2).reshape(128, -1)

    b1 = np.asarray(L0_ffn_b1)
    arrays = {
        "x": x.reshape(NB, DIM, H * W),
        "x_tok": x.reshape(NB, DIM, H * W).transpose(0, 2, 1).reshape(NB * H * W, DIM),
        "ln_w": tiles(L0_conv_ln_w),
        "ln_b": tiles(L0_conv_ln_b),
        "in_wT": np.asarray(L0_conv_in_proj_w).T,
        "conv_w": tiles(L0_conv_conv_w),
        "conv_b": tiles(L0_conv_conv_b),
        "xp_wT": np.asarray(L0_conv_x_proj_w).T,
        "dt_wT": np.asarray(L0_conv_dt_proj_w).T,
        "dt_b": np.asarray(L0_conv_dt_proj_b).reshape(1, -1),
        "A_log": tiles(L0_conv_A_log),
        "D_skip": tiles(L0_conv_D_skip),
        "out_wT": np.asarray(L0_conv_out_proj_w).T,
        "gate_wT": np.asarray(L0_ffn_gate_w).T,
        "gate_b": np.asarray(L0_ffn_gate_b).reshape(1, -1),
        "w1": np.asarray(L0_ffn_w1),
        "b1": b1.reshape(b1.shape[0], -1, 128).transpose(0, 2, 1),
        "w2": np.asarray(L0_ffn_w2),
        "b2": np.asarray(L0_ffn_b2),
    }
    arrays = {f"in_{k}": np.ascontiguousarray(a) for k, a in arrays.items()}
    nc = bacc.Bacc("TRN2", target_bir_lowering=False, num_devices=1)
    args = [nc.dram_tensor(k, a.shape, mybir.dt.from_np(a.dtype), kind="ExternalInput").ap()
            for k, a in arrays.items()]
    out = nc.dram_tensor("out_dram", (NB * H * W, DIM), F32, kind="ExternalOutput").ap()
    metaformer_layer(nc, *args, out)
    r = run(nc, [arrays], core_ids=[0])
    y = r.results[0]["out_dram"]
    return np.ascontiguousarray(y.reshape(NB, H * W, DIM).transpose(0, 2, 1)).reshape(NB, DIM, H, W)
```

```python
from contextlib import ExitStack

import concourse.bass as bass
from concourse import mybir

F32 = mybir.dt.float32
F32R = mybir.dt.float32r
I32 = mybir.dt.int32
ALU = mybir.AluOpType
ACT = mybir.ActivationFunctionType
AX_X = mybir.AxisListType.X

P = 128
EPS_CHANNEL = 1e-6
EPS_MAMBA = 1e-5
EPS_TOKEN = 1e-5
TC = 256
TOPK = 2
CAPACITY_FACTOR = 1.2
NPOOL = 3


LOG_LEAD = -0.0085392045
LOG_ROOT = 2.4858158
LOG_SQUARES = ((-1.8699235, 1.9141982), (-0.41215122, 3.5825396), (0.94338274, 1.4303126))


class Arena:

    def __init__(self, nc):
        self.nc, self.open, self.count = nc, [], 0

    def tensor(self, cols, dtype):
        self.count += 1
        t = self.nc.sbuf_tensor(f"buffer{self.count}", [P, cols], dtype)
        self.open.append(t)
        return t.__enter__()

    def take(self, cols, partitions=P):
        return self.tensor(cols, F32)[0:partitions, :]

    def take_both(self, cols, pattern, **sizes):
        plain = self.tensor(cols, F32)
        self.back_to(len(self.open) - 1)
        rounded = self.tensor(cols, F32R)
        return plain[0:P, :].rearrange(pattern, **sizes), rounded[0:P, :].rearrange(pattern, **sizes)

    def mark(self):
        return len(self.open)

    def back_to(self, mark):
        while len(self.open) > mark:
            self.open.pop().__exit__(None, None, None)


def at_least(eng, sem, value):
    if isinstance(value, int) and value <= 0:
        return
    eng.wait_ge(sem, value)


def metaformer_layer(nc, x, x_tok, ln_w, ln_b, in_wT, conv_w, conv_b, xp_wT, dt_wT, dt_b, A_log, D_skip,
                     out_wT, gate_wT, gate_b, w1, b1, w2, b2, out):
    NB, DIM, L = x.shape
    T = NB * L
    KD = DIM // P
    DI = in_wT.shape[1] // 2
    CI = DI // P
    NTAP = conv_w.shape[1] // CI
    HALO = NTAP - 1
    NS = A_log.shape[1] // CI
    R = dt_wT.shape[0]
    XD = xp_wT.shape[1]
    NE, _, HID = w1.shape
    HM = HID // P
    CAP = int(CAPACITY_FACTOR * T / NE)
    TILES = -(-CAP // P)
    NT = T // P
    STEPS = L // TC
    W2T = NB * TC
    HN = NS // 2
    SEG = TC + 1
    TT = TC // P
    assert NB == 2 and STEPS % 2 == 0 and STEPS >= 4 and W2T == 512 and DIM == 512

    u_d = nc.dram_tensor("u_d", [DI, T], F32).ap()
    z_d = nc.dram_tensor("z_d", [DI, T], F32).ap()
    xdbl_d = nc.dram_tensor("xdbl_d", [XD, T], F32).ap()
    tn_d = nc.dram_tensor("tn_d", [T, DIM], F32).ap()

    with ExitStack() as ctx:
        sems = {}

        def sem(name):
            if name not in sems:
                sems[name] = ctx.enter_context(nc.semaphore(name))
            return sems[name]

        arena = Arena(nc)
        ctx.callback(arena.back_to, 0)
        bank = [ctx.enter_context(nc.psum_tensor(f"bank{i}", [P, 512], F32)) for i in range(8)]

        ident = arena.take(P)
        mean_w = arena.take(P)
        ones = arena.take(P)
        below = arena.take(P)
        logits = arena.take(NT * NE)
        slot_get = arena.take(NE * TILES).bitcast(I32)
        slot_put = arena.take(NE * TILES).bitcast(I32)
        slot_w = arena.take(NE * TILES)
        LASTING = arena.mark()

        s_const = sem("constants_made")
        s_phase = sem("engines_through_phase")
        phase_count = {}

        in_w, in_w_r = arena.take_both(KD * 2 * DI, "p (k m) -> p k m", k=KD)
        _, in_hi_r = arena.take_both(KD * 2 * DI, "p (k m) -> p k m", k=KD)
        xp_w = arena.take(CI * XD).rearrange("p (c m) -> p c m", c=CI)
        cw = arena.take(CI * NTAP)
        cb = arena.take(CI)
        lw = arena.take(KD)
        lb = arena.take(KD)
        xn, xn_r = zip(*(arena.take_both(KD * W2T, "p (k t) -> p k t", k=KD) for _ in range(2)))
        xh, xh_r = zip(*(arena.take_both(KD * W2T, "p (k t) -> p k t", k=KD) for _ in range(2)))
        rstd = arena.take(W2T)
        xin = arena.take(CI * NB * (TC + HALO)).rearrange("p (c b t) -> p c b t", c=CI, b=NB)
        acc = [arena.take(W2T).rearrange("p (b t) -> p b t", b=NB) for _ in range(2)]
        ub = [arena.take(CI * W2T).rearrange("p (c b t) -> p c b t", c=CI, b=NB) for _ in range(2)]
        zb = [arena.take(CI * W2T).rearrange("p (c b t) -> p c b t", c=CI, b=NB) for _ in range(2)]
        xd = arena.take(W2T, XD)
        proj_ps = bank[0:4]
        mean_ps, var_ps, xd_ps = bank[4], bank[5], bank[6]

        def tok(q, b):
            return bass.ds(q * TC + b * L, TC)

        arena.back_to(LASTING)
        out_w = arena.take(CI * DIM).rearrange("p (c m) -> p c m", c=CI)
        dt_w = arena.take(DI, R + 1)
        A_neg = arena.take(CI * NS)
        dsk = arena.take(CI)
        gate_w = arena.take(KD * NE).rearrange("p (k e) -> p k e", k=KD)
        gate_bb = arena.take(NE)
        state = arena.take(NB * CI * NS).rearrange("p (b c n) -> p b c n", b=NB, c=CI)
        dtT = [arena.take(TC, R + 1) for _ in range(2)]
        Brep = [arena.take(NS * TC).rearrange("p (n t) -> p n t", n=NS) for _ in range(2)]
        Crep = [arena.take(NS * TC).rearrange("p (n t) -> p n t", n=NS) for _ in range(2)]
        delta = [arena.take(CI * TC).rearrange("p (c t) -> p c t", c=CI) for _ in range(2)]
        HC = CI // 2
        sp_e = arena.take(HC * TC)
        sp_l = arena.take(HC * TC)
        sp_q = arena.take(HC * TC)
        log_a = arena.take(len(LOG_SQUARES))
        RING = 4
        u_t = [arena.take(TC) for _ in range(RING)]
        z_t = [arena.take(TC) for _ in range(RING)]
        du = [arena.take(TC) for _ in range(2)]
        dA = [arena.take(HN * SEG) for _ in range(2)]
        hb = [arena.take(HN * SEG) for _ in range(4)]
        yg = [arena.take(TC) for _ in range(2)]
        x1 = arena.take(TT * DIM).rearrange("p (a m) -> p a m", a=TT)
        tn = arena.take(TT * DIM).rearrange("p (a m) -> p a m", a=TT)
        tnT = arena.take(DIM)
        bst = arena.take(TT * 6)
        mv = arena.take(TT * 2)
        rs = arena.take(TT)
        newt = arena.take(TT)
        sum_ps = bank[0:2]
        dt_ps = bank[2:4]
        out_ps = bank[4:6]
        tr_ps, lg_ps = bank[6], bank[7]

        PE_DT = (0, 2)
        ACT_RELU = (4, 8)
        ACT_EXP = (4, 10)
        ACT_SQUARE = (5, 7, 9, 11, 13, 15)
        DVE_LOG = (5, 5, 7, 9, 10, 11, 11, 13, 15, 15)
        LOG_STEPS = len(LOG_SQUARES) + 2

        def seg(t):
            return t.rearrange("p (n t) -> p n t", n=HN)

        arena.back_to(LASTING)
        _, w1_hi_r = arena.take_both(KD * HID, "p (k m) -> p k m", k=KD)
        w1_lo, w1_lo_r = arena.take_both(KD * HID, "p (k m) -> p k m", k=KD)
        _, w2_hi_r = arena.take_both(HM * DIM, "p (h m) -> p h m", h=HM)
        w2_lo, w2_lo_r = arena.take_both(HM * DIM, "p (h m) -> p h m", h=HM)
        b1_s = arena.take(HM)
        b2_s = arena.take(DIM)
        EXPERT_WEIGHTS = arena.mark()
        CH = 4
        HCH = HM // CH

        def w_chunk(which, t, ch):
            if which == 1:
                return t[:, :, ch * HCH * P:(ch + 1) * HCH * P]
            return t[:, ch * HCH:(ch + 1) * HCH, :]

        w_hi_r = {1: w1_hi_r, 2: w2_hi_r}
        w_lo, w_lo_r = {1: w1_lo, 2: w2_lo}, {1: w1_lo_r, 2: w2_lo_r}


        def table():
            return arena.take(NE * NT).rearrange("p (e j) -> p e j", e=NE)

        prob, rank, wm, hit, gtm, eqm, posg, posq, tmp, keep = (table() for _ in range(10))
        seg0 = table()
        tmax = arena.take(NT)
        tsum = arena.take(NT)
        pick = arena.take(NT)
        miss = arena.take(NT)
        thr = arena.take(NE).bitcast(I32)
        TRY = 3
        cand = arena.take(TRY * NE).bitcast(I32)
        bits = arena.take(TRY * NE).bitcast(I32)
        hits = arena.take(TRY * NE * NT)
        cnt = arena.take(TRY * NE)
        cond = arena.take(TRY * NE)
        gain = arena.take(NE)
        gain_i = arena.take(NE).bitcast(I32)
        need = arena.take(NE)
        base = arena.take(NE)
        word = arena.take(TOPK * NT).bitcast(I32)
        NCOL = 1 + 3 * TOPK
        cols = arena.take(NT * NCOL)
        cols_v = cols.rearrange("p (j c) -> p j c", c=NCOL)
        HOT = 4
        some_cols = [arena.take(HOT * NCOL).rearrange("p (g c) -> p g c", c=NCOL) for _ in range(2)]
        count_i = arena.take(P).bitcast(I32)
        count = arena.take(P)
        token_i = arena.take(NT).bitcast(I32)
        ROWS = NE * TILES
        lo_hot = [arena.take(HOT * TOPK * P).rearrange("p (g k m) -> p g k m", g=HOT, k=TOPK) for _ in range(2)]
        hi_hot = [arena.take(HOT * TOPK * 2 * ROWS).rearrange("p (g k m) -> p g k m", g=HOT, k=TOPK)
                  for _ in range(2)]
        hi_eq = arena.take(HOT * TOPK * ROWS).rearrange("p (g k m) -> p g k m", g=HOT, k=TOPK)
        assert NT % (2 * HOT) == 0
        zeros = arena.take(max(P, 2 * ROWS))
        found = arena.take(ROWS)
        table_ps = bank[5][:, 0:2 * ROWS]

        arena.back_to(EXPERT_WEIGHTS)
        BLK = 256
        blocks = [(t0, min(BLK, CAP - t0)) for t0 in range(0, CAP, BLK)]
        NBLK = len(blocks)
        tiles_of = [[(t0 + i, min(P, n - i)) for i in range(0, n, P)] for t0, n in blocks]
        _, h_hi_r = arena.take_both(HM * BLK, "p (h t) -> p h t", h=HM)
        h_lo, h_lo_r = arena.take_both(HM * BLK, "p (h t) -> p h t", h=HM)
        _, x_hi_r = zip(*(arena.take_both(KD * BLK, "p (k t) -> p k t", k=KD) for _ in range(2)))
        _, x_lo_r = zip(*(arena.take_both(KD * BLK, "p (k t) -> p k t", k=KD) for _ in range(2)))
        XG = 2
        xg = [arena.take(DIM) for _ in range(XG)]
        get = [arena.take(1).bitcast(I32) for _ in range(XG)]
        put = [arena.take(1).bitcast(I32) for _ in range(2)]
        put_w = [arena.take(1) for _ in range(2)]
        ye = [arena.take(DIM) for _ in range(2)]
        up_ps = bank[0:3]
        dn_ps = bank[3:5]
        xt_ps = bank[5:7]

        ND = TILES
        flat = [t for b in tiles_of for t in b]
        first_of = [sum(len(x_) for x_ in tiles_of[:k]) for k in range(NBLK)]
        assert len(flat) == ND and ND % 2 == 0 and 2 * ND % XG == 0 and (XG <= ND)

        def carry(eng, register):
            eng.reg_add(register, register, 1)
            eng.reg_sub(register, register, 1)

        def alone(eng):
            eng.wait_ge(s_const, 1)

        def barrier(eng):
            n = phase_count[eng] = phase_count.get(eng, 0) + 1
            eng.drain().then_inc(s_phase, 1)
            eng.wait_ge(s_phase, 5 * n)

        block = ctx.enter_context(nc.Block())

        @block.sync
        def _(sp):
            s_w = sem("A_weights_loaded")
            sp.dma_start(xp_w, xp_wT.rearrange("(c p) m -> p c m", p=P)).then_inc(s_w, 16)
            for dst, src in ((cw, conv_w), (cb, conv_b), (lw, ln_w), (lb, ln_b)):
                sp.dma_start(dst, src).then_inc(s_w, 16)
            x_v = x.rearrange("b (k p) t -> b p k t", p=P)
            u_v = u_d.rearrange("(c p) t -> p c t", p=P)
            z_v = z_d.rearrange("(c p) t -> p c t", p=P)

            def load_x(q, s):
                at_least(sp, sem("A_projected"), 16 * (q - 1))
                for b in range(NB):
                    sp.dma_start(xn[s][:, :, b * TC:(b + 1) * TC],
                                 x_v[b][:, :, bass.ds(q * TC, TC)]).then_inc(sem(f"A_x_loaded{s}"), 16)

            def store_xdbl(q):
                sp.wait_ge(sem("A_xdbl_copied"), q + 1)
                for b in range(NB):
                    sp.dma_start(xdbl_d[:, tok(q, b)], xd[:, b * TC:(b + 1) * TC]).then_inc(sem("A_xdbl_stored"), 16)

            def step_a(q, s, first, last):
                if not first:
                    store_xdbl(q - 1)
                sp.wait_ge(sem("A_proj_read"), 16 * q + CI)
                for b in range(NB):
                    sp.dma_start(z_v[:, :, tok(q, b)], zb[s][:, :, b, :]).then_inc(sem(f"A_z_stored{s}"), 16)
                if not last:
                    load_x(q + 2, s)
                sp.wait_ge(sem("A_silu_done"), CI * (q + 1))
                for b in range(NB):
                    sp.dma_start(u_v[:, :, tok(q, b)], ub[s][:, :, b, :]).then_inc(sem(f"A_u_stored{s}"), 16)

            load_x(0, 0)
            for k in range(KD):
                sp.dma_start(in_w[:, k, :], in_wT[k * P:(k + 1) * P, :]).then_inc(sem(f"A_in_w_loaded{k}"), 16)
            load_x(1, 1)
            step_a(0, 0, True, False)
            step_a(1, 1, False, False)
            with sp.Fori(1, STEPS // 2 - 1) as j:
                step_a(2 * j, 0, False, False)
                step_a(2 * j + 1, 1, False, False)
            step_a(STEPS - 2, 0, False, True)
            step_a(STEPS - 1, 1, False, True)
            store_xdbl(STEPS - 1)
            for name in ("A_z_stored", "A_u_stored"):
                for s in range(2):
                    sp.wait_ge(sem(f"{name}{s}"), 16 * STEPS)
            sp.wait_ge(sem("A_xdbl_stored"), 32 * STEPS)
            barrier(sp)

            s_w = sem("B_weights_loaded")
            sp.dma_start(out_w, out_wT.rearrange("(c p) m -> p c m", p=P)).then_inc(s_w, 16)
            sp.dma_start(dt_w[0:R, :], dt_wT).then_inc(s_w, 16)
            sp.dma_start(dt_w[R:R + 1, :], dt_b).then_inc(s_w, 16)
            sp.dma_start(A_neg, A_log).then_inc(s_w, 16)
            sp.dma_start(dsk, D_skip).then_inc(s_w, 16)
            sp.dma_start(gate_w, gate_wT.rearrange("(k p) e -> p k e", p=P)).then_inc(s_w, 16)
            sp.dma_start(gate_bb, gate_b.broadcast_to([P, NE])).then_inc(s_w, 16)

            def load_dt(q, b):
                at_least(sp, sem("B_dt_multiplied"), 2 * (2 * q + b - 1))
                sp.dma_start(dtT[b][0:R, :], xdbl_d[0:R, tok(q, b)]).then_inc(sem(f"B_dt_loaded{b}"), 16)

            def load_bc(q, b):
                n = NB * CI * q + CI * b
                at_least(sp, sem("B_scanned"), 2 * (n - CI))
                at_least(sp, sem("B_c_multiplied"), 2 * (n - CI))
                for rep, r0 in ((Brep, R), (Crep, R + NS)):
                    src = xdbl_d[r0:r0 + NS, tok(q, b)].rearrange("(a n) t -> a n t", a=1)
                    sp.dma_start(rep[b], src.broadcast_to([P, NS, TC])).then_inc(sem(f"B_bc_loaded{b}"), 16)

            def load_unit(q, b, c):
                n = NB * CI * q + CI * b + c
                at_least(sp, sem("B_gated"), n - RING + 1)
                r = c % RING
                for t, d in ((u_t, u_d), (z_t, z_d)):
                    sp.dma_start(t[r], d[c * P:(c + 1) * P, tok(q, b)]).then_inc(sem(f"B_uz_loaded{r}"), 16)

            def tile_rows(q, b):
                return bass.ds(q * TC + b * L, TC)

            def store_group(q, b):
                g = 2 * q + b
                sp.wait_ge(sem("B_normed"), TT * (g + 1))
                for t, d in ((x1, out), (tn, tn_d)):
                    sp.dma_start(d[tile_rows(q, b), :].rearrange("(a p) m -> p a m", p=P), t)\
                        .then_inc(sem("B_tokens_stored"), 16)

            def load_xt(q, b):
                at_least(sp, sem("B_tokens_stored"), 32 * (2 * q + b))
                sp.dma_start(x1, x_tok[tile_rows(q, b), :].rearrange("(a p) m -> p a m", p=P))\
                    .then_inc(sem("B_xt_loaded"), 16)

            def before(q, b):
                return (q, 0) if b else (q - 1, 1)

            def after(q, b):
                return (q + 1, 0) if b else (q, 1)

            def group_b(q, b, first, last):
                for c in range(CI):
                    load_unit(q, b, c)
                    if c == 0 and not last:
                        load_dt(*after(q, b))
                    if c == 4 and not last:
                        load_bc(*after(q, b))
                    if c == 6 and not first:
                        store_group(*before(q, b))
                    if c == 7:
                        load_xt(q, b)

            load_dt(0, 0)
            load_bc(0, 0)
            for b in range(NB):
                group_b(0, b, b == 0, False)
            with sp.Fori(1, STEPS - 1) as q:
                for b in range(NB):
                    group_b(q, b, False, False)
            for b in range(NB):
                group_b(STEPS - 1, b, False, b == 1)
            store_group(STEPS - 1, 1)
            sp.wait_ge(sem("B_tokens_stored"), 32 * NB * STEPS)
            barrier(sp)

            def load_expert(e):
                w1_v = w1[bass.ds(e, 1)].rearrange("e (k p) m -> p (e k) m", p=P)
                w2_v = w2[bass.ds(e, 1)].rearrange("e (h p) m -> p (e h) m", p=P)
                for ch in range(CH):
                    at_least(sp, sem("D_up_done"), (e * NBLK - 1) * HM + HCH * (ch + 1))
                    sp.dma_start(w_chunk(1, w1_lo, ch), w_chunk(1, w1_v, ch)).then_inc(sem(f"D_w1_loaded{ch}"), 16)
                at_least(sp, sem("D_gelu"), e * NBLK * HM)
                sp.dma_start(b1_s, b1[bass.ds(e, 1)].rearrange("e p h -> p (e h)")).then_inc(sem("D_b1_loaded"), 16)
                at_least(sp, sem("D_down_done"), ND * e)
                for ch in range(CH):
                    sp.dma_start(w_chunk(2, w2_lo, ch), w_chunk(2, w2_v, ch)).then_inc(sem(f"D_w2_loaded{ch}"), 16)
                at_least(sp, sem("D_biased"), ND * e)
                sp.dma_start(b2_s, b2[bass.ds(e, 1)].broadcast_to([P, DIM])).then_inc(sem("D_b2_loaded"), 16)

            load_expert(0)
            barrier(sp)

            with sp.Fori(0, NE // 2 - 1) as j:
                for r in range(2):
                    load_expert(2 * j + r + 1)
            load_expert(NE - 1)
            barrier(sp)

        @block.gpsimd
        def _(pool):
            pool.memset(ident, 0.0).then_inc(sem("pool_const"), 1)
            pool.memset(below, 1.0).then_inc(sem("pool_const"), 1)
            pool.memset(ones, 1.0).then_inc(s_const, 1)
            pool.memset(mean_w, 1.0 / DIM).then_inc(s_const, 1)
            pool.wait_ge(sem("pool_const"), 2)
            pool.affine_select(out=ident, in_=ident, compare_op=ALU.not_equal, fill=1.0, base=0,
                               pattern=[[-1, P]], channel_multiplier=1).then_inc(s_const, 1)
            pool.affine_select(out=below, in_=below, compare_op=ALU.is_gt, fill=0.0, base=0,
                               pattern=[[1, P]], channel_multiplier=-1).then_inc(s_const, 1)

            def add_tiles(src, dst, ready, name, q):
                half = KD // 2
                ready()
                pool.tensor_tensor(dst[:, 0:half, :], src[:, 0:half, :], src[:, half:KD, :], ALU.add)\
                    .then_inc(sem(name), 1)
                pool.wait_ge(sem(name), 2 * q + 1)
                pool.tensor_tensor(dst[:, 0, :], dst[:, 0, :], dst[:, 1, :], ALU.add).then_inc(sem(name), 1)

            def sums_a(q, s, half):
                def x_ready():
                    pool.wait_ge(sem(f"A_x_loaded{s}"), 32 * (half + 1))
                    at_least(pool, sem("A_projected"), 16 * (q - 1))

                add_tiles(xn[s], xh[s], x_ready, "A_x_added", q)
                add_tiles(xh[s], xh[s], lambda: pool.wait_ge(sem("A_squared"), q + 1), "A_sq_added", q)

            sums_a(0, 0, 0)
            sums_a(1, 1, 0)
            with pool.Fori(1, STEPS // 2) as j:
                sums_a(2 * j, 0, j)
                sums_a(2 * j + 1, 1, j)
            barrier(pool)

            def m_slot(c, h):
                return (2 * c + h) % 4

            def inputs(q, b, c):
                n = NB * CI * q + CI * b + c
                pool.wait_ge(sem("B_du"), n + 1)
                at_least(pool, sem("B_summed"), 2 * n + 1 - 3)
                if c == 0:
                    pool.wait_ge(sem(f"B_bc_loaded{b}"), 32 * (q + 1))
                pool.tensor_tensor(seg(hb[m_slot(c, 1)])[:, HN - NPOOL:, 1:SEG],
                                   du[c % 2].rearrange("p (o t) -> p o t", o=1).broadcast_to([P, NPOOL, TC]),
                                   Brep[b][:, NS - NPOOL:, :], ALU.mult).then_inc(sem("B_pool_started"), 1)

            def times_c(q, b, c, h):
                m = 2 * (NB * CI * q + CI * b + c) + h
                pool.wait_ge(sem("B_state_kept"), m + 1)
                hv = seg(hb[m_slot(c, h)])[:, :, 1:SEG]
                pool.tensor_tensor(hv, hv, Crep[b][:, h * HN:(h + 1) * HN, :], ALU.mult)\
                    .then_inc(sem("B_c_multiplied"), 1)

            def group_b(q, b, first):
                for c in range(CI):
                    inputs(q, b, c)
                    if c > 0:
                        times_c(q, b, c - 1, 1)
                    elif not first:
                        times_c(*((q, 0) if b else (q - 1, 1)), CI - 1, 1)
                    times_c(q, b, c, 0)

            for b in range(NB):
                group_b(0, b, b == 0)
            with pool.Fori(1, STEPS) as q:
                for b in range(NB):
                    group_b(q, b, False)
            times_c(STEPS - 1, 1, CI - 1, 1)
            barrier(pool)

            pool.iota(token_i, pattern=[[P, NT]], base=1, channel_multiplier=1).then_inc(sem("C_tables"), 1)
            pool.iota(count_i, pattern=[[1, P]], base=0, channel_multiplier=0).then_inc(sem("C_tables"), 1)
            for e in range(NE):
                pool.memset(rank[:, e, :], float(NE - 1 - e)).then_inc(sem("C_tables"), 1)
                pool.memset(base[:, e:e + 1], float(e * TILES * P)).then_inc(sem("C_tables"), 1)
            pool.memset(zeros, 0.0).then_inc(sem("C_zeros"), 1)
            pool.memset(seg0, 1.0).then_inc(sem("C_seg"), 1)
            pool.wait_ge(sem("C_seg"), 1)
            pool.memset(seg0[:, :, 0], 0.0).then_inc(sem("C_tables"), 1)
            for which in (1, 2):
                for ch in range(CH):
                    pool.wait_ge(sem(f"D_w{which}_rounded"), ch + 1)
                    lo = w_chunk(which, w_lo[which], ch)
                    pool.tensor_tensor(w_chunk(which, w_lo_r[which], ch), lo,
                                       w_chunk(which, w_hi_r[which], ch).bitcast(F32), ALU.subtract)\
                        .then_inc(sem(f"D_w{which}_split"), 1)
            last_token = pool.alloc_register("last_token")
            pool.reg_mov(last_token, T - 1)
            barrier(pool)

            def gather(j, w, i):
                o = w * ND + i
                n = flat[i][1]
                at_least(pool, sem(f"D_transposed{o % XG}"), j * (2 * ND // XG) + o // XG)
                pool.wait_ge(sem("D_get_ready"), 2 * ND * j + o + 1)
                carry(pool, last_token)
                pool.indirect_dma_start(xg[o % XG][0:n, :], None, tn_d,
                                        bass.IndirectOffsetOnAxis(get[o % XG][0:n, :], 0),
                                        bounds_check=last_token, oob_is_err=False)\
                    .then_inc(sem(f"D_gathered{o % XG}"), 16)

            def gathers(j, w, k):
                for i in range(len(tiles_of[k])):
                    gather(j, w, first_of[k] + i)

            def adds(j, w, k):
                e = 2 * j + w
                if k == 0:
                    for p in range(2):
                        at_least(pool, sem(f"D_added{p}"), 16 * (ND // 2) * e)
                for i in range(first_of[k], first_of[k] + len(tiles_of[k])):
                    n = flat[i][1]
                    pool.wait_ge(sem("D_weighted"), ND * e + i + 1)
                    carry(pool, last_token)
                    pool.indirect_dma_start(out, bass.IndirectOffsetOnAxis(put[i % 2][0:n, :], 0),
                                            ye[i % 2][0:n, :], None, bounds_check=last_token,
                                            oob_is_err=False, compute_op=ALU.add)\
                        .then_inc(sem(f"D_added{i % 2}"), 16)

            def round_d(j, last):
                for w in range(2):
                    for k in range(NBLK):
                        if k + 1 < NBLK:
                            gathers(j, w, k + 1)
                        elif w == 0:
                            gathers(j, 1, 0)
                        elif not last:
                            gathers(j + 1, 0, 0)
                        adds(j, w, k)

            gathers(0, 0, 0)
            round_d(0, False)
            with pool.Fori(1, NE // 2 - 1) as j:
                round_d(j, False)
            round_d(NE // 2 - 1, True)
            for p in range(2):
                pool.wait_ge(sem(f"D_added{p}"), 16 * (ND // 2) * NE)
            barrier(pool)

        @block.scalar
        def _(act):
            act.wait_ge(sem("A_weights_loaded"), 80)

            def square(q, s):
                act.wait_ge(sem("A_centred"), q + 1)
                act.activation(xh[s], xn[s], ACT.Square).then_inc(sem("A_squared"), 1)

            def root(q):
                act.wait_ge(sem("A_var_scaled"), q + 1)
                act.activation(rstd, rstd, ACT.Sqrt).then_inc(sem("A_rooted"), 1)

            def affine(q, s):
                act.wait_ge(sem("A_scaled"), q + 1)
                for k in range(KD):
                    i = act.activation(xn[s][:, k, :], xn[s][:, k, :], ACT.Identity,
                                       bias=lb[:, k:k + 1], scale=lw[:, k:k + 1])
                i.then_inc(sem("A_normalised"), 1)

            def copy_z(q, s, i):
                act.wait_ge(sem("A_projected"), 16 * q + i + 1)
                act.activation(zb[s][:, i], proj_ps[i % 4][:, :].rearrange("p (b t) -> p b t", b=NB), ACT.Silu)\
                    .then_inc(sem("A_proj_read"), 1)

            def copy_xin(q, c):
                act.wait_ge(sem("A_projected"), 16 * q + CI + c + 1)
                if c == 0:
                    at_least(act, sem("A_halo_saved"), q + 1)
                act.activation(xin[:, c, :, HALO:], proj_ps[c % 4][:, :].rearrange("p (b t) -> p b t", b=NB),
                               ACT.Copy).then_inc(sem("A_proj_read"), 1)

            def silu_u(q, s, c):
                act.wait_ge(sem("A_convolved"), CI * q + c + 1)
                act.activation(ub[s][:, c], acc[c % 2], ACT.Silu).then_inc(sem("A_silu_done"), 1)

            def copy_xdbl(q):
                act.wait_ge(sem("A_xdbl_done"), q + 1)
                at_least(act, sem("A_xdbl_stored"), 32 * q)
                act.activation(xd, xd_ps[0:XD, :], ACT.Copy).then_inc(sem("A_xdbl_copied"), 1)

            def step_a(q, s, half, first, last):
                at_least(act, sem(f"A_z_stored{s}"), 32 * half)
                for i in range(CI):
                    copy_z(q, s, i)
                    if i == 2 and not last:
                        square(q + 1, 1 - s)
                    if i == 5 and not first:
                        copy_xdbl(q - 1)
                    if i == 6 and not last:
                        root(q + 1)
                if not last:
                    affine(q + 1, 1 - s)
                at_least(act, sem(f"A_u_stored{s}"), 32 * half)
                for c in range(CI):
                    copy_xin(q, c)
                    if c >= 1:
                        silu_u(q, s, c - 1)
                silu_u(q, s, CI - 1)

            square(0, 0)
            root(0)
            affine(0, 0)
            step_a(0, 0, 0, True, False)
            step_a(1, 1, 0, False, False)
            with act.Fori(1, STEPS // 2 - 1) as j:
                step_a(2 * j, 0, j, False, False)
                step_a(2 * j + 1, 1, j, False, False)
            step_a(STEPS - 2, 0, STEPS // 2 - 1, False, False)
            step_a(STEPS - 1, 1, STEPS // 2 - 1, False, True)
            copy_xdbl(STEPS - 1)
            barrier(act)

            act.wait_ge(sem("B_weights_loaded"), 112)
            nc.scalar.preload_act_table_set("natural_log_exp_and_others")
            act.activation(A_neg, A_neg, ACT.Exp).then_inc(sem("B_a_exp"), 1)
            act.wait_ge(sem("B_a_exp"), 1)
            act.activation(A_neg, A_neg, ACT.Copy, scale=-1.0).then_inc(sem("B_a_ready"), 1)
            act.wait_ge(sem("B_a_ready"), 1)
            act.wait_ge(sem("B_set_up"), 5 + len(LOG_SQUARES))

            def relu_v(q, b, i):
                g2 = 2 * (2 * q + b) + i
                act.wait_ge(sem("B_dt_multiplied"), g2 + 1)
                for a in range(2):
                    o = delta[b][:, i * HC + 2 * a:i * HC + 2 * a + 2, :].rearrange("p c t -> p (c t)")
                    act.activation(o, dt_ps[a][:, :], ACT.Relu).then_inc(sem("B_relu"), 1)

            def exp_v(q, b, i):
                g2 = 2 * (2 * q + b) + i
                at_least(act, sem("B_product_started"), g2)
                at_least(act, sem("B_squared"), len(LOG_SQUARES) * g2)
                for a in range(2):
                    ins = act.activation(sp_e[:, a * 512:(a + 1) * 512], dt_ps[a][:, :], ACT.Abs)
                ins.then_inc(sem("B_abs"), 1)
                act.wait_ge(sem("B_abs"), g2 + 1)
                act.activation(sp_e, sp_e, ACT.Exp, scale=-1.0).then_inc(sem("B_exp"), 1)

            def square(q, b, i, k):
                g2 = 2 * (2 * q + b) + i
                if k == 0:
                    act.wait_ge(sem("B_exp"), g2 + 1)
                at_least(act, sem("B_square_used"), len(LOG_SQUARES) * g2 + k)
                act.activation(sp_q, sp_e, ACT.Square, bias=log_a[:, k:k + 1]).then_inc(sem("B_squared"), 1)

            def keep_state(q, b, c, h):
                m = 2 * (NB * CI * q + CI * b + c) + h
                act.wait_ge(sem("B_scanned"), m + 1)
                act.activation(state[:, b, c, h * HN:(h + 1) * HN], seg(hb[(2 * c + h) % 4])[:, :, TC], ACT.Copy)\
                    .then_inc(sem("B_state_kept"), 1)

            def decays(q, b, c, h):
                m = 2 * (NB * CI * q + CI * b + c) + h
                if c in (0, HC) and h == 0:
                    act.wait_ge(sem("B_delta_made"), 2 * (2 * q + b) + 1 + c // HC)
                for n in range(HN):
                    act.activation(seg(dA[h])[:, n, 1:SEG], delta[b][:, c, :], ACT.Exp,
                                   scale=A_neg[:, c * NS + h * HN + n:c * NS + h * HN + n + 1])
                at_least(act, sem("B_summed"), m - 3)
                at_least(act, sem("B_state_kept"), m + 1 - 2 * NB * CI)
                act.activation(seg(hb[(2 * c + h) % 4])[:, :, 0], state[:, b, c, h * HN:(h + 1) * HN], ACT.Copy)\
                    .then_inc(sem("B_decays"), 1)

            def skip(q, b, c):
                n = NB * CI * q + CI * b + c
                act.wait_ge(sem("B_du"), n + 1)
                act.activation(u_t[c % RING], u_t[c % RING], ACT.Identity, scale=dsk[:, c:c + 1])\
                    .then_inc(sem("B_skip"), 1)

            def copy_x1(q, b):
                g = 2 * q + b
                act.wait_ge(sem("B_out_done"), CI * (g + 1))
                for a in range(TT):
                    act.activation(x1[:, a, :], out_ps[a][:, :], ACT.Copy).then_inc(sem("B_x1_copied"), 1)

            def token_rstd(q, b):
                g = 2 * q + b
                act.wait_ge(sem("B_stats"), g + 1)
                act.activation(rs, mv.rearrange("p (a c) -> p a c", c=2)[:, :, 1], ACT.Ln).then_inc(sem("B_rs_log"), 1)
                act.wait_ge(sem("B_rs_log"), g + 1)
                act.activation(rs, rs, ACT.Exp, scale=-0.5).then_inc(sem("B_rs"), 1)

            def copy_tnT(q, b, a):
                act.wait_ge(sem("B_transposed"), TT * (2 * q + b) + a + 1)
                at_least(act, sem("B_logits_done"), TT * (2 * q + b) + a)
                act.activation(tnT, tr_ps[:, :], ACT.Copy).then_inc(sem("B_tnT"), 1)

            def before(q, b):
                return (q, 0) if b else (q - 1, 1)

            def after(q, b):
                return (q + 1, 0) if b else (q, 1)

            def group_b(q, b, first, last):
                for c in range(CI):
                    for h in range(2):
                        if c > 0:
                            keep_state(q, b, c - 1, h)
                        elif not first:
                            keep_state(*before(q, b), CI - 1, h)
                        decays(q, b, c, h)
                        if h == 0:
                            skip(q, b, c)
                        if not last:
                            if 2 * c + h in ACT_RELU:
                                relu_v(*after(q, b), ACT_RELU.index(2 * c + h))
                            if 2 * c + h in ACT_EXP:
                                exp_v(*after(q, b), ACT_EXP.index(2 * c + h))
                            if 2 * c + h in ACT_SQUARE:
                                square(*after(q, b), *divmod(ACT_SQUARE.index(2 * c + h), len(LOG_SQUARES)))
                    if not first:
                        if c == 2:
                            copy_x1(*before(q, b))
                        if c == 3:
                            token_rstd(*before(q, b))
                        if c in (5, 6):
                            copy_tnT(*before(q, b), c - 5)

            for i in range(2):
                relu_v(0, 0, i)
                exp_v(0, 0, i)
                for k in range(len(LOG_SQUARES)):
                    square(0, 0, i, k)
            for b in range(NB):
                group_b(0, b, b == 0, False)
            with act.Fori(1, STEPS - 1) as q:
                for b in range(NB):
                    group_b(q, b, False, False)
            for b in range(NB):
                group_b(STEPS - 1, b, False, b == 1)
            for h in range(2):
                keep_state(STEPS - 1, 1, CI - 1, h)
            copy_x1(STEPS - 1, 1)
            token_rstd(STEPS - 1, 1)
            for a in range(TT):
                copy_tnT(STEPS - 1, 1, a)
            barrier(act)

            def round_w(which, e, ch):
                act.wait_ge(sem(f"D_w{which}_loaded{ch}"), 16 * (e + 1))
                act.activation(w_chunk(which, w_hi_r[which], ch), w_chunk(which, w_lo[which], ch), ACT.Copy)\
                    .then_inc(sem(f"D_w{which}_rounded"), 1)

            act.wait_ge(sem("C_shifted"), 1)
            act.activation(prob, prob, ACT.Exp).then_inc(sem("C_exp"), 1)
            for which in (1, 2):
                for ch in range(CH):
                    round_w(which, 0, ch)
            barrier(act)

            def gelu(e, k, h):
                t0, n = blocks[k]
                up = (e * NBLK + k) * HM + h
                if k == 0 and h == 0:
                    act.wait_ge(sem("D_b1_loaded"), 16 * (e + 1))
                act.wait_ge(sem("D_up_done"), up + 1)
                act.activation(h_lo[:, h, 0:n], up_ps[h % 3][:, 0:n], ACT.Gelu,
                               bias=b1_s[:, h:h + 1]).then_inc(sem("D_gelu"), 1)
                if h % 2 == 1:
                    act.wait_ge(sem("D_gelu"), up + 1)
                    act.activation(h_hi_r[:, h - 1:h + 1, 0:n], h_lo[:, h - 1:h + 1, 0:n], ACT.Copy)\
                        .then_inc(sem("D_h_rounded"), 1)

            W2_AT = (5, 9, 12, 15)

            def expert_d(e, first, last):
                for k in range(NBLK):
                    for h in range(HM):
                        gelu(e, k, h)
                        if k == 0 and not first and h in W2_AT:
                            round_w(2, e, W2_AT.index(h))
                if not last:
                    for ch in range(CH):
                        round_w(1, e + 1, ch)

            expert_d(0, True, False)
            expert_d(1, False, False)
            with act.Fori(1, NE // 2 - 1) as j:
                for w in range(2):
                    expert_d(2 * j + w, False, False)
            expert_d(NE - 2, False, False)
            expert_d(NE - 1, False, True)
            barrier(act)

        @block.tensor
        def _(pe):
            pe.wait_ge(s_const, 4)
            pe.wait_ge(sem("A_weights_loaded"), 80)

            def mean(q, s):
                pe.wait_ge(sem("A_x_added"), 2 * (q + 1))
                at_least(pe, sem("A_centred"), q)
                pe.matmul(mean_ps[:, :], mean_w, xh[s][:, 0, :], start=True, stop=True)\
                    .then_inc(sem("A_mean_done"), 1)

            def var(q, s):
                pe.wait_ge(sem("A_sq_added"), 2 * (q + 1))
                at_least(pe, sem("A_var_scaled"), q)
                pe.matmul(var_ps[:, :], mean_w, xh[s][:, 0, :], start=True, stop=True)\
                    .then_inc(sem("A_var_done"), 1)

            def project(q, s, i):
                at_least(pe, sem("A_proj_read"), 16 * q + i - 3)
                m = (CI + i) % (2 * CI)
                o = proj_ps[i % 4][:, :]
                for k in range(KD):
                    hi, lo = in_hi_r[:, k, m * P:(m + 1) * P], in_w_r[:, k, m * P:(m + 1) * P]
                    pe.matmul(o, hi, xh_r[s][:, k, :], start=(k == 0), stop=False)
                    pe.matmul(o, hi, xn_r[s][:, k, :], start=False, stop=False)
                    ins = pe.matmul(o, lo, xh_r[s][:, k, :], start=False, stop=(k == KD - 1))
                ins.then_inc(sem("A_projected"), 1)

            def xdbl(q, s):
                pe.wait_ge(sem("A_silu_done"), CI * (q + 1))
                at_least(pe, sem("A_xdbl_copied"), q)
                for c in range(CI):
                    i = pe.matmul(xd_ps[0:XD, :], xp_w[:, c, :], ub[s][:, c].rearrange("p b t -> p (b t)"),
                                  start=(c == 0), stop=(c == CI - 1))
                i.then_inc(sem("A_xdbl_done"), 1)

            def step_a(q, s, half, first, last):
                pe.wait_ge(sem("A_xn_ready"), q + 1)
                for i in range(16):
                    if i == 3 and not last:
                        mean(q + 1, 1 - s)
                    if i == 5 and not first:
                        xdbl(q - 1, 1 - s)
                    if i == 6 and not last:
                        var(q + 1, 1 - s)
                    project(q, s, i)

            mean(0, 0)
            var(0, 0)
            pe.wait_ge(sem("A_w_split"), KD)
            step_a(0, 0, 0, True, False)
            step_a(1, 1, 0, False, False)
            with pe.Fori(1, STEPS // 2 - 1) as j:
                step_a(2 * j, 0, j, False, False)
                step_a(2 * j + 1, 1, j, False, False)
            step_a(STEPS - 2, 0, STEPS // 2 - 1, False, False)
            step_a(STEPS - 1, 1, STEPS // 2 - 1, False, True)
            xdbl(STEPS - 1, 1)
            barrier(pe)

            pe.wait_ge(sem("B_weights_loaded"), 112)
            pe.wait_ge(sem("B_set_up"), 5 + len(LOG_SQUARES))

            def dt_product(q, b, i):
                g2 = 2 * (2 * q + b) + i
                if i == 0:
                    pe.wait_ge(sem(f"B_dt_loaded{b}"), 16 * (q + 1))
                at_least(pe, sem("B_abs"), g2)
                for a in range(HC):
                    c = i * HC + a
                    ins = pe.matmul(dt_ps[a // 2][:, (a % 2) * TC:(a % 2 + 1) * TC],
                                    dt_w[:, c * P:(c + 1) * P], dtT[b], start=True, stop=True)
                ins.then_inc(sem("B_dt_multiplied"), 1)

            def sums(q, b, c):
                n = NB * CI * q + CI * b + c
                at_least(pe, sem("B_gated"), n - 1)
                o = sum_ps[c % 2][:, 0:TC]
                pe.wait_ge(sem("B_skip"), n + 1)
                pe.matmul(o, ident, u_t[c % RING], start=True, stop=False)
                for h in range(2):
                    pe.wait_ge(sem("B_c_multiplied"), 2 * n + h + 1)
                    for k in range(HN):
                        ins = pe.matmul(o, ident, seg(hb[(2 * c + h) % 4])[:, k, 1:SEG],
                                        start=False, stop=(h == 1 and k == HN - 1))
                    ins.then_inc(sem("B_summed"), 1)

            def out_product(q, b, c):
                n = NB * CI * q + CI * b + c
                if c == 0:
                    at_least(pe, sem("B_x1_copied"), TT * (2 * q + b))
                pe.wait_ge(sem("B_gated"), n + 1)
                for a in range(TT):
                    ins = pe.matmul(out_ps[a][:, :], yg[c % 2][:, a * P:(a + 1) * P], out_w[:, c, :],
                                    start=(c == 0), stop=False)
                if c == CI - 1:
                    pe.wait_ge(sem("B_xt_loaded"), 16 * (2 * q + b + 1))
                    for a in range(TT):
                        ins = pe.matmul(out_ps[a][:, :], ident, x1[:, a, :], start=False, stop=True)
                ins.then_inc(sem("B_out_done"), 1)

            def transpose_tn(q, b, a):
                t = TT * (2 * q + b) + a
                pe.wait_ge(sem("B_normed"), t + 1)
                at_least(pe, sem("B_tnT"), t)
                for k in range(KD):
                    ins = pe.transpose(tr_ps[:, k * P:(k + 1) * P], tn[:, a, k * P:(k + 1) * P], ident)
                ins.then_inc(sem("B_transposed"), 1)

            def logit(q, b, a):
                t = TT * (2 * q + b) + a
                pe.wait_ge(sem("B_tnT"), t + 1)
                at_least(pe, sem("B_logits_kept"), t)
                for k in range(KD):
                    ins = pe.matmul(lg_ps[:, 0:NE], tnT[:, k * P:(k + 1) * P], gate_w[:, k, :],
                                    start=(k == 0), stop=(k == KD - 1))
                ins.then_inc(sem("B_logits_done"), 1)

            def before(q, b):
                return (q, 0) if b else (q - 1, 1)

            def after(q, b):
                return (q + 1, 0) if b else (q, 1)

            def group_b(q, b, first, last):
                for c in range(CI):
                    if c in PE_DT and not last:
                        dt_product(*after(q, b), PE_DT.index(c))
                    sums(q, b, c)
                    if c > 0:
                        out_product(q, b, c - 1)
                    elif not first:
                        out_product(*before(q, b), CI - 1)
                    if not first:
                        if c in (4, 5):
                            logit(*before(q, b), c - 4)
                        if c in (3, 4):
                            transpose_tn(*before(q, b), c - 3)

            for i in range(2):
                dt_product(0, 0, i)
            for b in range(NB):
                group_b(0, b, b == 0, False)
            with pe.Fori(1, STEPS - 1) as q:
                for b in range(NB):
                    group_b(q, b, False, False)
            for b in range(NB):
                group_b(STEPS - 1, b, False, b == 1)
            out_product(STEPS - 1, 1, CI - 1)
            for a in range(TT):
                transpose_tn(STEPS - 1, 1, a)
                logit(STEPS - 1, 1, a)
            barrier(pe)

            with pe.Fori(0, 15) as i:
                pe.wait_ge(sem("C_counted"), i + 1)
                pe.matmul(bank[0][:, 0:TRY * NE], ones, cnt, start=True, stop=True).then_inc(sem("C_total"), 1)
            pe.wait_ge(sem("C_masks"), 1)
            flat2 = "p e j -> p (e j)"
            pe.matmul(bank[1][:, 0:NE * NT], below, gtm.rearrange(flat2), start=True, stop=True)
            pe.matmul(bank[2][:, 0:NE * NT], ones, gtm.rearrange(flat2), start=True, stop=True)
            pe.matmul(bank[3][:, 0:NE * NT], below, eqm.rearrange(flat2), start=True, stop=True)
            pe.matmul(bank[4][:, 0:NE * NT], ones, eqm.rearrange(flat2), start=True, stop=True)\
                .then_inc(sem("C_prefixes"), 1)
            pe.wait_ge(sem("C_zeros"), 1)
            pe.matmul(table_ps, zeros[:, 0:P], zeros[:, 0:2 * ROWS], start=True, stop=False)
            with pe.Fori(0, NT // (2 * HOT)) as j:
                for r in range(2):
                    pe.wait_ge(sem("C_hot"), 2 * j + r + 1)
                    for g in range(HOT):
                        for k in range(TOPK):
                            ins = pe.matmul(table_ps, lo_hot[r][:, g, k, :], hi_hot[r][:, g, k, :],
                                            start=False, stop=False)
                    ins.then_inc(sem("C_hot_used"), 1)
            pe.matmul(table_ps, zeros[:, 0:P], zeros[:, 0:2 * ROWS], start=False, stop=True).then_inc(sem("C_table"), 1)
            barrier(pe)


            def transposes(j, w, k):
                for i, (t0, n) in enumerate(tiles_of[k]):
                    o = w * ND + first_of[k] + i
                    pe.wait_ge(sem(f"D_gathered{o % XG}"), 16 * (j * (2 * ND // XG) + o // XG + 1))
                    at_least(pe, sem("D_xt_copied"), j * 2 * ND + o - 1)
                    for kk in range(KD):
                        ins = pe.transpose(xt_ps[o % 2][:, kk * P:kk * P + n], xg[o % XG][0:n, kk * P:(kk + 1) * P],
                                           ident[0:n, 0:n])
                    ins.then_inc(sem(f"D_transposed{o % XG}"), 1)

            def up(j, w, k):
                t0, n = blocks[k]
                e = 2 * j + w
                xb = (w * NBLK + k) % 2
                pe.wait_ge(sem("D_xt_copied"), ND * e + first_of[k] + len(tiles_of[k]))
                for h in range(HM):
                    if k == 0 and h % HCH == 0:
                        pe.wait_ge(sem("D_w1_split"), CH * e + h // HCH + 1)
                    at_least(pe, sem("D_gelu"), (e * NBLK + k) * HM + h - 2)
                    o = up_ps[h % 3][:, 0:n]
                    for kk in range(KD):
                        hi, lo = w1_hi_r[:, kk, h * P:(h + 1) * P], w1_lo_r[:, kk, h * P:(h + 1) * P]
                        pe.matmul(o, hi, x_hi_r[xb][:, kk, 0:n], start=(kk == 0), stop=False)
                        pe.matmul(o, hi, x_lo_r[xb][:, kk, 0:n], start=False, stop=False)
                        ins = pe.matmul(o, lo, x_hi_r[xb][:, kk, 0:n], start=False, stop=(kk == KD - 1))
                    ins.then_inc(sem("D_up_done"), 1)

            def down(j, w, k):
                e = 2 * j + w
                for i, (t0, n) in enumerate(tiles_of[k]):
                    o = first_of[k] + i
                    at_least(pe, sem("D_biased"), ND * e + o - 1)
                    c0 = t0 - blocks[k][0]
                    ps = dn_ps[o % 2][0:n, :]
                    for h in range(HM):
                        if i == 0 and k == 0 and h % HCH == 0:
                            pe.wait_ge(sem("D_w2_split"), CH * e + h // HCH + 1)
                        if i == 0 and h % 2 == 0:
                            pe.wait_ge(sem("D_h_split"), (e * NBLK + k) * (HM // 2) + h // 2 + 1)
                        hi, lo = h_hi_r[:, h, c0:c0 + n], h_lo_r[:, h, c0:c0 + n]
                        pe.matmul(ps, hi, w2_hi_r[:, h, :], start=(h == 0), stop=False)
                        pe.matmul(ps, hi, w2_lo_r[:, h, :], start=False, stop=False)
                        ins = pe.matmul(ps, lo, w2_hi_r[:, h, :], start=False, stop=(h == HM - 1))
                    ins.then_inc(sem("D_down_done"), 1)

            def round_d(j, last):
                for w in range(2):
                    for k in range(NBLK):
                        up(j, w, k)
                        if k + 1 < NBLK:
                            transposes(j, w, k + 1)
                        elif w == 0:
                            transposes(j, 1, 0)
                        elif not last:
                            transposes(j + 1, 0, 0)
                        down(j, w, k)

            transposes(0, 0, 0)
            round_d(0, False)
            with pe.Fori(1, NE // 2 - 1) as j:
                round_d(j, False)
            round_d(NE // 2 - 1, True)
            barrier(pe)

        @block.vector
        def _(dve):
            dve.wait_ge(sem("A_weights_loaded"), 80)
            dve.memset(xin[:, :, :, 0:HALO], 0.0).then_inc(sem("A_halo_saved"), 1)

            def over_k(t):
                return t.rearrange("p (o t) -> p o t", o=1).broadcast_to([P, KD, W2T])

            def centre(q, s):
                dve.wait_ge(sem("A_mean_done"), q + 1)
                dve.tensor_tensor(xn[s], xn[s], over_k(mean_ps[:, :]), ALU.subtract).then_inc(sem("A_centred"), 1)

            def scale_var(q):
                dve.wait_ge(sem("A_var_done"), q + 1)
                dve.tensor_scalar(rstd, var_ps[:, :], 1.0 + EPS_MAMBA, EPS_CHANNEL * EPS_MAMBA, ALU.mult, ALU.add)\
                    .then_inc(sem("A_var_scaled"), 1)

            def scale(q, s):
                dve.wait_ge(sem("A_rooted"), q + 1)
                dve.reciprocal(rstd, rstd).then_inc(sem("A_inverted"), 1)
                dve.wait_ge(sem("A_inverted"), q + 1)
                dve.tensor_tensor(xn[s], xn[s], over_k(rstd), ALU.mult).then_inc(sem("A_scaled"), 1)

            def split_x(q, s):
                dve.wait_ge(sem("A_normalised"), q + 1)
                dve.tensor_copy(xh_r[s], xn[s]).then_inc(sem("A_x_rounded"), 1)
                dve.wait_ge(sem("A_x_rounded"), q + 1)
                dve.tensor_tensor(xn_r[s], xn[s], xh_r[s].bitcast(F32), ALU.subtract)\
                    .then_inc(sem("A_xn_ready"), 1)

            def split_w(k):
                dve.wait_ge(sem(f"A_in_w_loaded{k}"), 16)
                dve.tensor_copy(in_hi_r[:, k, :], in_w[:, k, :]).then_inc(sem("A_w_rounded"), 1)
                dve.wait_ge(sem("A_w_rounded"), k + 1)
                dve.tensor_tensor(in_w_r[:, k, :], in_w[:, k, :], in_hi_r[:, k, :].bitcast(F32),
                                  ALU.subtract).then_inc(sem("A_w_split"), 1)

            def convolve(q, c):
                dve.wait_ge(sem("A_proj_read"), 16 * q + CI + c + 1)
                at_least(dve, sem("A_silu_done"), CI * q + c - 1)
                o = acc[c % 2]
                taps = NTAP - 1
                dve.tensor_scalar(o, xin[:, c, :, 0:TC], cw[:, c * NTAP:c * NTAP + 1], cb[:, c:c + 1], ALU.mult, ALU.add)\
                    .then_inc(sem("A_tap"), 1)
                for k in range(1, NTAP):
                    dve.wait_ge(sem("A_tap"), taps * (CI * q + c) + k)
                    i = dve.scalar_tensor_tensor(out=o, in0=xin[:, c, :, k:k + TC],
                                                 scalar=cw[:, c * NTAP + k:c * NTAP + k + 1], in1=o,
                                                 op0=ALU.mult, op1=ALU.add)
                    i.then_inc(sem("A_tap" if k < taps else "A_convolved"), 1)

            def save_halo(q):
                dve.wait_ge(sem("A_convolved"), CI * (q + 1))
                dve.tensor_copy(xin[:, :, :, 0:HALO], xin[:, :, :, TC:TC + HALO]).then_inc(sem("A_halo_saved"), 1)

            def step_a(q, s, last):
                if not last:
                    centre(q + 1, 1 - s)
                    scale_var(q + 1)
                    scale(q + 1, 1 - s)
                    split_x(q + 1, 1 - s)
                for c in range(CI):
                    convolve(q, c)
                save_halo(q)

            centre(0, 0)
            scale_var(0)
            scale(0, 0)
            split_w(0)
            split_x(0, 0)
            for k in range(1, KD):
                split_w(k)
            step_a(0, 0, False)
            step_a(1, 1, False)
            with dve.Fori(1, STEPS // 2 - 1) as j:
                step_a(2 * j, 0, False)
                step_a(2 * j + 1, 1, False)
            step_a(STEPS - 2, 0, False)
            step_a(STEPS - 1, 1, True)
            barrier(dve)

            for t in dtT:
                dve.memset(t[R:R + 1, :], 1.0).then_inc(sem("B_set_up"), 1)
            dve.memset(state, 0.0).then_inc(sem("B_set_up"), 1)
            for k, (a, _) in enumerate(LOG_SQUARES):
                dve.memset(log_a[:, k:k + 1], a).then_inc(sem("B_set_up"), 1)
            for t in dA:
                dve.memset(seg(t)[:, :, 0], 0.0).then_inc(sem("B_set_up"), 1)
            dve.wait_ge(sem("B_weights_loaded"), 112)
            dve.wait_ge(sem("B_set_up"), 5 + len(LOG_SQUARES))

            def log_step(q, b, i, k):
                g2 = 2 * (2 * q + b) + i
                if k == 0:
                    dve.wait_ge(sem("B_exp"), g2 + 1)
                    at_least(dve, sem("B_delta_made"), g2)
                    dve.scalar_tensor_tensor(out=sp_l, in0=sp_e, scalar=LOG_ROOT, in1=sp_e,
                                             op0=ALU.subtract, op1=ALU.mult).then_inc(sem("B_product_started"), 1)
                elif k < LOG_STEPS - 1:
                    if k == 1:
                        dve.wait_ge(sem("B_product_started"), g2 + 1)
                    else:
                        dve.wait_ge(sem("B_square_used"), len(LOG_SQUARES) * g2 + k - 1)
                    dve.wait_ge(sem("B_squared"), len(LOG_SQUARES) * g2 + k)
                    dve.scalar_tensor_tensor(out=sp_l, in0=sp_q, scalar=LOG_SQUARES[k - 1][1], in1=sp_l,
                                             op0=ALU.add, op1=ALU.mult).then_inc(sem("B_square_used"), 1)
                else:
                    dve.wait_ge(sem("B_square_used"), len(LOG_SQUARES) * (g2 + 1))
                    dve.wait_ge(sem("B_relu"), 2 * (g2 + 1))
                    o = delta[b][:, i * HC:(i + 1) * HC, :].rearrange("p c t -> p (c t)")
                    dve.scalar_tensor_tensor(out=o, in0=sp_l, scalar=LOG_LEAD, in1=o, op0=ALU.mult, op1=ALU.add)\
                        .then_inc(sem("B_delta_made"), 1)

            def input_u(q, b, c):
                n = NB * CI * q + CI * b + c
                r = c % RING
                if c in (0, HC):
                    dve.wait_ge(sem("B_delta_made"), 2 * (2 * q + b) + 1 + c // HC)
                dve.wait_ge(sem(f"B_uz_loaded{r}"), 32 * (q * (NB * CI // RING) + (CI * b + c) // RING + 1))
                at_least(dve, sem("B_pool_started"), n - 1)
                dve.tensor_tensor(du[c % 2], delta[b][:, c, :], u_t[r], ALU.mult).then_inc(sem("B_du"), 1)

            def inputs(q, b, c, h):
                n = NB * CI * q + CI * b + c
                m = 2 * n + h
                own = HN - h * NPOOL
                hs = hb[(2 * c + h) % 4]
                if c == 0 and h == 0:
                    dve.wait_ge(sem(f"B_bc_loaded{b}"), 32 * (q + 1))
                at_least(dve, sem("B_summed"), m - 3)
                if h == 0:
                    dve.wait_ge(sem("B_du"), n + 1)
                dve.tensor_tensor(seg(hs)[:, 0:own, 1:SEG],
                                  du[c % 2].rearrange("p (o t) -> p o t", o=1).broadcast_to([P, own, TC]),
                                  Brep[b][:, h * HN:h * HN + own, :], ALU.mult).then_inc(sem("B_started"), 1)

            def scan(q, b, c, h):
                n = NB * CI * q + CI * b + c
                m = 2 * n + h
                hs = hb[(2 * c + h) % 4]
                dve.wait_ge(sem("B_started"), m + 1)
                if h == 1:
                    dve.wait_ge(sem("B_pool_started"), n + 1)
                dve.wait_ge(sem("B_decays"), m + 1)
                dve.tensor_tensor_scan(hs, dA[h], hs, 0.0, ALU.mult, ALU.add).then_inc(sem("B_scanned"), 1)

            def gate(q, b, c):
                n = NB * CI * q + CI * b + c
                r = c % RING
                dve.wait_ge(sem("B_summed"), 2 * (n + 1))
                at_least(dve, sem("B_out_done"), n - 1)
                dve.tensor_tensor(yg[c % 2], sum_ps[c % 2][:, 0:TC], z_t[r], ALU.mult).then_inc(sem("B_gated"), 1)

            def statistics(q, b):
                g = 2 * q + b
                for a in range(TT):
                    dve.wait_ge(sem("B_x1_copied"), TT * g + a + 1)
                    dve.bn_stats(bst[:, 6 * a:6 * a + 6], x1[:, a, :]).then_inc(sem("B_bn"), 1)
                for a in range(TT):
                    alone(dve)
                    dve.wait_ge(sem("B_bn"), TT * g + a + 1)
                    dve.bn_aggr(mv[:, 2 * a:2 * a + 2], bst[:, 6 * a:6 * a + 6]).then_inc(sem("B_aggr"), 1)
                dve.wait_ge(sem("B_aggr"), TT * (g + 1))
                v = mv.rearrange("p (a c) -> p a c", c=2)[:, :, 1]
                dve.tensor_scalar(v, v, EPS_TOKEN, None, ALU.add).then_inc(sem("B_stats"), 1)

            def normalise(q, b):
                g = 2 * q + b
                at_least(dve, sem("B_tokens_stored"), 32 * g)
                dve.wait_ge(sem("B_rs"), g + 1)
                v = mv.rearrange("p (a c) -> p a c", c=2)[:, :, 1]
                dve.tensor_tensor(newt, rs, rs, ALU.mult).then_inc(sem("B_newton"), 1)
                dve.wait_ge(sem("B_newton"), 4 * g + 1)
                dve.tensor_tensor(newt, newt, v, ALU.mult).then_inc(sem("B_newton"), 1)
                dve.wait_ge(sem("B_newton"), 4 * g + 2)
                dve.tensor_scalar(newt, newt, -0.5, 1.5, ALU.mult, ALU.add).then_inc(sem("B_newton"), 1)
                dve.wait_ge(sem("B_newton"), 4 * g + 3)
                dve.tensor_tensor(rs, rs, newt, ALU.mult).then_inc(sem("B_newton"), 1)
                dve.wait_ge(sem("B_newton"), 4 * g + 4)
                for a in range(TT):
                    dve.tensor_scalar(tn[:, a, :], x1[:, a, :], mv[:, 2 * a:2 * a + 1], rs[:, a:a + 1],
                                      ALU.subtract, ALU.mult).then_inc(sem("B_normed"), 1)

            def keep_logits(q, b, a):
                t = TT * (2 * q + b) + a
                dve.wait_ge(sem("B_logits_done"), t + 1)
                j0 = (q * TT + (b * (L // P) + a)) * NE
                dve.tensor_tensor(logits[:, bass.ds(j0, NE)], lg_ps[:, 0:NE], gate_bb, ALU.add)\
                    .then_inc(sem("B_logits_kept"), 1)

            def before(q, b):
                return (q, 0) if b else (q - 1, 1)

            def after(q, b):
                return (q + 1, 0) if b else (q, 1)

            def group_b(q, b, first, last):
                for c in range(CI):
                    for h in range(2):
                        scan(q, b, c, h)
                        if h == 0:
                            inputs(q, b, c, 1)
                        elif c < CI - 1:
                            inputs(q, b, c + 1, 0)
                        elif not last:
                            inputs(*after(q, b), 0, 0)
                        if h == 0:
                            if c < CI - 1:
                                input_u(q, b, c + 1)
                            elif not last:
                                input_u(*after(q, b), 0)
                            if c >= 2:
                                gate(q, b, c - 2)
                            elif not first:
                                gate(*before(q, b), CI - 2 + c)
                        if not last:
                            for k, at in enumerate(DVE_LOG):
                                if at == 2 * c + h:
                                    log_step(*after(q, b), *divmod(k, LOG_STEPS))
                    if not first:
                        if c == 2:
                            statistics(*before(q, b))
                        if c == 3:
                            normalise(*before(q, b))
                        if c in (6, 7):
                            keep_logits(*before(q, b), c - 6)

            for i in range(2):
                for k in range(LOG_STEPS):
                    log_step(0, 0, i, k)
            input_u(0, 0, 0)
            inputs(0, 0, 0, 0)
            for b in range(NB):
                group_b(0, b, b == 0, False)
            with dve.Fori(1, STEPS - 1) as q:
                for b in range(NB):
                    group_b(q, b, False, False)
            for b in range(NB):
                group_b(STEPS - 1, b, False, b == 1)
            for c in (CI - 2, CI - 1):
                gate(STEPS - 1, 1, c)
            statistics(STEPS - 1, 1)
            normalise(STEPS - 1, 1)
            for a in range(TT):
                keep_logits(STEPS - 1, 1, a)
            barrier(dve)

            s_chain = sem("C_chain")
            chain = [0]

            def link(ins):
                chain[0] += 1
                ins.then_inc(s_chain, 1)
                dve.wait_ge(s_chain, chain[0])

            def by_tile(t):
                return t.rearrange("p e j -> p j e")

            def over_e(t):
                return t.rearrange("p (o j) -> p o j", o=1).broadcast_to([P, NE, NT])

            def over_j(t):
                return t.rearrange("p (e o) -> p e o", o=1).broadcast_to([P, NE, NT])

            lg = logits.rearrange("p (j e) -> p j e", e=NE)
            link(dve.tensor_reduce(tmax, lg, AX_X, ALU.max))
            dve.tensor_tensor(prob, lg.rearrange("p j e -> p e j"), over_e(tmax), ALU.subtract)\
                .then_inc(sem("C_shifted"), 1)
            dve.wait_ge(sem("C_exp"), 1)
            link(dve.tensor_reduce(tsum, by_tile(prob), AX_X, ALU.add))
            link(dve.reciprocal(tsum, tsum))
            link(dve.tensor_tensor(prob, prob, over_e(tsum), ALU.mult))
            dve.wait_ge(sem("C_tables"), 2 * NE + 3)
            for s in range(1, NE):
                link(dve.tensor_tensor(tmp[:, 0:NE - s], prob[:, 0:NE - s], prob[:, s:NE], ALU.is_ge))
                link(dve.tensor_tensor(rank[:, s:NE], rank[:, s:NE], tmp[:, 0:NE - s], ALU.add))
                link(dve.tensor_tensor(rank[:, 0:NE - s], rank[:, 0:NE - s], tmp[:, 0:NE - s], ALU.subtract))
            link(dve.tensor_scalar(hit, rank, float(TOPK), None, ALU.is_lt))
            link(dve.tensor_tensor(wm, prob, hit, ALU.mult))
            link(dve.scalar_tensor_tensor(out=wm, in0=hit, scalar=1.0, in1=wm, op0=ALU.subtract, op1=ALU.add))
            link(dve.memset(thr, 0))
            for t in range(TRY):
                link(dve.memset(bits[:, t * NE:(t + 1) * NE], (t + 1) << 28))

            def over_try(t):
                return t.rearrange("p (t e) -> p t e", t=1).broadcast_to([P, TRY, NE])

            wm_v = wm.rearrange("p (t e) j -> p t e j", t=1).broadcast_to([P, TRY, NE, NT])
            cand_v = cand.bitcast(F32).rearrange("p (t e j) -> p t e j", e=NE, j=1).broadcast_to([P, TRY, NE, NT])
            hits_v = hits.rearrange("p (t e j) -> p t e j", t=TRY, e=NE)
            with dve.Fori(0, 15) as i:
                dve.tensor_tensor(cand.rearrange("p (t e) -> p t e", e=NE), over_try(thr),
                                  bits.rearrange("p (t e) -> p t e", e=NE), ALU.bitwise_or)\
                    .then_inc(sem("C_cand"), 1)
                dve.wait_ge(sem("C_cand"), i + 1)
                dve.tensor_tensor(hits_v, wm_v, cand_v, ALU.is_ge).then_inc(sem("C_hit"), 1)
                dve.wait_ge(sem("C_hit"), i + 1)
                dve.tensor_reduce(cnt.rearrange("p (t e) -> p t e", e=NE), hits_v, AX_X, ALU.add)\
                    .then_inc(sem("C_counted"), 1)
                dve.wait_ge(sem("C_total"), i + 1)
                dve.tensor_scalar(cond, bank[0][:, 0:TRY * NE], float(CAP), None, ALU.is_ge).then_inc(sem("C_cond"), 1)
                dve.wait_ge(sem("C_cond"), i + 1)
                dve.tensor_reduce(gain, cond.rearrange("p (t e) -> p e t", e=NE), AX_X, ALU.add)\
                    .then_inc(sem("C_gain"), 1)
                dve.wait_ge(sem("C_gain"), i + 1)
                dve.tensor_tensor(gain_i, gain, bits[:, 0:NE], ALU.mult).then_inc(sem("C_gain_bits"), 1)
                dve.wait_ge(sem("C_gain_bits"), i + 1)
                dve.tensor_tensor(thr, thr, gain_i, ALU.bitwise_or).then_inc(sem("C_thr"), 1)
                dve.wait_ge(sem("C_thr"), i + 1)
                dve.tensor_scalar(bits, bits, 2, None, ALU.logical_shift_right).then_inc(sem("C_bits_done"), 1)
                dve.wait_ge(sem("C_bits_done"), i + 1)
            link(dve.tensor_tensor(gtm, wm, over_j(thr.bitcast(F32)), ALU.is_gt))
            dve.tensor_tensor(eqm, wm, over_j(thr.bitcast(F32)), ALU.is_equal).then_inc(sem("C_masks"), 1)
            dve.wait_ge(sem("C_prefixes"), 1)
            flat2 = "p e j -> p (e j)"

            def ps(i):
                return bank[i][:, 0:NE * NT]

            for pos, inside, total in ((posg, 1, 2), (posq, 3, 4)):
                link(dve.tensor_tensor_scan(pos.rearrange(flat2), seg0.rearrange(flat2), ps(total), 0.0,
                                            ALU.mult, ALU.add))
                if pos is posg:
                    link(dve.tensor_scalar(need, posg[:, :, NT - 1], -1.0, float(CAP), ALU.mult, ALU.add))
                link(dve.tensor_tensor(pos.rearrange(flat2), pos.rearrange(flat2), ps(total), ALU.subtract))
                link(dve.tensor_tensor(pos.rearrange(flat2), pos.rearrange(flat2), ps(inside), ALU.add))
            link(dve.tensor_tensor(tmp, posq, over_j(need), ALU.is_lt))
            link(dve.tensor_tensor(tmp, tmp, eqm, ALU.mult))
            link(dve.tensor_tensor(keep, gtm, tmp, ALU.add))
            link(dve.tensor_tensor(posq, posq, over_j(need), ALU.min))
            link(dve.tensor_tensor(posg, posg, posq, ALU.add))
            link(dve.tensor_tensor(posg, posg, over_j(base), ALU.add))
            link(dve.tensor_copy(count, count_i))
            link(dve.tensor_copy(cols_v[:, :, 0], token_i))
            for k in range(TOPK):
                link(dve.scalar_tensor_tensor(out=hit, in0=rank, scalar=float(k), in1=keep,
                                              op0=ALU.is_equal, op1=ALU.mult))
                link(dve.tensor_tensor(tmp, hit, prob, ALU.mult))
                link(dve.tensor_reduce(cols_v[:, :, 5 + k], by_tile(tmp), AX_X, ALU.add))
                link(dve.tensor_tensor(tmp, hit, posg, ALU.mult))
                link(dve.tensor_reduce(pick, by_tile(tmp), AX_X, ALU.add))
                link(dve.tensor_reduce(miss, by_tile(hit), AX_X, ALU.add))
                none = float(2 * ROWS * P)
                link(dve.tensor_scalar(miss, miss, -none, none, ALU.mult, ALU.add))
                link(dve.tensor_tensor(miss, miss, pick, ALU.add))
                link(dve.tensor_copy(word[:, 0:NT], miss))
                log2p = P.bit_length() - 1
                link(dve.tensor_scalar(word[:, NT:2 * NT], word[:, 0:NT], P - 1, None, ALU.bitwise_and))
                link(dve.tensor_scalar(word[:, 0:NT], word[:, 0:NT], log2p, None, ALU.logical_shift_right))
                link(dve.tensor_copy(cols_v[:, :, 1 + k], word[:, NT:2 * NT]))
                link(dve.tensor_copy(cols_v[:, :, 3 + k], word[:, 0:NT]))

            def one_hots(j, r, first):
                t = 2 * j + r
                if not first:
                    dve.wait_ge(sem("C_hot_used"), t - 1)
                    dve.wait_ge(sem("C_hot"), t - 1)
                cols_r = some_cols[r]
                dve.tensor_copy(cols_r, cols[:, bass.ds(t * HOT * NCOL, HOT * NCOL)]
                                .rearrange("p (g c) -> p g c", c=NCOL)).then_inc(sem("C_cols"), 1)

                def numbers(m):
                    return count[:, 0:m].rearrange("p (g k m) -> p g k m", g=1, k=1).broadcast_to([P, HOT, TOPK, m])

                def per_choice(c0, m):
                    return cols_r[:, :, c0:c0 + TOPK].rearrange("p g (k m) -> p g k m", m=1)\
                        .broadcast_to([P, HOT, TOPK, m])

                token = cols_r[:, :, 0:1].rearrange("p g (k m) -> p g k m", m=1).broadcast_to([P, HOT, TOPK, ROWS])
                dve.wait_ge(sem("C_cols"), t + 1)
                dve.tensor_tensor(lo_hot[r], numbers(P), per_choice(1, P), ALU.is_equal)
                dve.tensor_tensor(hi_eq, numbers(ROWS), per_choice(1 + TOPK, ROWS), ALU.is_equal)\
                    .then_inc(sem("C_hi_eq"), 1)
                dve.wait_ge(sem("C_hi_eq"), t + 1)
                dve.tensor_tensor(hi_hot[r][:, :, :, 0:ROWS], hi_eq, token, ALU.mult)
                dve.tensor_tensor(hi_hot[r][:, :, :, ROWS:], hi_eq, per_choice(1 + 2 * TOPK, ROWS), ALU.mult)\
                    .then_inc(sem("C_hot"), 1)

            for r in range(2):
                one_hots(0, r, True)
            with dve.Fori(1, NT // (2 * HOT)) as j:
                for r in range(2):
                    one_hots(j, r, False)
            dve.wait_ge(sem("C_table"), 1)
            link(dve.tensor_copy(slot_w, table_ps[:, ROWS:]))
            link(dve.tensor_scalar(found, table_ps[:, 0:ROWS], -1.0, 0.0, ALU.add, ALU.max))
            link(dve.tensor_copy(slot_get, found))
            link(dve.tensor_scalar(found, table_ps[:, 0:ROWS], 0.0, float(2 * T), ALU.is_equal, ALU.mult))
            link(dve.scalar_tensor_tensor(out=found, in0=table_ps[:, 0:ROWS], scalar=-1.0, in1=found,
                                          op0=ALU.add, op1=ALU.add))
            link(dve.tensor_copy(slot_put, found))
            barrier(dve)

            def ready_get(j, w, k):
                for i in range(first_of[k], first_of[k] + len(tiles_of[k])):
                    o = w * ND + i
                    at_least(dve, sem(f"D_gathered{o % XG}"), 16 * (j * (2 * ND // XG) + o // XG))
                    dve.tensor_copy(get[o % XG], slot_get[:, bass.ds(2 * ND * j + o, 1)])\
                        .then_inc(sem("D_get_ready"), 1)

            def copy_xt(j, w, k):
                for i, (t0, n) in enumerate(tiles_of[k]):
                    o = w * ND + first_of[k] + i
                    if i == 0:
                        at_least(dve, sem("D_up_done"), HM * (2 * NBLK * j + w * NBLK + k - 1))
                    dve.wait_ge(sem(f"D_transposed{o % XG}"), j * (2 * ND // XG) + o // XG + 1)
                    c0 = t0 - blocks[k][0]
                    g = ND * (2 * j + w) + first_of[k] + i
                    xb = (w * NBLK + k) % 2
                    src = xt_ps[o % 2][:, :].rearrange("p (k t) -> p k t", k=KD)[:, :, 0:n]
                    dve.tensor_copy(x_hi_r[xb][:, :, c0:c0 + n], src).then_inc(sem("D_xt_rounded"), 1)
                    dve.wait_ge(sem("D_xt_rounded"), g + 1)
                    dve.tensor_tensor(x_lo_r[xb][:, :, c0:c0 + n], src, x_hi_r[xb][:, :, c0:c0 + n].bitcast(F32), ALU.subtract)\
                        .then_inc(sem("D_xt_copied"), 1)

            def split_w(which, e, ch):
                dve.wait_ge(sem(f"D_w{which}_rounded"), CH * e + ch + 1)
                dve.tensor_tensor(w_chunk(which, w_lo_r[which], ch), w_chunk(which, w_lo[which], ch),
                                  w_chunk(which, w_hi_r[which], ch).bitcast(F32), ALU.subtract)\
                    .then_inc(sem(f"D_w{which}_split"), 1)

            def split_h(j, w, k, first):
                e = 2 * j + w
                n = blocks[k][1]
                for h in range(0, HM, 2):
                    dve.wait_ge(sem("D_h_rounded"), (e * NBLK + k) * (HM // 2) + h // 2 + 1)
                    lo = h_lo[:, h:h + 2, 0:n]
                    dve.tensor_tensor(h_lo_r[:, h:h + 2, 0:n], lo, h_hi_r[:, h:h + 2, 0:n].bitcast(F32), ALU.subtract).then_inc(sem("D_h_split"), 1)
                    if k == 0 and not first and h >= HM // 2:
                        split_w(2, e, (h - HM // 2) // 2)

            def weigh(j, w, k):
                e = 2 * j + w
                if k == 0:
                    dve.wait_ge(sem("D_b2_loaded"), 16 * (e + 1))
                for i, (t0, n) in enumerate(tiles_of[k]):
                    o = first_of[k] + i
                    g = ND * e + o
                    at_least(dve, sem(f"D_added{o % 2}"), 16 * ((ND // 2) * e + o // 2))
                    dve.tensor_copy(put[o % 2], slot_put[:, bass.ds(2 * ND * j + w * ND + o, 1)])\
                        .then_inc(sem("D_put_ready"), 1)
                    dve.tensor_copy(put_w[o % 2], slot_w[:, bass.ds(2 * ND * j + w * ND + o, 1)])\
                        .then_inc(sem("D_put_ready"), 1)
                    dve.wait_ge(sem("D_down_done"), g + 1)
                    dve.tensor_tensor(ye[o % 2][0:n, :], dn_ps[o % 2][0:n, :], b2_s[0:n, :], ALU.add)\
                        .then_inc(sem("D_biased"), 1)
                    dve.wait_ge(sem("D_biased"), g + 1)
                    dve.wait_ge(sem("D_put_ready"), 2 * (g + 1))
                    dve.tensor_scalar(ye[o % 2][0:n, :], ye[o % 2][0:n, :], put_w[o % 2][0:n, :], None,
                                      ALU.mult).then_inc(sem("D_weighted"), 1)

            def round_d(j, first, last):
                for w in range(2):
                    for k in range(NBLK):
                        nxt = (j, w, k + 1) if k + 1 < NBLK else (j, 1, 0) if w == 0 else (j + 1, 0, 0)
                        end = last and w == 1 and k == NBLK - 1
                        if not end:
                            ready_get(*nxt)
                        split_h(j, w, k, first and w == 0)
                        if not end:
                            copy_xt(*nxt)
                            if k == NBLK - 1:
                                for ch in range(CH):
                                    split_w(1, 2 * j + w + 1, ch)
                        weigh(j, w, k)

            ready_get(0, 0, 0)
            copy_xt(0, 0, 0)
            round_d(0, True, False)
            with dve.Fori(1, NE // 2 - 1) as j:
                round_d(j, False, False)
            round_d(NE // 2 - 1, False, True)
            barrier(dve)


def kernel(x, L0_conv_ln_w, L0_conv_ln_b, L0_conv_in_proj_w, L0_conv_conv_w, L0_conv_conv_b, L0_conv_x_proj_w,
           L0_conv_dt_proj_w, L0_conv_dt_proj_b, L0_conv_A_log, L0_conv_D_skip, L0_conv_out_proj_w,
           L0_ffn_gate_w, L0_ffn_gate_b, L0_ffn_w1, L0_ffn_b1, L0_ffn_w2, L0_ffn_b2):
    import numpy as np
    import concourse.bacc as bacc
    from concourse.bass_utils import run_bass_kernel_spmd as run

    x = np.asarray(x)
    NB, DIM, H, W = x.shape

    def tiles(a):
        a = np.asarray(a)
        a = a.reshape(a.shape[0] // 128, 128, -1)
        return a.transpose(1, 0, 2).reshape(128, -1)

    b1 = np.asarray(L0_ffn_b1)
    arrays = {
        "x": x.reshape(NB, DIM, H * W),
        "x_tok": x.reshape(NB, DIM, H * W).transpose(0, 2, 1).reshape(NB * H * W, DIM),
        "ln_w": tiles(L0_conv_ln_w),
        "ln_b": tiles(L0_conv_ln_b),
        "in_wT": np.asarray(L0_conv_in_proj_w).T,
        "conv_w": tiles(L0_conv_conv_w),
        "conv_b": tiles(L0_conv_conv_b),
        "xp_wT": np.asarray(L0_conv_x_proj_w).T,
        "dt_wT": np.asarray(L0_conv_dt_proj_w).T,
        "dt_b": np.asarray(L0_conv_dt_proj_b).reshape(1, -1),
        "A_log": tiles(L0_conv_A_log),
        "D_skip": tiles(L0_conv_D_skip),
        "out_wT": np.asarray(L0_conv_out_proj_w).T,
        "gate_wT": np.asarray(L0_ffn_gate_w).T,
        "gate_b": np.asarray(L0_ffn_gate_b).reshape(1, -1),
        "w1": np.asarray(L0_ffn_w1),
        "b1": b1.reshape(b1.shape[0], -1, 128).transpose(0, 2, 1),
        "w2": np.asarray(L0_ffn_w2),
        "b2": np.asarray(L0_ffn_b2),
    }
    arrays = {f"in_{k}": np.ascontiguousarray(a) for k, a in arrays.items()}
    nc = bacc.Bacc("TRN2", target_bir_lowering=False, num_devices=1)
    args = [nc.dram_tensor(k, a.shape, mybir.dt.from_np(a.dtype), kind="ExternalInput").ap()
            for k, a in arrays.items()]
    out = nc.dram_tensor("out_dram", (NB * H * W, DIM), F32, kind="ExternalOutput").ap()
    metaformer_layer(nc, *args, out)
    r = run(nc, [arrays], core_ids=[0])
    y = r.results[0]["out_dram"]
    return np.ascontiguousarray(y.reshape(NB, H * W, DIM).transpose(0, 2, 1)).reshape(NB, DIM, H, W)
```
